# Optimizing a Trainium2 kernel written in Bass

```python
import numpy as np
import jax
import jax.numpy as jnp

def _softmax(x, axis=-1):
    return jax.nn.softmax(x, axis=axis)

def _gelu(x):
    return jax.nn.gelu(x, approximate=True)

def _silu(x):
    return jax.nn.silu(x)

def _sigmoid(x):
    return jax.nn.sigmoid(x)

def _layernorm(x, axis=-1, eps=1e-05):
    m = jnp.mean(x, axis=axis, keepdims=True)
    v = jnp.var(x, axis=axis, keepdims=True)
    return (x - m) / jnp.sqrt(v + eps)

def _scatter_add(tgt, idx, src, axis=0):
    return tgt.at[idx].add(src)

def _segment_sum(src, seg, n):
    return jax.ops.segment_sum(src, seg, n)
kernel_name = 'mk_conv_attn_hybrid_d2_conv_nhwc768_r4_42ea50'

def setup_inputs(seed: int=0):
    np.random.seed(seed)
    _w = jnp.asarray

    def _rec_inputs():
        import jax
        import jax.numpy as jnp
        _gk = jax.random.key(seed)
        x = -0.0002221 + 1 * jax.random.normal(jax.random.fold_in(_gk, 1), (8, 16, 16, 192), jnp.float32)
        return x
    x = _rec_inputs()

    def _L0_conv_setup():
        import jax, jax.numpy as jnp
        import numpy as np
        B, H, W, DIM = (8, 16, 16, 192)
        NH = 12
        HD = DIM // NH
        WS = 14
        N = WS * WS
        MLP = 4 * DIM
        EPS = 1e-05

        def layernorm(x, w, b):
            mu = jnp.mean(x, axis=-1, keepdims=True)
            var = jnp.var(x, axis=-1, keepdims=True)
            return (x - mu) * jax.lax.rsqrt(var + EPS) * w + b

        def window_partition(x, ws):
            b, h, w, c = x.shape
            pad_h = (ws - h % ws) % ws
            pad_w = (ws - w % ws) % ws
            x = jnp.pad(x, ((0, 0), (0, pad_h), (0, pad_w), (0, 0)))
            hp, wp = (h + pad_h, w + pad_w)
            x = x.reshape(b, hp // ws, ws, wp // ws, ws, c)
            windows = x.transpose(0, 1, 3, 2, 4, 5).reshape(-1, ws, ws, c)
            return (windows, (hp, wp))

        def window_unpartition(windows, ws, pad_hw, hw):
            hp, wp = pad_hw
            h, w = hw
            b = windows.shape[0] // (hp * wp // ws // ws)
            x = windows.reshape(b, hp // ws, wp // ws, ws, ws, -1)
            x = x.transpose(0, 1, 3, 2, 4, 5).reshape(b, hp, wp, -1)
            return x[:, :h, :w, :]
        key = jax.random.key(seed)
        ks = jax.random.split(key, 8)
        f = lambda k, shape: jax.random.normal(k, shape, jnp.float32) * 0.02
        return {'x': jax.random.normal(ks[0], (B, H, W, DIM), jnp.float32), 'n1_w': jnp.ones((DIM,), jnp.float32), 'n1_b': jnp.zeros((DIM,), jnp.float32), 'qkv_w': f(ks[1], (DIM, 3 * DIM)), 'qkv_b': jnp.zeros((3 * DIM,), jnp.float32), 'proj_w': f(ks[2], (DIM, DIM)), 'proj_b': jnp.zeros((DIM,), jnp.float32), 'rel_pos_h': f(ks[3], (2 * WS - 1, HD)), 'rel_pos_w': f(ks[4], (2 * WS - 1, HD)), 'n2_w': jnp.ones((DIM,), jnp.float32), 'n2_b': jnp.zeros((DIM,), jnp.float32), 'lin1_w': f(ks[5], (DIM, MLP)), 'lin1_b': jnp.zeros((MLP,), jnp.float32), 'lin2_w': f(ks[6], (MLP, DIM)), 'lin2_b': jnp.zeros((DIM,), jnp.float32)}
    _L0_conv_all = _L0_conv_setup()
    _L0_conv_in = {k: v for k, v in _L0_conv_all.items() if k in ('n1_w', 'n1_b', 'qkv_w', 'qkv_b', 'proj_w', 'proj_b', 'rel_pos_h', 'rel_pos_w', 'n2_w', 'n2_b', 'lin1_w', 'lin1_b', 'lin2_w', 'lin2_b')}
    del _L0_conv_all

    def _L1_attn_setup():
        import math
        import jax, jax.numpy as jnp
        import numpy as np
        EMBED_DIM = 192
        NUM_HEADS = 3
        HEAD_DIM = EMBED_DIM // NUM_HEADS
        key = jax.random.key(seed)
        k1, k2, k3 = jax.random.split(key, 3)
        B, S, D = (4, 512, EMBED_DIM)
        inputs = jax.random.normal(k1, (B, S, D), dtype=jnp.float32)
        W_qkv = jax.random.normal(k2, (D, NUM_HEADS * D), dtype=jnp.float32) * (1.0 / math.sqrt(D))
        b_qkv = jnp.zeros((NUM_HEADS * D,), dtype=jnp.float32)
        W_out = jax.random.normal(k3, (D, D), dtype=jnp.float32) * (1.0 / math.sqrt(D))
        b_out = jnp.zeros((D,), dtype=jnp.float32)
        return {'inputs': inputs, 'W_qkv': W_qkv, 'b_qkv': b_qkv, 'W_out': W_out, 'b_out': b_out}
    _L1_attn_all = _L1_attn_setup()
    _L1_attn_in = {k: v for k, v in _L1_attn_all.items() if k in ('W_qkv', 'b_qkv', 'W_out', 'b_out')}
    del _L1_attn_all

    def _L1_ffn_setup():
        import jax, jax.numpy as jnp
        import numpy as np
        key = jax.random.key(seed)
        ks = jax.random.split(key, 6)
        B, N, D, E, S, H = (4, 1024, 192, 4, 256, 768)
        sc = lambda d: 1.0 / np.sqrt(d)
        return {'x': jax.random.normal(ks[0], (B, N, D), dtype=jnp.float32), 'phi': jax.random.normal(ks[1], (E, S, D), dtype=jnp.float32) * sc(D), 'w1': jax.random.normal(ks[2], (E, D, H), dtype=jnp.float32) * sc(D), 'b1': jnp.zeros((E, H), dtype=jnp.float32), 'w2': jax.random.normal(ks[3], (E, H, D), dtype=jnp.float32) * sc(H), 'b2': jnp.zeros((E, D), dtype=jnp.float32)}
    _L1_ffn_all = _L1_ffn_setup()
    _L1_ffn_in = {k: v for k, v in _L1_ffn_all.items() if k in ('phi', 'w1', 'b1', 'w2', 'b2')}
    del _L1_ffn_all
    return {'x': x, 'L0_conv_n1_w': _L0_conv_in['n1_w'], 'L0_conv_n1_b': _L0_conv_in['n1_b'], 'L0_conv_qkv_w': _L0_conv_in['qkv_w'], 'L0_conv_qkv_b': _L0_conv_in['qkv_b'], 'L0_conv_proj_w': _L0_conv_in['proj_w'], 'L0_conv_proj_b': _L0_conv_in['proj_b'], 'L0_conv_rel_pos_h': _L0_conv_in['rel_pos_h'], 'L0_conv_rel_pos_w': _L0_conv_in['rel_pos_w'], 'L0_conv_n2_w': _L0_conv_in['n2_w'], 'L0_conv_n2_b': _L0_conv_in['n2_b'], 'L0_conv_lin1_w': _L0_conv_in['lin1_w'], 'L0_conv_lin1_b': _L0_conv_in['lin1_b'], 'L0_conv_lin2_w': _L0_conv_in['lin2_w'], 'L0_conv_lin2_b': _L0_conv_in['lin2_b'], 'L1_attn_W_qkv': _L1_attn_in['W_qkv'], 'L1_attn_b_qkv': _L1_attn_in['b_qkv'], 'L1_attn_W_out': _L1_attn_in['W_out'], 'L1_attn_b_out': _L1_attn_in['b_out'], 'L1_ffn_phi': _L1_ffn_in['phi'], 'L1_ffn_w1': _L1_ffn_in['w1'], 'L1_ffn_b1': _L1_ffn_in['b1'], 'L1_ffn_w2': _L1_ffn_in['w2'], 'L1_ffn_b2': _L1_ffn_in['b2']}

def reference(x, L0_conv_n1_w, L0_conv_n1_b, L0_conv_qkv_w, L0_conv_qkv_b, L0_conv_proj_w, L0_conv_proj_b, L0_conv_rel_pos_h, L0_conv_rel_pos_w, L0_conv_n2_w, L0_conv_n2_b, L0_conv_lin1_w, L0_conv_lin1_b, L0_conv_lin2_w, L0_conv_lin2_b, L1_attn_W_qkv, L1_attn_b_qkv, L1_attn_W_out, L1_attn_b_out, L1_ffn_phi, L1_ffn_w1, L1_ffn_b1, L1_ffn_w2, L1_ffn_b2):
    import jax
    import jax.numpy as jnp

    def _L0_conv_ref(x, n1_w, n1_b, qkv_w, qkv_b, proj_w, proj_b, rel_pos_h, rel_pos_w, n2_w, n2_b, lin1_w, lin1_b, lin2_w, lin2_b):
        import jax, jax.numpy as jnp
        import numpy as np
        B, H, W, DIM = (8, 16, 16, 192)
        NH = 12
        HD = DIM // NH
        WS = 14
        N = WS * WS
        MLP = 4 * DIM
        EPS = 1e-05

        def layernorm(x, w, b):
            mu = jnp.mean(x, axis=-1, keepdims=True)
            var = jnp.var(x, axis=-1, keepdims=True)
            return (x - mu) * jax.lax.rsqrt(var + EPS) * w + b

        def window_partition(x, ws):
            b, h, w, c = x.shape
            pad_h = (ws - h % ws) % ws
            pad_w = (ws - w % ws) % ws
            x = jnp.pad(x, ((0, 0), (0, pad_h), (0, pad_w), (0, 0)))
            hp, wp = (h + pad_h, w + pad_w)
            x = x.reshape(b, hp // ws, ws, wp // ws, ws, c)
            windows = x.transpose(0, 1, 3, 2, 4, 5).reshape(-1, ws, ws, c)
            return (windows, (hp, wp))

        def window_unpartition(windows, ws, pad_hw, hw):
            hp, wp = pad_hw
            h, w = hw
            b = windows.shape[0] // (hp * wp // ws // ws)
            x = windows.reshape(b, hp // ws, wp // ws, ws, ws, -1)
            x = x.transpose(0, 1, 3, 2, 4, 5).reshape(b, hp, wp, -1)
            return x[:, :h, :w, :]
        shortcut = x
        h = layernorm(x, n1_w, n1_b)
        win, pad_hw = window_partition(h, WS)
        bw = win.shape[0]
        qkv = win.reshape(bw, N, DIM) @ qkv_w + qkv_b
        qkv = qkv.reshape(bw, N, 3, NH, HD).transpose(2, 0, 3, 1, 4)
        qkv = qkv.reshape(3, bw * NH, N, HD)
        q, k, v = (qkv[0], qkv[1], qkv[2])
        scale = HD ** (-0.5)
        attn = jnp.einsum('bqc,bkc->bqk', q * scale, k)
        coords = jnp.arange(WS)[:, None] - jnp.arange(WS)[None, :] + (WS - 1)
        Rh = rel_pos_h[coords]
        Rw = rel_pos_w[coords]
        r_q = q.reshape(-1, WS, WS, HD)
        rel_h = jnp.einsum('bhwc,hkc->bhwk', r_q, Rh)
        rel_w = jnp.einsum('bhwc,wkc->bhwk', r_q, Rw)
        attn = (attn.reshape(-1, WS, WS, WS, WS) + rel_h[:, :, :, :, None] + rel_w[:, :, :, None, :]).reshape(-1, N, N)
        attn = jax.nn.softmax(attn, axis=-1)
        out = jnp.einsum('bqk,bkc->bqc', attn, v)
        out = out.reshape(bw, NH, WS, WS, HD).transpose(0, 2, 3, 1, 4)
        out = out.reshape(bw, WS, WS, DIM) @ proj_w + proj_b
        out = window_unpartition(out, WS, pad_hw, (H, W))
        x = shortcut + out
        h2 = layernorm(x, n2_w, n2_b)
        mlp = jax.nn.gelu(h2 @ lin1_w + lin1_b, approximate=False) @ lin2_w + lin2_b
        return x + mlp

    def _L1_attn_ref(inputs, W_qkv, b_qkv, W_out, b_out):
        import math
        import jax, jax.numpy as jnp
        import numpy as np
        EMBED_DIM = 192
        NUM_HEADS = 3
        HEAD_DIM = EMBED_DIM // NUM_HEADS
        B, S, D = inputs.shape
        qkv = inputs @ W_qkv + b_qkv
        q, k, v = jnp.split(qkv, 3, axis=2)

        def split_heads(x):
            return x.reshape(B, S, NUM_HEADS, HEAD_DIM).transpose(0, 2, 1, 3)
        q, k, v = (split_heads(q), split_heads(k), split_heads(v))
        scale = 1.0 / math.sqrt(HEAD_DIM)
        attn = jnp.einsum('bhsd,bhtd->bhst', q, k) * scale
        causal = jnp.tril(jnp.ones((S, S), dtype=bool))
        attn = jnp.where(causal[None, None], attn, -jnp.inf)
        attn = jax.nn.softmax(attn, axis=-1)
        out = jnp.einsum('bhst,bhtd->bhsd', attn, v)
        out = out.transpose(0, 2, 1, 3).reshape(B, S, D)
        return out @ W_out + b_out

    def _L1_ffn_ref(x, phi, w1, b1, w2, b2):
        import jax, jax.numpy as jnp
        import numpy as np
        logits = jnp.einsum('bnd,esd->bnes', x, phi)
        B, N, E, S = logits.shape
        dispatch = jax.nn.softmax(logits, axis=1)
        combine = jax.nn.softmax(logits.reshape(B, N, E * S), axis=-1).reshape(B, N, E, S)
        slots = jnp.einsum('bnd,bnes->besd', x, dispatch)
        h = jax.nn.gelu(jnp.einsum('besd,edh->besh', slots, w1) + b1[None, :, None, :])
        y = jnp.einsum('besh,ehd->besd', h, w2) + b2[None, :, None, :]
        out = jnp.einsum('besd,bnes->bnd', y, combine)
        return out

    def _gn(v, G=32, eps=1e-05):
        B_, H_, W_, C_ = v.shape
        g = v.reshape(B_, H_, W_, G, C_ // G)
        m = jnp.mean(g, axis=(1, 2, 4), keepdims=True)
        s = jnp.var(g, axis=(1, 2, 4), keepdims=True)
        return ((g - m) / jnp.sqrt(s + eps)).reshape(v.shape)

    def _ln_c(v, eps=1e-06):
        m = jnp.mean(v, axis=-1, keepdims=True)
        s = jnp.var(v, axis=-1, keepdims=True)
        return (v - m) / jnp.sqrt(s + eps)

    def _ln_t(v, eps=1e-05):
        m = jnp.mean(v, axis=-1, keepdims=True)
        s = jnp.var(v, axis=-1, keepdims=True)
        return (v - m) / jnp.sqrt(s + eps)

    def _to_tokens(v):
        B_, H_, W_, C_ = v.shape
        return v.reshape(B_, H_ * W_, C_)

    def _from_tokens(t, like):
        return t.reshape(like.shape)
    x = _L0_conv_ref(x, L0_conv_n1_w, L0_conv_n1_b, L0_conv_qkv_w, L0_conv_qkv_b, L0_conv_proj_w, L0_conv_proj_b, L0_conv_rel_pos_h, L0_conv_rel_pos_w, L0_conv_n2_w, L0_conv_n2_b, L0_conv_lin1_w, L0_conv_lin1_b, L0_conv_lin2_w, L0_conv_lin2_b)
    t = _to_tokens(x)
    t = t + _L1_attn_ref(_ln_t(t), L1_attn_W_qkv, L1_attn_b_qkv, L1_attn_W_out, L1_attn_b_out)
    t = t + _L1_ffn_ref(_ln_t(t), L1_ffn_phi, L1_ffn_w1, L1_ffn_b1, L1_ffn_w2, L1_ffn_b2)
    x = _from_tokens(t, x)
    return x

_drawn_inputs = setup_inputs


def setup_inputs(seed=0):
    import zlib

    import numpy as np

    out = dict(_drawn_inputs(seed))
    spreads = {'L0_conv_n1_w': (1.0, 0.6),
     'L0_conv_n1_b': (0.0, 0.8),
     'L0_conv_qkv_b': (0.0, 0.1),
     'L0_conv_proj_b': (0.0, 0.1),
     'L0_conv_n2_w': (1.0, 0.6),
     'L0_conv_n2_b': (0.0, 0.76),
     'L0_conv_lin1_b': (0.0, 0.1),
     'L0_conv_lin2_b': (0.0, 0.1),
     'L1_attn_b_qkv': (0.0, 0.1),
     'L1_attn_b_out': (0.0, 0.1),
     'L1_ffn_b1': (0.0, 0.1),
     'L1_ffn_b2': (0.0, 0.1)}
    factors = {'L0_conv_qkv_w': 5.37, 'L0_conv_rel_pos_h': 8.0, 'L0_conv_rel_pos_w': 8.0}
    for name, (base, spread) in spreads.items():
        noise = np.random.default_rng([zlib.crc32(name.encode()), seed]).standard_normal(out[name].shape)
        drawn = base * np.exp(spread * noise) if base else spread * noise
        out[name] = jnp.asarray(drawn.astype(out[name].dtype))
    for name, factor in factors.items():
        out[name] = (out[name] * factor).astype(out[name].dtype)
    return out
```

```python
from contextlib import ExitStack

import concourse.bass as bass
from concourse import mybir

P = 128
F32 = mybir.dt.float32
F32R = mybir.dt.float32r
BF16 = mybir.dt.bfloat16
ALU = mybir.AluOpType
ACT = mybir.ActivationFunctionType
AX = mybir.AxisListType

B, H, W, D = 8, 16, 16, 192
T = H * W
TT = T // P
PAIRS = B // 2
NT = 2 * TT
N = NT * P
R1 = D - P
MLP = 4 * D
MC = MLP // P
WS, NH, HD = 14, 12, 16
G, HG = 3, 4
HALF = WS // 2
QT = HALF * WS
EW = W - WS
EREAL = 2 * H * EW
EPAD = WS * WS - EW * EW
EKEYS = EREAL + EPAD
QCOLS = WS * WS + EREAL
UH = 2
MAIN = 2 * NH // UH
UNITS = MAIN + NH // UH       
AH, AD = 3, 64
NE, NS = 4, 256
ST = NE * NS // P
CQ, CK, CV = 0, G * P, 2 * G * P
CL1 = CV + D
CA = CL1 + MLP
CAV = CA + 3 * P
CPHI = CA + 3 * D
CW1 = CPHI + NE * NS
WALL = CW1 + NE * MLP
CHUNK = 160
N1, N2, L1B, E1B = 6, 14, 18, 24
NCHUNK = WALL // CHUNK
QKV_CHUNKS = CL1 // CHUNK
EPS = 1e-5
NEG = -1.0e30


def build(nc, x, xe, wall0, wall1, rel, wp, w2a, w2e, bias_cols, bias_rows, b2r, c_ident, c_cw, c_oh, c_ohp,
          c_kw, c_kwe, c_mask, out):
    with ExitStack() as ctx:
        def sb(name, shape, dt=F32):
            return ctx.enter_context(nc.sbuf_tensor(name, shape, dt))

        def sem(name):
            return ctx.enter_context(nc.semaphore(name))

        xres = sb("xres", [P, B * TT, D])
        ws = sb("ws", [P, 4, WALL], F32R)
        xs = sb("xs", [P, 3, N + P + 4 * QT], F32R)
        ident = sb("ident", [P, P])
        wproj = sb("wproj", [P, 2, 2, D])
        bcol = sb("bcol", [P, 48])
        brow = sb("brow", [P, 2, D])
        stage = sb("stage", [P, 2, CHUNK])
        st6 = sb("st6", [P, NT + 1, 6])
        mv = sb("mv", [P, NT + 1, 2])
        rstd = sb("rstd", [P, NT + 1])
        mhalf = sb("mhalf", [P, NT + 1])
        xn = sb("xn", [P, NT + 1, 256])
        xt = sb("xt", [P, 2, N + P])
        nm = sb("nm", [P, 2, HG])
        rs = sb("rs", [P, 2, HG])
        AREA = 16640
        area = sb("area", [P, AREA])
        ps = ctx.enter_context(nc.psum_tensor("ps", [P, 8, 512], F32))

        def views(spec):
            got, at = [], 0
            for shape in spec:
                size = 1
                for n in shape:
                    size *= n
                v = area[:, at:at + size]
                if len(shape) == 2:
                    v = v.rearrange("p (a b) -> p a b", b=shape[1])
                elif len(shape) == 3:
                    v = v.rearrange("p (a b c) -> p a b c", b=shape[1], c=shape[2])
                elif len(shape) == 4:
                    v = v.rearrange("p (a b c d) -> p a b c d", b=shape[1], c=shape[2], d=shape[3])
                got.append(v)
                at += size
            assert at <= AREA, at
            return got

        (qa, qw, ka, kae, cw, ohg, kw, kwe, ohp, relt, pp, pt, o, ve, vee, xedge) = views([
            (2 * G, QCOLS), (2 * G, QCOLS), (G, 2, T), (G, 2, EKEYS), (W, H), (G, T), (T,), (EKEYS,), (EPAD,),
            (2 * WS, 32), (2, 2 * UH, EKEYS), (2, 2, 512), (NT + 1, D), (NT, NH, HD + 1), (3, NH, HD + 1), (D,)])
        qraw = pp.rearrange("p a b c -> p (a b c)")[:, 0:G * N].rearrange("p (g n) -> p g n", g=G)
        (hT, w2l) = views([(MC, N), (MC, D)])
        (cqk, cq2, cv, cp, cpt, co) = views([(2, N), (2, N), (NT, AH, AD + 1), (2, 3 * P), (2, 3 * P), (NT, D)])
        (lsb, cc, ct, dt_, _, w2x, b2row) = views([(2, NE * NS), (2, NE * NS), (ST, N), (ST, T), (1024,), (NE * MC, D),
                                                   (NE, D)])
        dd = cc
        sl = lsb.rearrange("p a b -> p (a b)").rearrange("p (s c) -> p s c", c=256)
        yy = area[:, 0:2 * ST * D].rearrange("p (b s d) -> p b s d", b=2, d=D)
        dstart = 4 * NE * NS + ST * N
        hTd = area[:, dstart:dstart + MC * N].rearrange("p (a b) -> p a b", b=N)
        slots = [ws[:, k, 0:NE * 2 * NS] for k in range(3)]
        dstat = sb("dstat", [P, 6, ST])
        identb = sb("identb", [P, P], BF16)
        maskb = sb("maskb", [P, P], BF16)
        ot0, ot1 = area[:, AREA - 2 * N:AREA - N], area[:, AREA - N:AREA]

        ld_x, ld_w, ld_c, ld_l2, ld_w2 = sem("ld_x"), sem("ld_w"), sem("ld_c"), sem("ld_l2"), sem("ld_w2")
        ld_p, ld_e = sem("ld_p"), sem("ld_e")
        setup_dve, setup_pool = sem("setup_dve"), sem("setup_pool")
        dve_own, pool_own = sem("dve_own"), sem("pool_own")
        w_split = sem("w_split")
        ln_mv, ln_rstd, ln_xn = sem("ln_mv"), sem("ln_rstd"), sem("ln_xn")
        ln_tr, ln_tr_e, ln_xt, ln_xt_e, ln_split = sem("ln_tr"), sem("ln_tr_e"), sem("ln_xt"), sem("ln_xt_e"), sem("ln_split")
        a_q, a_k, a_v, a_qraw, a_ka, a_ve, a_kae = (sem(n) for n in ("a_q", "a_k", "a_v", "a_qraw", "a_ka", "a_ve", "a_kae"))
        a_rel, a_qa, a_qw = sem("a_rel"), sem("a_qa"), sem("a_qw")
        a_s, a_nm, a_p, a_t, a_ptd, a_pta, a_o, a_on = (sem(n) for n in ("a_s", "a_nm", "a_p", "a_t", "a_ptd", "a_pta", "a_o", "a_on"))
        o_tr, o_td, o_ta, o_proj, o_res = (sem(n) for n in ("o_tr", "o_td", "o_ta", "o_proj", "o_res"))
        b_h, b_gelu, b_y, b_res = (sem(n) for n in ("b_h", "b_gelu", "b_y", "b_res"))
        c_qk, c_v, c_qt, c_ve, c_s, c_nm, c_p, c_t, c_pt, c_o, c_on = (
            sem(n) for n in ("c_qk", "c_v", "c_qt", "c_ve", "c_s", "c_nm", "c_p", "c_t", "c_pt", "c_o", "c_on"))
        d_l, d_nrm, d_c, d_lsb, d_ct, d_cte, d_lt, d_ncm, d_dt, d_dtr, d_de, d_sl, d_sle, d_st, d_sh, d_ss = (
            sem("d_" + n) for n in ("l", "nrm", "c", "lsb", "ct", "cte", "lt", "ncm", "dt", "dtr", "de", "sl", "sle", "st", "sh", "ss"))
        d_h, d_gelu, d_y, d_ye, d_o, d_res, stored = (sem(n) for n in ("d_h", "d_gelu", "d_y", "d_ye", "d_o", "d_res", "stored"))

        mm = nc.tensor.matmul

        def product(out_, wcols, xcols, weights_moving=False):
            x0, x1, x2 = xcols
            c0, c1 = wcols
            pairs = [(ws[:, 0, c0:c1], x0), (ws[:, 1, c0:c1], x0), (ws[:, 0, c0:c1], x1), (ws[:, 2, c0:c1], x2),
                     (ws[0:R1, 3, c0:c1], x2[0:R1])]
            for n, (w_, x_) in enumerate(pairs):
                l, r = (x_, w_) if weights_moving else (w_, x_)
                last = mm(out_, l, r, start=n == 0, stop=n == len(pairs) - 1)
            return last

        def xcols(a, b):
            return [xs[:, k, a:b] for k in range(3)]

        def scols(a, b):
            return [s[:, a:b] for s in slots]

        def loop(eng, body):
            with eng.Fori(0, PAIRS - 1) as it:
                body(it, True)
            body(PAIRS - 1, False)

        a_xw, a_own, c_own, d_own, ln_hi = sem("a_xw"), sem("a_own"), sem("c_own"), sem("d_own"), sem("ln_hi")

        def unit(u):
            if u < MAIN:
                return QT, 2, 2 * QT, u // (NH // UH), u % (NH // UH) * UH
            return P, 1, EKEYS, None, (u - MAIN) * UH

        from_one = dict(pe=(a_v, a_s, b_y, d_st, d_o, d_sl, d_y, o_proj), dve=(o_res, b_res, a_ptd, a_on, d_res, d_ye, d_ss), act=(b_gelu, d_cte, d_gelu, a_pta))

        def start_counts(eng, name):
            for s_ in from_one[name]:
                eng.sem_inc(s_, 1)

        def slot_cols(b, h):
            def a(t):
                return t.rearrange("p (e b s) -> p e b s", e=NE, b=2)[:, 2 * h:2 * h + 2, b, :]
            return a, None

        gate = [sem(f"gate_{n}") for n in ("pe", "dve", "pool")]

        def gated(eng, n):
            eng.sem_inc(gate[n], 1)

        block = ctx.enter_context(nc.Block())

        @block.sync
        def _(sp):
            sp.dma_start(xres[:, 0:NT, :], x[0:N].rearrange("(t p) d -> p t d", p=P)).then_inc(ld_x, 16)
            sp.dma_start(xedge, xe[0]).then_inc(ld_x, 16)
            for dst, src in ((ident[:], c_ident), (bcol[:], bias_cols), (brow[:], bias_rows), (cw, c_cw),
                             (ohg[:, 0], c_oh), (ohp, c_ohp), (kw, c_kw), (kwe, c_kwe),
                             (pt[:, 0, 0, 0:P], c_mask)):
                sp.dma_start(dst, src).then_inc(ld_c, 16)
            sp.dma_start(xres[:, NT:, :], x[N:].rearrange("(t p) d -> p t d", p=P)).then_inc(ld_x, 16)
            for dst, src in ((relt.rearrange("p a b -> p (a b)"), rel.rearrange("p a b -> p (a b)")), (wproj[:], wp)):
                sp.dma_start(dst, src).then_inc(ld_p, 16)
            for n in range(1, PAIRS):
                sp.wait_ge(ln_xn, n)
                sp.dma_start(xedge, xe[n]).then_inc(ld_e, 16)
            sp.wait_ge(o_res, 1 + 2 * PAIRS)
            sp.dma_start(w2l, w2a).then_inc(ld_l2, 16)
            sp.wait_ge(o_res, 1 + 4 * PAIRS)
            sp.dma_start(w2x, w2e).then_inc(ld_w2, 16)
            sp.dma_start(b2row, b2r).then_inc(ld_w2, 16)
            for it in range(PAIRS):
                sp.wait_ge(d_res, 1 + NT * (it + 1))
                sp.dma_start(out[it * N:(it + 1) * N].rearrange("(t p) d -> p t d", p=P),
                             xres[:, it * NT:(it + 1) * NT, :]).then_inc(stored, 16)
            sp.wait_ge(stored, 16 * PAIRS)

        @block.gpsimd
        def _(pool):
            own = [0]

            def step(ins):
                own[0] += 1
                ins.then_inc(pool_own, 1)

            nc.gpsimd.memset(mhalf[:], -0.5).then_inc(setup_pool, 1)
            pool.wait_ge(setup_pool, 1)
            nc.gpsimd.memset(ot1[R1:P, :], 1.0).then_inc(setup_pool, 1)
            pool.wait_ge(setup_pool, 2)

            def norm_scale(f, tiles, k):
                pool.wait_ge(ln_mv, f + 1)
                gated(pool, 2)
                nc.gpsimd.tensor_scalar(rstd[:, 0:tiles], mv[:, 0:tiles, 1], EPS, 1.0, ALU.add, ALU.mult).then_inc(pool_own, 1)
                pool.wait_ge(pool_own, k)
                nc.gpsimd.tensor_tensor(rstd[:, 0:tiles], rstd[:, 0:tiles], mhalf[:, 0:tiles], ALU.pow).then_inc(ln_rstd, 1)

            def split_chunk(c, k):
                pool.wait_ge(ld_w, c * 32 + 32)
                gated(pool, 2)
                cols = bass.ds(c * CHUNK, CHUNK)
                nc.gpsimd.tensor_copy(ws[:, 0, cols], stage[:, 0, :]).then_inc(pool_own, 1)
                nc.gpsimd.tensor_copy(ws[:, 2, cols], stage[:, 1, :]).then_inc(pool_own, 1)
                pool.wait_ge(pool_own, k + 2)
                nc.gpsimd.tensor_tensor(ws[:, 1, cols], stage[:, 0, :], ws[:, 0, cols].bitcast(F32), ALU.subtract).then_inc(pool_own, 1)
                nc.gpsimd.tensor_tensor(ws[0:R1, 3, cols], stage[0:R1, 1, :], ws[0:R1, 2, cols].bitcast(F32), ALU.subtract).then_inc(pool_own, 1)
                pool.wait_ge(pool_own, k + 4)
                pool.sem_inc(w_split, 1)
                if isinstance(c, int) and c == NCHUNK - 1:
                    return
                cols2 = bass.ds((c + 1) * CHUNK, CHUNK)
                pool.dma_start(stage[:, 0, :], wall0[:, cols2]).then_inc(ld_w, 16)
                pool.dma_start(stage[:, 1, :], wall1[:, cols2]).then_inc(ld_w, 16)

            pool.dma_start(stage[:, 0, :], wall0[:, 0:CHUNK]).then_inc(ld_w, 16)
            pool.dma_start(stage[:, 1, :], wall1[:, 0:CHUNK]).then_inc(ld_w, 16)
            k = 0
            for c in range(QKV_CHUNKS):
                split_chunk(c, k)
                k += 4
                if c == 0:
                    norm_scale(0, NT + 1, k + 1)
                    k += 1
            k0 = k
            rest = NCHUNK - QKV_CHUNKS
            per = -(-rest // PAIRS)

            def body(it, nxt, chunks):
                n = 4 * per + 1
                base = it * n + k0
                pool.wait_ge(ln_split, it + 1)
                pool.wait_ge(a_v, 1 + it * 3)
                gated(pool, 2)
                for k in range(3):
                    nc.gpsimd.tensor_copy(xs[:, k, N + P:].rearrange("p (i y x) -> p i y x", i=2, x=WS),
                                          xs[:, k, 0:N].bitcast(F32).rearrange("p (i y x) -> p i y x", i=2, x=W)[:, :, 0:WS, 0:WS])\
                        .then_inc(a_xw, 1)
                pool.wait_ge(a_ka, it * G + G)
                pool.wait_ge(a_s, 1 + it * UNITS)
                gated(pool, 2)
                kf = ka.rearrange("p g i t -> p (g i) t")
                kef = kae.rearrange("p g i t -> p (g i) t")
                nc.gpsimd.tensor_copy(kef[:, :, 0:EREAL // 2].rearrange("p a (y x) -> p a y x", x=EW),
                                      kf.rearrange("p a (y x) -> p a y x", x=W)[:, :, :, WS:W]).then_inc(a_kae, 1)
                nc.gpsimd.tensor_copy(kef[:, :, EREAL // 2:EREAL], kf[:, :, WS * W:T]).then_inc(a_kae, 1)
                if nxt:
                    norm_scale(it + 1, NT + 1, base + 1)
                for c in range(chunks):
                    split_chunk(it * per + QKV_CHUNKS + c, base + nxt + 4 * c)

            with pool.Fori(0, PAIRS - 1) as it:
                body(it, True, per)
            last = rest - (PAIRS - 1) * per
            base = (PAIRS - 1) * (4 * per + 1) + k0
            body(PAIRS - 1, False, last)
            k1 = base + 4 * last
            for ph in range(1, 4):
                for n in range(PAIRS):
                    k1 += 1
                    norm_scale(4 * ph + n, NT, k1)

        @block.vector
        def _(dve):
            V = nc.vector
            start_counts(dve, "dve")

            def tiles_of(n, tiles):
                return [xres[:, n * NT + j, :] for j in range(NT)] + ([xedge] if tiles > NT else [])

            def front_norm(f, n, tiles, used=()):
                xt_ = tiles_of(n, tiles)
                if tiles > NT:
                    dve.wait_ge(ld_e, 16 * n)
                for j in range(tiles):
                    last = V.bn_stats(st6[:, j, :], xt_[j])
                last.then_inc(dve_own, 1)
                dve.wait_ge(dve_own, f + 1)
                gated(dve, 1)
                for j in range(tiles):
                    last = V.bn_aggr(mv[:, j, :], st6[:, j, :])
                last.then_inc(ln_mv, 1)
                dve.wait_ge(ln_rstd, f + 1)
                dve.wait_ge(ln_tr, 2 * f)
                for s_, v_ in used:
                    dve.wait_ge(s_, v_)
                for j in range(tiles):
                    V.tensor_scalar(xn[:, j, 0:D], xt_[j], mv[:, j, 0:1], rstd[:, j:j + 1], ALU.subtract, ALU.mult)
                    last = V.tensor_scalar(xn[:, j, D:256], xt_[j][:, P:D], mv[:, j, 0:1], rstd[:, j:j + 1],
                                           ALU.subtract, ALU.mult)
                last.then_inc(ln_xn, 1)

            def front_split(f, tiles, *used):
                c = tiles * P
                dve.wait_ge(ln_xt, 2 * f + 2)
                if tiles > NT:
                    dve.wait_ge(ln_xt_e, f + 1)
                for s_, v_ in used:
                    dve.wait_ge(s_, v_)
                V.tensor_copy(xs[:, 0, 0:c], xt[:, 0, 0:c])
                V.tensor_copy(xs[:, 2, 0:c], xt[:, 1, 0:c]).then_inc(ln_hi, 1)
                dve.wait_ge(ln_hi, f + 1)
                V.tensor_tensor(xs[:, 1, 0:c], xt[:, 0, 0:c], xs[:, 0, 0:c].bitcast(F32), ALU.subtract)
                V.tensor_tensor(xs[R1:P, 2, 0:c], xt[R1:P, 1, 0:c], xs[R1:P, 2, 0:c].bitcast(F32), ALU.subtract)\
                    .then_inc(ln_split, 1)

            def residual(it, banks, ready, n0, done):
                for b in range(2):
                    dve.wait_ge(ready, 2 * n0 + b + 2)
                    rows = xres[:, bass.ds(it * NT + 2 * b, 2), :]
                    V.tensor_tensor(rows, ps[:, banks[b], 0:2 * D].rearrange("p (t d) -> p t d", d=D), rows,
                                    ALU.add).then_inc(done, 1)

            V.memset(ve.rearrange("p a b c -> p (a b c)"), 1.0)
            V.memset(vee.rearrange("p a b c -> p (a b c)"), 1.0).then_inc(setup_dve, 1)
            dve.wait_ge(ld_c, 16 * 9)
            dve.wait_ge(setup_dve, 1)
            for s in range(3):
                rows = slice(EREAL, P) if s < 2 else slice(0, P)
                V.tensor_copy(vee[rows, s, :, 0:HD], brow[rows, 0, :].rearrange("p (h c) -> p h c", c=HD))
            V.tensor_scalar(bcol[:, 3:6], bcol[:, 3:6], HD ** -0.5, None, ALU.mult)
            V.tensor_scalar(bcol[:, 10:12], bcol[:, 10:12], AD ** -0.5, None, ALU.mult)
            V.tensor_copy(maskb[:], pt[:, 0, 0, 0:P])
            V.tensor_copy(identb[:], ident[:]).then_inc(setup_dve, 1)
            dve.wait_ge(setup_dve, 2)
            for g in range(G):
                for i in range(2):
                    V.tensor_scalar(kae[:, g, i, EREAL:EKEYS], ohp, bcol[:, 3 + g:4 + g], None, ALU.add)
            for g in (2, 1, 0):
                last = V.tensor_scalar(ohg[:, g], ohg[:, 0], bcol[:, 3 + g:4 + g], None, ALU.add)
            last.then_inc(setup_dve, 1)
            dve.wait_ge(ld_x, 48)
            front_norm(0, 0, NT + 1)
            front_split(0, NT + 1)
            dve.wait_ge(setup_dve, 3)

            def body_a(it, nxt):
                for g in range(G):
                    dve.wait_ge(a_k, it * G + g + 1)
                    V.scalar_tensor_tensor(ka[:, g], ps[:, 3 + g, :].rearrange("p (i t) -> p i t", i=2), HD ** -0.5,
                                           ohg[:, g].unsqueeze(1).broadcast_to([P, 2, T]), ALU.mult, ALU.add)\
                        .then_inc(a_ka, 1)
                for i in range(2):
                    dve.wait_ge(a_v, 1 + it * 3 + i + 1)
                    for t in range(2):
                        V.tensor_tensor(ve[0:QT, 2 * i + t, :, 0:HD],
                                        ps[0:QT, 6 if i == 0 else 0, t * D:t * D + D].rearrange("p (h c) -> p h c", c=HD),
                                        brow[0:QT, 0, :].rearrange("p (h c) -> p h c", c=HD), ALU.add).then_inc(a_ve, 1)
                dve.wait_ge(a_v, 1 + it * 3 + 3)
                for i in range(2):
                    V.tensor_tensor(vee[0:EREAL, i, :, 0:HD],
                                    ps[EREAL * i:EREAL * i + EREAL, 1, 0:D].rearrange("p (h c) -> p h c", c=HD),
                                    brow[0:EREAL, 0, :].rearrange("p (h c) -> p h c", c=HD), ALU.add).then_inc(a_ve, 1)
                for q in range(4):
                    dve.wait_ge(a_rel, it * 8 + 5 + q)
                    got = ps[:, (6, 0, 1, 2)[q], 0:384].rearrange("p (x a y) -> p x a y", a=2 * G, y=H)
                    nx = min(4, WS - 4 * q)
                    V.tensor_copy(qw[:, :, 0:2 * QT].rearrange("p a (y x) -> p x a y", x=WS)[:, 4 * q:4 * q + nx],
                                  got[:, 0:nx, :, 0:WS])
                    last = V.tensor_tensor(
                        qw[:, :, QCOLS - EREAL // 2:QCOLS].rearrange("p a (y x) -> p x a y", x=W)[:, 4 * q:4 * q + 4],
                        got[:, :, :, WS:H], cw[:, 4 * q:4 * q + 4, WS:H].unsqueeze(2).broadcast_to([P, 4, 2 * G, H - WS]),
                        ALU.add)
                    if nx < 4:
                        last = V.tensor_tensor(
                            qw[:, :, 2 * QT:2 * QT + EREAL // 2].rearrange("p a (y x) -> p x a y", x=EW),
                            got[:, nx:4], cw[:, WS:W].unsqueeze(2).broadcast_to([P, EW, 2 * G, H]), ALU.add)
                    last.then_inc(a_qw, 1)
                base = it * UNITS
                for u in range(UNITS + 2):
                    if u < UNITS:
                        rows, parts, keys, i, h = unit(u)
                        dve.wait_ge(a_s, 1 + base + u + 1)
                        if u >= 2:
                            dve.wait_ge(a_p, base + u - 1)
                        b0 = UH * (u % 2)
                        V.tensor_reduce(nm[0:rows, u % 2, 0:UH * parts],
                                        ps[0:rows, b0:b0 + UH, 0:parts * keys].rearrange("p h (t k) -> p h t k", k=keys),
                                        AX.X, ALU.max, negate=True).then_inc(a_nm, 1)
                    if 1 <= u <= UNITS:
                        rows, parts, keys, i, h = unit(u - 1)
                        half, wide = keys // 2, UH * parts * rows
                        dve.wait_ge(a_t, base + u)
                        if u >= 3:
                            dve.wait_ge(a_o, base + u - 2)
                        V.tensor_copy(pt[0:half, (u - 1) % 2, 0, 0:wide], ps[0:half, 4, 0:wide]).then_inc(a_ptd, 1)
                    if u >= 2:
                        v = u - 2
                        rows, parts, keys, i, h = unit(v)
                        dve.wait_ge(a_o, base + v + 1)
                        n = UH * parts
                        po = ps[0:rows, 6, 0:n * (HD + 1)].rearrange("p (a c) -> p a c", c=HD + 1)
                        V.reciprocal(rs[0:rows, v % 2, 0:n], po[:, :, HD]).then_inc(a_own, 1)
                        dve.wait_ge(a_own, base + v + 1)
                        tile = 2 * i if parts == 2 else NT
                        V.tensor_tensor(
                            o[0:rows, tile:tile + parts, h * HD:(h + UH) * HD].rearrange("p t (h c) -> p t h c", c=HD),
                            po[:, :, 0:HD].rearrange("p (t h) c -> p t h c", h=UH),
                            rs[0:rows, v % 2, 0:n].rearrange("p (t h) -> p t h", h=UH).unsqueeze(3)
                            .broadcast_to([rows, parts, UH, HD]), ALU.mult).then_inc(a_on, 1)
                    if nxt and u == 8:
                        front_norm(it + 1, it + 1, NT + 1, [(ln_tr_e, it + 1)])
                    if nxt and u == 14:
                        front_split(it + 1, NT + 1, (a_v, 3 * it + 4))
                dve.wait_ge(o_tr, it + 1)
                for dst, bank, rows in ((ot0, 0, P), (ot1, 1, R1)):
                    last = V.tensor_copy(
                        dst[0:rows, :].rearrange("p (i y x) -> p i y x", i=2, x=W)[:, :, 0:WS, 0:WS],
                        ps[0:rows, bank, 0:4 * QT].rearrange("p (i y x) -> p i y x", i=2, x=WS))
                last.then_inc(o_td, 1)
                residual(it, (3, 4), o_proj, it, o_res)

            loop(dve, body_a)

            dve.wait_ge(o_res, 1 + 2 * PAIRS)
            front_norm(PAIRS, 0, NT, [(ln_tr_e, PAIRS)])
            front_split(PAIRS, NT, (a_v, 1 + 3 * PAIRS))

            def body_b(it, nxt):
                if nxt:
                    front_norm(it + (PAIRS + 1), it + 1, NT)
                    front_split(it + (PAIRS + 1), NT, (b_h, MC * it + MC))
                residual(it, (4, 5), b_y, it, b_res)

            loop(dve, body_b)

            dve.wait_ge(b_res, 1 + 2 * PAIRS)
            V.memset(cv.rearrange("p a b c -> p (a b c)"), 1.0).then_inc(setup_dve, 1)
            dve.wait_ge(setup_dve, 4)
            front_norm(2 * PAIRS, 0, NT)
            front_split(2 * PAIRS, NT, (b_h, MC * PAIRS))

            def body_c(it, nxt):
                for b in range(2):
                    dve.wait_ge(c_v, it * 2 + b + 1)
                    for t in range(2):
                        last = V.tensor_tensor(cv[:, 2 * b + t, :, 0:AD],
                                               ps[:, 3 + b, t * D:t * D + D].rearrange("p (h c) -> p h c", c=AD),
                                               brow[:, 1, :].rearrange("p (h c) -> p h c", c=AD), ALU.add)
                    last.then_inc(c_ve, 1)
                n = 2 * AH
                base = it * n
                for u in range(n + 2):
                    if u < n:
                        dve.wait_ge(c_s, base + u + 1)
                        if u >= 2:
                            dve.wait_ge(c_p, base + u - 1)
                        V.reduce_max(nm[:, u % 2, 0:1], ps[:, u % 2, 0:P], AX.X, negate=True)
                        V.reduce_max(nm[:, u % 2, 1:2], ps[:, u % 2, P:3 * P], AX.X, negate=True).then_inc(c_nm, 1)
                    if u >= 2:
                        v = u - 2
                        b, h = v // AH, v % AH
                        dve.wait_ge(c_o, base + v + 1)
                        po = ps[:, 5 + v % 2, 0:2 * (AD + 1)].rearrange("p (t c) -> p t c", c=AD + 1)
                        V.reciprocal(rs[:, v % 2, 0:2], po[:, :, AD]).then_inc(c_own, 1)
                        dve.wait_ge(c_own, base + v + 1)
                        V.tensor_tensor(co[:, 2 * b:2 * b + 2, AD * h:AD * h + AD], po[:, :, 0:AD],
                                        rs[:, v % 2, 0:2].unsqueeze(2).broadcast_to([P, 2, AD]), ALU.mult).then_inc(c_on, 1)
                    if nxt and u == 3:
                        front_norm(it + (2 * PAIRS + 1), it + 1, NT)
                    if nxt and u == 6:
                        front_split(it + (2 * PAIRS + 1), NT, (c_v, 2 * it + 2))
                dve.wait_ge(o_tr, it + (PAIRS + 1))
                V.tensor_copy(ot1[0:R1, :], ps[0:R1, 1, :]).then_inc(o_td, 1)
                residual(it, (2, 3), o_proj, it + PAIRS, o_res)

            loop(dve, body_c)

            dve.wait_ge(o_res, 1 + 4 * PAIRS)
            front_norm(3 * PAIRS, 0, NT)
            front_split(3 * PAIRS, NT, (c_v, 2 * PAIRS))
            ncm, csum, rcs, nrm, rsum, rrs = (dstat[:, k, :] for k in range(6))

            def body_d(it, nxt):
                for b in range(2):
                    i2 = it * 2 + b
                    for j in range(2):
                        n = 2 * b + j
                        i4 = it * 4 + n
                        dve.wait_ge(d_l, i4 + 1)
                        dve.wait_ge(d_st, 1 + i2 * 2)
                        dve.wait_ge(d_o, 1 + it * 2)
                        V.tensor_copy(lsb[:, j, :], ps[:, 2 * j:2 * j + 2, :].rearrange("p a c -> p (a c)")).then_inc(d_lsb, 1)
                        dve.wait_ge(d_lsb, i4 + 1)
                        V.reduce_max(nrm[:, n:n + 1], lsb[:, j, :], AX.X, negate=True).then_inc(d_nrm, 1)
                    for k in range(4):
                        dve.wait_ge(d_lt, i2 * 4 + k + 1)
                        V.tensor_reduce(ncm[:, 2 * k:2 * k + 2], ps[:, k, :].rearrange("p (s n) -> p s n", s=2), AX.X,
                                        ALU.max, negate=True).then_inc(d_ncm, 1)
                    for j in range(2):
                        n = 2 * b + j
                        dve.wait_ge(d_dtr, i2 * 2 + j + 1)
                        V.tensor_copy(dd[:, j, :], ps[:, 4:6, :].rearrange("p a c -> p (a c)")).then_inc(d_de, 1)
                    dve.wait_ge(d_dt, i2 * 4 + 4)
                    V.reciprocal(rcs, csum).then_inc(d_own, 1)
                    dve.wait_ge(d_own, i2 + 1)
                    for k in range(4):
                        dve.wait_ge(d_sl, 1 + i2 * 4 + k + 1)
                        got = ps[:, k, 0:2 * D].rearrange("p (s d) -> p s d", d=D)
                        V.tensor_tensor(sl[:, 2 * k:2 * k + 2, 0:D], got,
                                        rcs[:, 2 * k:2 * k + 2].unsqueeze(2).broadcast_to([P, 2, D]), ALU.mult)
                        V.tensor_tensor(sl[:, 2 * k:2 * k + 2, D:256], got[:, :, P:D],
                                        rcs[:, 2 * k:2 * k + 2].unsqueeze(2).broadcast_to([P, 2, R1]), ALU.mult)\
                            .then_inc(d_sle, 1)
                    for h in range(2):
                        dve.wait_ge(d_sh, i2 * 2 + h + 1)
                        a, z = slot_cols(b, h)
                        bank = (4, 6)[h], (5, 0)[h]
                        V.tensor_tensor(a(slots[1]), ps[:, bank[0], :].rearrange("p (e s) -> p e s", e=2),
                                        a(slots[0]).bitcast(F32), ALU.subtract)
                        V.tensor_tensor(a(slots[2])[R1:P], ps[R1:P, bank[1], :].rearrange("p (e s) -> p e s", e=2),
                                        a(slots[2])[R1:P].bitcast(F32), ALU.subtract).then_inc(d_ss, 1)
                V.reciprocal(rrs[:, 0:NT], rsum[:, 0:NT])
                if nxt:
                    front_norm(it + (3 * PAIRS + 1), it + 1, NT, [(d_sl, 1 + 8 * it + 8)])
                for e in range(NE):
                    for b in range(2):
                        dve.wait_ge(d_y, 1 + it * 2 * NE + 2 * e + b + 1)
                        V.tensor_tensor(yy[:, b, 2 * e:2 * e + 2, :],
                                        ps[:, 4 + b, 0:2 * D].rearrange("p (s d) -> p s d", d=D),
                                        b2row[:, e, :].unsqueeze(1).broadcast_to([P, 2, D]), ALU.add).then_inc(d_ye, 1)
                    if nxt and e == 1:
                        front_split(it + (3 * PAIRS + 1), NT, (d_l, 4 * it + 4))
                for n in range(NT):
                    if n % 2 == 0:
                        dve.wait_ge(d_o, 1 + it * 2 + n // 2 + 1)
                    xt_ = xres[:, it * NT + n, :]
                    V.scalar_tensor_tensor(xt_, ps[:, (6, 0)[n // 2], (n % 2) * D:(n % 2) * D + D], rrs[:, n:n + 1], xt_,
                                           ALU.mult, ALU.add).then_inc(d_res, 1)

            loop(dve, body_d)

        @block.scalar
        def _(act):
            A = nc.scalar
            start_counts(act, "act")

            def front_turned(f, tiles, affine):
                act.wait_ge(ln_split, f)
                for k in range(2):
                    act.wait_ge(ln_tr, 2 * f + k + 1)
                    sc = dict(scale=bcol[:, affine + k:affine + k + 1], bias=bcol[:, affine + 2 + k:affine + 3 + k]) if affine else {}
                    A.activation(xt[:, k, 0:N], ps[:, 7, :], ACT.Identity, **sc).then_inc(ln_xt, 1)
                if tiles > NT:
                    act.wait_ge(ln_tr_e, f + 1)
                    for k in range(2):
                        sc = dict(scale=bcol[:, affine + k:affine + k + 1], bias=bcol[:, affine + 2 + k:affine + 3 + k])
                        last = A.activation(xt[:, k, N:N + P], ps[:, 7, k * P:k * P + P], ACT.Identity, **sc)
                    last.then_inc(ln_xt_e, 1)

            act.wait_ge(ld_c, 16 * 9)
            front_turned(0, NT + 1, N1)

            def body_a(it, nxt):
                for g in range(G):
                    act.wait_ge(a_q, it * G + g + 1)
                    A.activation(qraw[:, g, :], ps[:, g, :], ACT.Identity, bias=bcol[:, g:g + 1]).then_inc(a_qraw, 1)
                for q in range(4):
                    act.wait_ge(a_rel, it * 8 + q + 1)
                    got = ps[:, 2 + q, 0:384].rearrange("p (y a x) -> p y a x", a=2 * G, x=W)
                    ny = min(4, WS - 4 * q)
                    A.activation(qa[:, :, 4 * q * WS:(4 * q + ny) * WS].rearrange("p a (y x) -> p y a x", x=WS),
                                 got[:, 0:ny, :, 0:WS], ACT.Copy)
                    c0 = 2 * QT + 4 * q * EW
                    last = A.activation(qa[:, :, c0:c0 + 4 * EW].rearrange("p a (y x) -> p y a x", x=EW),
                                        got[:, :, :, WS:W], ACT.Copy)
                    if ny < 4:
                        last = A.activation(qa[:, :, QCOLS - EREAL // 2:QCOLS].rearrange("p a (y x) -> p y a x", x=W),
                                            got[:, ny:4], ACT.Copy)
                    last.then_inc(a_qa, 1)
                base = it * UNITS
                for u in range(UNITS + 1):
                    if u >= 1:
                        rows, parts, keys, i, h = unit(u - 1)
                        half, wide = keys // 2, UH * parts * rows
                        act.wait_ge(a_t, base + u)
                        if u >= 3:
                            act.wait_ge(a_o, base + u - 2)
                        A.activation(pt[0:half, (u - 1) % 2, 1, 0:wide], ps[0:half, 5, 0:wide], ACT.Copy)\
                            .then_inc(a_pta, 1)
                    if u < UNITS:
                        rows, parts, keys, i, h = unit(u)
                        act.wait_ge(a_nm, base + u + 1)
                        for k in range(UH * parts):
                            c0 = k % parts * keys
                            last = A.activation(pp[0:rows, u % 2, k, 0:keys],
                                                ps[0:rows, UH * (u % 2) + k // parts, c0:c0 + keys],
                                                ACT.Exp, bias=nm[0:rows, u % 2, k:k + 1])
                        last.then_inc(a_p, 1)
                    if nxt and u == 11:
                        front_turned(it + 1, NT + 1, N1)
                act.wait_ge(o_tr, it + 1)
                for dst, c0, rows in ((ot0, 0, P), (ot1, P, R1)):
                    d4 = dst[0:rows, :].rearrange("p (i y x) -> p i y x", i=2, x=W)
                    s3 = ps[0:rows, 2, c0:c0 + P].rearrange("p (i c) -> p i c", i=2)
                    A.activation(d4[:, :, 0:WS, WS:W], s3[:, :, 0:WS * EW].rearrange("p i (y x) -> p i y x", x=EW), ACT.Copy)
                    last = A.activation(dst[0:rows, :].rearrange("p (i t) -> p i t", i=2)[:, :, WS * W:T], s3[:, :, EREAL // 2:EREAL], ACT.Copy)
                last.then_inc(o_ta, 1)

            loop(act, body_a)
            front_turned(PAIRS, NT, N2)
            act.wait_ge(o_res, 1 + 2 * PAIRS)

            def body_b(it, nxt):
                act.wait_ge(b_y, 1 + it * 2)
                for m in range(MC):
                    act.wait_ge(b_h, it * MC + m + 1)
                    A.activation(hT[:, m, :], ps[:, m % 4, :], ACT.Gelu, bias=bcol[:, L1B + m:L1B + m + 1]).then_inc(b_gelu, 1)
                if nxt:
                    front_turned(it + (PAIRS + 1), NT, N2)

            loop(act, body_b)
            front_turned(2 * PAIRS, NT, 0)

            def body_c(it, nxt):
                act.wait_ge(c_qk, it * 3 + 1)
                A.activation(cqk[:, 0, :], ps[:, 0, :], ACT.Identity, scale=AD ** -0.5, bias=bcol[:, 10:11])
                act.wait_ge(c_qk, it * 3 + 2)
                A.activation(cqk[:, 1, :], ps[:, 1, :], ACT.Identity, bias=bcol[:, 12:13])
                act.wait_ge(c_qk, it * 3 + 3)
                A.activation(cq2[0:AD, 0, :], ps[0:AD, 2, :], ACT.Identity, scale=AD ** -0.5, bias=bcol[0:AD, 11:12])
                A.activation(cq2[0:AD, 1, :], ps[AD:P, 2, :], ACT.Identity, bias=bcol[AD:P, 13:14]).then_inc(c_qt, 1)
                n = 2 * AH
                base = it * n
                for u in range(n + 1):
                    if u >= 1:
                        act.wait_ge(c_t, base + u)
                        if u >= 3:
                            act.wait_ge(c_o, base + u - 2)
                        A.activation(cpt[:, (u - 1) % 2, :], ps[:, 3 + (u - 1) % 2, 0:3 * P], ACT.Copy).then_inc(c_pt, 1)
                    if u < n:
                        act.wait_ge(c_nm, base + u + 1)
                        A.activation(cp[:, u % 2, 0:P], ps[:, u % 2, 0:P], ACT.Exp, bias=nm[:, u % 2, 0:1])
                        A.activation(cp[:, u % 2, P:3 * P], ps[:, u % 2, P:3 * P], ACT.Exp, bias=nm[:, u % 2, 1:2]).then_inc(c_p, 1)
                    if nxt and u == 5:
                        front_turned(it + (2 * PAIRS + 1), NT, 0)
                act.wait_ge(o_tr, it + (PAIRS + 1))
                A.activation(ot0[:], ps[:, 0, :], ACT.Copy).then_inc(o_ta, 1)

            loop(act, body_c)
            front_turned(3 * PAIRS, NT, 0)
            ncm, csum, rcs, nrm, rsum, rrs = (dstat[:, k, :] for k in range(6))

            def body_d(it, nxt):
                for b in range(2):
                    i2 = it * 2 + b
                    for j in range(2):
                        n = 2 * b + j
                        i4 = it * 4 + n
                        act.wait_ge(d_nrm, i4 + 1)
                        act.wait_ge(d_sl, 1 + i2 * 4)
                        act.wait_ge(d_o, 1 + it * 2)
                        A.activation(cc[:, j, :], lsb[:, j, :], ACT.Exp,
                                     bias=nrm[:, n:n + 1], accum_out=rsum[:, n:n + 1]).then_inc(d_c, 1)
                        act.wait_ge(d_ct, i4 + 1)
                        A.activation(ct[:, :, n * P:n * P + P], ps[:, 4:6, :].rearrange("p a (s c) -> p (a s) c", c=P), ACT.Copy)\
                            .then_inc(d_cte, 1)
                    for k in range(4):
                        act.wait_ge(d_ncm, i2 * 4 + k + 1)
                        for s in range(2):
                            st = 2 * k + s
                            last = A.activation(dt_[:, st, :], ps[:, k, s * T:s * T + T], ACT.Exp, bias=ncm[:, st:st + 1],
                                                accum_out=csum[:, st:st + 1])
                        last.then_inc(d_dt, 1)
                    for h in range(2):
                        act.wait_ge(d_st, 1 + i2 * 2 + h + 1)
                        a, _ = slot_cols(b, h)
                        bank = (4, 6)[h], (5, 0)[h]
                        A.activation(a(slots[0]), ps[:, bank[0], :].rearrange("p (e s) -> p e s", e=2), ACT.Copy)
                        A.activation(a(slots[2]), ps[:, bank[1], :].rearrange("p (e s) -> p e s", e=2), ACT.Copy).then_inc(d_sh, 1)
                if nxt:
                    front_turned(it + (3 * PAIRS + 1), NT, 0)
                for e in range(NE):
                    act.wait_ge(d_y, 1 + it * 2 * NE + 2 * e)
                    for m in range(MC):
                        act.wait_ge(d_h, it * NE * MC + e * MC + m + 1)
                        A.activation(hTd[:, m, :], ps[:, (e * MC + m) % 4, :], ACT.Gelu_apprx_tanh,
                                     bias=bcol[:, E1B + e * MC + m:E1B + e * MC + m + 1]).then_inc(d_gelu, 1)

            loop(act, body_d)

        @block.tensor
        def _(pe):
            tr = nc.tensor.transpose
            start_counts(pe, "pe")

            def front_turn(f, tiles, *free):
                pe.wait_ge(ln_xn, f + 1)
                pe.wait_ge(ln_xt, 2 * f)
                for s_, v_ in free:
                    pe.wait_ge(s_, v_)
                for k in range(2):
                    if k:
                        pe.wait_ge(ln_xt, 2 * f + 1)
                    for j in range(NT):
                        last = tr(ps[:, 7, j * P:j * P + P], xn[:, j, k * P:k * P + P], ident[:])
                    last.then_inc(ln_tr, 1)
                if tiles > NT:
                    pe.wait_ge(ln_xt, 2 * f + 2)
                    for k in range(2):
                        last = tr(ps[:, 7, k * P:k * P + P], xn[:, NT, k * P:k * P + P], ident[:])
                    last.then_inc(ln_tr_e, 1)

            pe.wait_ge(ld_c, 16 * 9)
            front_turn(0, NT + 1)
            pe.wait_ge(ld_p, 32)
            pe.wait_ge(w_split, QKV_CHUNKS)

            def scores_full(u, i, h):
                a = 2 * (h // HG) + i
                for t in range(2):
                    for k in range(UH):
                        q = slice(32 * (h % HG + k), 32 * (h % HG + k) + 32)
                        dst = ps[0:QT, UH * (u % 2) + k, 2 * QT * t:2 * QT * t + 2 * QT]
                        kv = ka[q, a // 2, i, :].rearrange("p (y x) -> p y x", x=W)[:, 0:WS, 0:WS]
                        kwv = kw[q].rearrange("p (y x) -> p y x", x=W)[:, 0:WS, 0:WS]
                        mm(dst, qa[q, a, QT * t:QT * t + QT], kv, start=True, stop=False)
                        last = mm(dst, qw[q, a, QT * t:QT * t + QT], kwv, start=False, stop=True)
                return last

            def scores_border(u, h):
                g = h // HG
                for i in range(2):
                    a = 2 * g + i
                    for part in range(2):
                        for k in range(UH):
                            q = slice(32 * (h % HG + k), 32 * (h % HG + k) + 32)
                            c, c0 = 64 * i + 32 * part, 2 * QT + 32 * part
                            dst = ps[c:c + 32, UH * (u % 2) + k, 0:EKEYS]
                            mm(dst, qa[q, a, c0:c0 + 32], kae[q, g, i, :], start=True, stop=False)
                            last = mm(dst, qw[q, a, c0:c0 + 32], kwe[q], start=False, stop=True)
                return last

            def body_a(it, nxt):
                pe.wait_ge(ln_split, it + 1)
                pe.wait_ge(o_res, 1 + it * 2)
                for g in range(G):
                    product(ps[:, g, :], (CQ + g * P, CQ + g * P + P), xcols(0, N)).then_inc(a_q, 1)
                for g in range(G):
                    product(ps[:, 3 + g, :], (CK + g * P, CK + g * P + P), xcols(0, N)).then_inc(a_k, 1)
                for i in range(2):
                    if i:
                        pe.wait_ge(a_qraw, it * G + 1)
                    pe.wait_ge(a_xw, it * 3 + 3)
                    for t in range(2):
                        at = N + P + (2 * i + t) * QT
                        last = product(ps[0:QT, 6 if i == 0 else 0, t * D:t * D + D], (CV, CV + D),
                                       xcols(at, at + QT), True)
                    last.then_inc(a_v, 1)
                pe.wait_ge(a_qraw, it * G + 2)
                product(ps[:, 1, 0:D], (CV, CV + D), xcols(N, N + P), True).then_inc(a_v, 1)
                pe.wait_ge(a_qraw, it * G + 3)
                gated(pe, 0)
                q4 = qraw.rearrange("p g (i t) -> p (g i) t", i=2)
                for n in range(8):
                    if 1 <= n <= 3:
                        pe.wait_ge(a_ka, it * G + n)
                    if 4 <= n <= 6:
                        pe.wait_ge(a_ve, it * 6 + 2 * (n - 3))
                    if n == 7:
                        pe.wait_ge(a_qa, it * 4 + 1)
                    if n:
                        gated(pe, 0)
                    bank = (2, 3, 4, 5, 6, 0, 1, 2)[n]
                    for k in range(4):
                        at = 4 * (n % 4) + k
                        local = at if at < WS else at - WS
                        for r in range(HG):
                            q = slice(32 * r, 32 * r + 32)
                            rows = q4[q].rearrange("p a (y x) -> p a y x", x=W)
                            src = rows[:, :, at, :] if n < 4 else rows[:, :, :, at]
                            last = mm(ps[q, bank, 96 * k:96 * k + 96], relt[q, (0 if n < 4 else WS) + local, :], src,
                                      start=True, stop=True)
                    last.then_inc(a_rel, 1)
                base = it * UNITS
                for u in range(UNITS + 2):
                    if u < UNITS:
                        rows, parts, keys, i, h = unit(u)
                        if u == 0:
                            pe.wait_ge(a_qa, it * 4 + 4)
                            pe.wait_ge(a_qw, it * 4 + 4)
                        if u >= 2:
                            pe.wait_ge(a_p, base + u - 1)
                        if u == MAIN:
                            pe.wait_ge(a_kae, it * 2 + 2)
                        gated(pe, 0)
                        (scores_full(u, i, h) if u < MAIN else scores_border(u, h)).then_inc(a_s, 1)
                    if 1 <= u <= UNITS:
                        v = u - 1
                        rows, parts, keys, i, h = unit(v)
                        half = keys // 2
                        pe.wait_ge(a_p, base + u)
                        pe.wait_ge(a_ptd, 1 + base + v)
                        pe.wait_ge(a_pta, 1 + base + v)
                        for k in range(2):
                            for n in range(UH * parts):
                                last = tr(ps[0:half, 4 + k, n * rows:n * rows + rows],
                                          pp[0:rows, v % 2, n, k * half:k * half + half], ident[0:rows, 0:rows])
                        last.then_inc(a_t, 1)
                    if u >= 2:
                        v = u - 2
                        rows, parts, keys, i, h = unit(v)
                        pe.wait_ge(a_ptd, 1 + base + v + 1)
                        pe.wait_ge(a_pta, 1 + base + v + 1)
                        pe.wait_ge(a_on, 1 + base + v)
                        for n in range(UH):
                            for t in range(parts):
                                at = (n * parts + t) * rows
                                c = (t * UH + n) * (HD + 1)
                                if parts == 2:
                                    for k in range(2):
                                        last = mm(ps[0:QT, 6, c:c + HD + 1], pt[0:QT, v % 2, k, at:at + QT],
                                                  ve[0:QT, 2 * i + k, h + n, :], start=k == 0, stop=k == 1)
                                else:
                                    for b in range(2):
                                        for k in range(2):
                                            last = mm(ps[64 * b:64 * b + 64, 6, c:c + HD + 1],
                                                      pt[:, v % 2, k, at + 64 * b:at + 64 * b + 64],
                                                      vee[:, b if k == 0 else 2, h + n, :], start=k == 0, stop=k == 1)
                        last.then_inc(a_o, 1)
                    if nxt and u == 11:
                        front_turn(it + 1, NT + 1, (ln_xt_e, it + 1))
                pe.wait_ge(a_on, 1 + base + UNITS)
                for m in range(NT):
                    tr(ps[:, 0, m * QT:m * QT + QT], o[0:QT, m, 0:P], ident[0:QT, 0:QT])
                for m in range(NT):
                    tr(ps[0:R1, 1, m * QT:m * QT + QT], o[0:QT, m, P:D], ident[0:QT, 0:QT])
                tr(ps[:, 2, 0:P], o[:, NT, 0:P], ident[:])
                tr(ps[0:R1, 2, P:2 * P], o[:, NT, P:D], ident[:]).then_inc(o_tr, 1)
                project(it, 0, (3, 4))

            def project(f, which, banks):
                pe.wait_ge(o_td, f + 1)
                pe.wait_ge(o_ta, f + 1)
                for j in range(NT):
                    dst = ps[:, banks[j // 2], (j % 2) * D:(j % 2) * D + D]
                    mm(dst, ot0[:, j * P:j * P + P], wproj[:, which, 0, :], start=True, stop=False)
                    last = mm(dst, ot1[0:R1 + 1, j * P:j * P + P], wproj[0:R1 + 1, which, 1, :], start=False, stop=True)
                    if j % 2:
                        last.then_inc(o_proj, 1)

            pe.wait_ge(setup_pool, 2)
            pe.wait_ge(setup_dve, 3)
            loop(pe, body_a)

            front_turn(PAIRS, NT, (ln_xt_e, PAIRS))
            pe.wait_ge(w_split, NCHUNK)
            pe.wait_ge(ld_l2, 16)

            def body_b(it, nxt):
                pe.wait_ge(ln_split, it + (PAIRS + 1))
                for m in range(MC):
                    pe.wait_ge(b_gelu, 1 + it * MC + max(0, m - 3))
                    product(ps[:, m % 4, :], (CL1 + m * P, CL1 + m * P + P), xcols(0, N)).then_inc(b_h, 1)
                if nxt:
                    front_turn(it + (PAIRS + 1), NT)
                pe.wait_ge(b_gelu, 1 + it * MC + MC)
                pe.wait_ge(b_res, 1 + it * 2)
                for j in range(NT):
                    dst = ps[:, 4 + j // 2, (j % 2) * D:(j % 2) * D + D]
                    mm(dst, ot1[96:97, 0:P], wproj[96:97, 0, 1, :], start=True, stop=False)
                    for m in range(MC):
                        last = mm(dst, hT[:, m, j * P:j * P + P], w2l[:, m, :], start=False, stop=m == MC - 1)
                    if j % 2:
                        last.then_inc(b_y, 1)

            loop(pe, body_b)

            front_turn(2 * PAIRS, NT)

            def body_c(it, nxt):
                pe.wait_ge(ln_split, it + (2 * PAIRS + 1))
                pe.wait_ge(o_res, 1 + it * 2 + 2 * PAIRS)
                for k in range(3):
                    product(ps[:, k, :], (CA + k * P, CA + k * P + P), xcols(0, N)).then_inc(c_qk, 1)
                for j in range(NT):
                    last = product(ps[:, 3 + j // 2, (j % 2) * D:(j % 2) * D + D], (CAV, CAV + D),
                                   xcols(j * P, j * P + P), True)
                    if j % 2:
                        last.then_inc(c_v, 1)
                n = 2 * AH
                base = it * n
                pe.wait_ge(c_qt, it + 1)
                pe.wait_ge(c_ve, it * 2 + 2)
                for u in range(n + 2):
                    if u < n:
                        b, h = u // AH, u % AH
                        if u >= 2:
                            pe.wait_ge(c_p, base + u - 1)
                        if h < 2:
                            rows = slice(AD * h, AD * h + AD)
                            q, k = cqk[rows, 0, :], cqk[rows, 1, :]
                        else:
                            q, k = cq2[0:AD, 0, :], cq2[0:AD, 1, :]
                        t0 = b * T
                        mm(ps[:, u % 2, 0:P], q[:, t0:t0 + P], k[:, t0:t0 + P], start=True, stop=False)
                        mm(ps[:, u % 2, 0:P], identb[:], maskb[:], start=False, stop=True)
                        mm(ps[:, u % 2, P:3 * P], q[:, t0 + P:t0 + T], k[:, t0:t0 + T], start=True, stop=False)
                        mm(ps[:, u % 2, 2 * P:3 * P], identb[:], maskb[:], start=False, stop=True).then_inc(c_s, 1)
                    if 1 <= u <= n:
                        v = u - 1
                        pe.wait_ge(c_p, base + u)
                        if v >= 2:
                            pe.wait_ge(c_pt, base + v - 1)
                        for k in range(3):
                            last = tr(ps[:, 3 + v % 2, k * P:k * P + P], cp[:, v % 2, k * P:k * P + P], ident[:])
                        last.then_inc(c_t, 1)
                    if u >= 2:
                        v = u - 2
                        b, h = v // AH, v % AH
                        pe.wait_ge(c_pt, base + v + 1)
                        if v >= 2:
                            pe.wait_ge(c_on, base + v - 1)
                        bank = ps[:, 5 + v % 2, :]
                        mm(bank[:, 0:AD + 1], cpt[:, v % 2, 0:P], cv[:, 2 * b, h, :], start=True, stop=True)
                        mm(bank[:, AD + 1:2 * AD + 2], cpt[:, v % 2, P:2 * P], cv[:, 2 * b, h, :], start=True, stop=False)
                        mm(bank[:, AD + 1:2 * AD + 2], cpt[:, v % 2, 2 * P:3 * P], cv[:, 2 * b + 1, h, :], start=False,
                           stop=True).then_inc(c_o, 1)
                    if nxt and u == 5:
                        front_turn(it + (2 * PAIRS + 1), NT)
                pe.wait_ge(c_on, base + n)
                for j in range(NT):
                    tr(ps[:, 0, j * P:j * P + P], co[:, j, 0:P], ident[:])
                for j in range(NT):
                    last = tr(ps[0:R1, 1, j * P:j * P + P], co[:, j, P:D], ident[:])
                last.then_inc(o_tr, 1)
                project(it + PAIRS, 1, (2, 3))

            loop(pe, body_c)

            front_turn(3 * PAIRS, NT)
            pe.wait_ge(ld_w2, 32)

            def body_d(it, nxt):
                pe.wait_ge(ln_split, it + (3 * PAIRS + 1))
                for b in range(2):
                    i2 = it * 2 + b
                    for j in range(2):
                        n = 2 * b + j
                        i4 = it * 4 + n
                        if b:
                            pe.wait_ge(d_sle, i2 * 4)
                            pe.wait_ge(d_ss, 1 + i2 * 2)
                        else:
                            pe.wait_ge(d_res, 1 + it * NT)
                        for c in range(2):
                            last = product(ps[:, 2 * j + c, :], (CPHI + 512 * c, CPHI + 512 * c + 512),
                                           xcols(n * P, n * P + P), True)
                        last.then_inc(d_l, 1)
                    for j in range(2):
                        n = 2 * b + j
                        i4 = it * 4 + n
                        pe.wait_ge(d_c, i4 + 1)
                        pe.wait_ge(d_cte, 1 + i4)
                        for s in range(ST):
                            last = tr(ps[:, 4 + s // 4, (s % 4) * P:(s % 4) * P + P], cc[:, j, s * P:s * P + P], ident[:])
                        last.then_inc(d_ct, 1)
                    pe.wait_ge(d_lsb, i2 * 2 + 2)
                    for k in range(4):
                        for s in range(2):
                            for j in range(2):
                                last = tr(ps[:, k, s * T + j * P:s * T + j * P + P],
                                          lsb[:, j, (2 * k + s) * P:(2 * k + s) * P + P], ident[:])
                        last.then_inc(d_lt, 1)
                    pe.wait_ge(d_cte, 1 + i2 * 2 + 2)
                    pe.wait_ge(d_dt, i2 * 4 + 4)
                    for j in range(2):
                        if j:
                            pe.wait_ge(d_de, i2 * 2 + 1)
                        for s in range(ST):
                            last = tr(ps[:, 4 + s // 4, (s % 4) * P:(s % 4) * P + P], dt_[:, s, j * P:j * P + P], ident[:])
                        last.then_inc(d_dtr, 1)
                    pe.wait_ge(d_de, i2 * 2 + 2)
                    for k in range(4):
                        for s in range(2):
                            st = 2 * k + s
                            for j in range(2):
                                last = mm(ps[:, k, s * D:s * D + D], dd[:, j, st * P:st * P + P], xn[:, 2 * b + j, 0:D],
                                          start=j == 0, stop=j == 1)
                        last.then_inc(d_sl, 1)
                    for h in range(2):
                        pe.wait_ge(d_sle, i2 * 4 + 2 * h + 2)
                        for part in range(2):
                            bank = ((4, 6)[h], (5, 0)[h])[part]
                            for s in range(4):
                                last = tr(ps[:, bank, s * P:s * P + P], sl[:, 4 * h + s, part * P:part * P + P], ident[:])
                        last.then_inc(d_st, 1)
                if nxt:
                    front_turn(it + (3 * PAIRS + 1), NT)
                pe.wait_ge(d_ss, 1 + it * 4 + 4)
                for e in range(NE):
                    for m in range(MC):
                        pe.wait_ge(d_gelu, 1 + it * NE * MC + max(0, e * MC + m - 3))
                        product(ps[:, (e * MC + m) % 4, :], (CW1 + (e * MC + m) * P, CW1 + (e * MC + m) * P + P),
                                scols(512 * e, 512 * e + 512)).then_inc(d_h, 1)
                    pe.wait_ge(d_gelu, 1 + it * NE * MC + e * MC + MC)
                    pe.wait_ge(d_ye, 1 + it * 2 * NE + 2 * e)
                    for b in range(2):
                        for s in range(2):
                            for m in range(MC):
                                last = mm(ps[:, 4 + b, s * D:s * D + D], hTd[:, m, b * T + s * P:b * T + s * P + P],
                                          w2x[:, e * MC + m, :], start=m == 0, stop=m == MC - 1)
                        last.then_inc(d_y, 1)
                pe.wait_ge(d_ye, 1 + it * 2 * NE + 2 * NE)
                pe.wait_ge(d_gelu, 1 + it * NE * MC + NE * MC)
                for n in range(NT):
                    for s in range(ST):
                        last = mm(ps[:, (6, 0)[n // 2], (n % 2) * D:(n % 2) * D + D], ct[:, s, n * P:n * P + P],
                                  yy[:, n // 2, s, :], start=s == 0, stop=s == ST - 1)
                    if n % 2:
                        last.then_inc(d_o, 1)

            loop(pe, body_d)


INPUTS = ("x", "xe", "wall0", "wall1", "rel", "wp", "w2a", "w2e", "bias_cols", "bias_rows", "b2r", "c_ident", "c_cw",
          "c_oh", "c_ohp", "c_kw", "c_kwe", "c_mask")


def lay_out(v):
    import numpy as np

    f = np.float32
    v = {k.replace("L0_conv_", "c_").replace("L1_attn_", "a_").replace("L1_ffn_", "f_"): np.asarray(a) for k, a in v.items()}
    x = v["x"].astype(f, copy=False)
    border = np.concatenate([x[:, :, WS:W].reshape(B, -1, D), x[:, WS:H].reshape(B, -1, D)], 1)

    def spread(w):
        out = np.zeros((w.shape[0], G, HG, 32), f)
        out[..., 0:HD] = w.reshape(-1, G, HG, HD)
        return out.reshape(w.shape[0], G * P)

    qkv, aq = v["c_qkv_w"], v["a_W_qkv"]
    wall = np.concatenate([
        spread(qkv[:, 0:D]), spread(qkv[:, D:2 * D]), qkv[:, 2 * D:], v["c_lin1_w"],
        aq[:, 0:P], aq[:, D:D + P], aq[:, P:D], aq[:, D + P:2 * D], aq[:, 2 * D:],
        v["f_phi"].reshape(NE * NS, D).T, v["f_w1"].transpose(1, 0, 2).reshape(D, NE * MLP)], 1)
    rel = np.zeros((HG, 32, 2 * WS, 32), f)
    for y in range(WS):
        for c in range(HD):
            rel[:, c, y, c] = 1
        for k in range(WS):
            rel[:, 0:HD, y, HD + k] = v["c_rel_pos_h"][y - k + WS - 1]
            rel[:, 0:HD, WS + y, k] = v["c_rel_pos_w"][y - k + WS - 1]
    wp = np.zeros((P, 2, 2, D), f)
    for n, (w, b) in enumerate(((v["c_proj_w"], v["c_proj_b"]), (v["a_W_out"], v["a_b_out"]))):
        wp[:, n, 0], wp[0:R1, n, 1], wp[R1, n, 1] = w[0:P], w[P:], b
    wp[96, 0, 1] = v["c_lin2_b"]
    cols = np.zeros((P, 48), f)
    cb, ab = v["c_qkv_b"], v["a_b_qkv"]
    cols[:, 0:G] = spread(cb[None, 0:D]).reshape(G, P).T
    cols[:, G:2 * G] = spread(cb[None, D:2 * D]).reshape(G, P).T
    for at, w, b in ((N1, v["c_n1_w"], v["c_n1_b"]), (N2, v["c_n2_w"], v["c_n2_b"])):
        cols[:, at], cols[:, at + 1] = w[0:P], np.concatenate([w[P:], w[P:]])
        cols[:, at + 2], cols[:, at + 3] = b[0:P], np.concatenate([b[P:], b[P:]])
    cols[:, 10], cols[0:AD, 11], cols[:, 12], cols[AD:P, 13] = ab[0:P], ab[P:D], ab[D:D + P], ab[D + P:2 * D]
    cols[:, L1B:L1B + MC] = v["c_lin1_b"].reshape(MC, P).T
    cols[:, E1B:E1B + NE * MC] = v["f_b1"].reshape(NE * MC, P).T
    rows = np.concatenate([cb[None, 2 * D:], ab[None, 2 * D:], v["f_b2"]])
    oh, kw = np.zeros((HG, 32, H, W), f), np.zeros((HG, 32, H, W), f)
    cw = np.zeros((HG, 32, W, H), f)
    for y in range(H):
        for xx in range(W):
            oh[:, HD + y % WS, y, xx] = 1
            kw[:, xx % WS, y, xx] = 1
            if y >= WS or xx >= WS:
                cw[:, WS + 2 * (y >= WS) + (xx >= WS) - 1, xx, y] = 1
    window = lambda y, xx: 2 * (y >= WS) + (xx >= WS) - 1
    keys = [(y, xx) for y in range(H) for xx in range(WS, W)] + [(y, xx) for y in range(WS, H) for xx in range(W)]
    pads = [(y, xx) for y in range(WS) for xx in range(WS) if y >= EW or xx >= EW]
    kwe, ohp = np.zeros((HG, 32, EKEYS), f), np.zeros((HG, 32, EPAD), f)
    for n, (y, xx) in enumerate(keys):
        kwe[:, xx % WS, n] = 1
        twice = n < EREAL // 2 and y >= WS
        for w in range(3):
            kwe[:, WS + w, n] = 0 if w == window(y, xx) and not twice else NEG
    for n, (y, xx) in enumerate(pads):
        kwe[:, xx, EREAL + n] = 1
        ohp[:, HD + y, n] = 1
        for w, real in enumerate((xx < EW, y < EW, False)):
            kwe[:, WS + w, EREAL + n] = NEG if real else 0
    mask = np.where(np.arange(P)[None] > np.arange(P)[:, None], NEG, 0).astype(f)
    got = dict(
        x=x.reshape(B * T, D), xe=border.reshape(PAIRS, P, D), wall0=wall[0:P], wall1=np.concatenate([wall[P:], wall[P:]]),
        rel=rel.reshape(P, 2 * WS, 32), wp=wp, w2a=v["c_lin2_w"].reshape(MC, P, D).transpose(1, 0, 2),
        w2e=v["f_w2"].reshape(NE * MC, P, D).transpose(1, 0, 2), bias_cols=cols,
        bias_rows=np.broadcast_to(rows[None, 0:2], (P, 2, D)), b2r=np.broadcast_to(rows[None, 2:], (P, NE, D)), c_ident=np.eye(P, dtype=f), c_cw=cw.reshape(P, W, H),
        c_oh=oh.reshape(P, T), c_ohp=ohp.reshape(P, EPAD), c_kw=kw.reshape(P, T), c_kwe=kwe.reshape(P, EKEYS), c_mask=mask)
    return {k: np.ascontiguousarray(a) for k, a in got.items()}


def kernel(**inputs):
    import concourse.bacc as bacc
    from concourse.bass_utils import run_bass_kernel_spmd

    laid = lay_out(inputs)
    nc = bacc.Bacc("TRN2", target_bir_lowering=False, num_devices=1)
    args = {k: nc.dram_tensor("in_" + k, laid[k].shape, F32, kind="ExternalInput").ap() for k in INPUTS}
    out = nc.dram_tensor("out", (B * T, D), F32, kind="ExternalOutput").ap()
    build(nc, **args, out=out)
    r = run_bass_kernel_spmd(nc, [{"in_" + k: laid[k] for k in INPUTS}], core_ids=[0])
    return r.results[0]["out"].reshape(B, H, W, D)
```

```python
from contextlib import ExitStack

import concourse.bass as bass
from concourse import mybir

P = 128
F32 = mybir.dt.float32
F32R = mybir.dt.float32r
BF16 = mybir.dt.bfloat16
ALU = mybir.AluOpType
ACT = mybir.ActivationFunctionType
AX = mybir.AxisListType

B, H, W, D = 8, 16, 16, 192
T = H * W
TT = T // P
PAIRS = B // 2
NT = 2 * TT
N = NT * P
R1 = D - P
MLP = 4 * D
MC = MLP // P
WS, NH, HD = 14, 12, 16
G, HG = 3, 4
HP = NH // 2
HALF = WS // 2
QT = HALF * WS
QR = HALF * W
EW = W - WS
EREAL = 2 * H * EW
EPAD = WS * WS - EW * EW
EKEYS = EREAL + EPAD
UH = 2
MAIN = 2 * NH // UH
UNITS = MAIN + NH // UH
H_BANKS = 0, 2, 1, 3
REL_BANKS = (2, 4, 5, 1), (7, 3, 6, 0)
AH, AD = 3, 64
NE, NS = 4, 256
ST = NE * NS // P
CQ, CK, CV = 0, G * P, 2 * G * P
CL1 = CV + D
CA = CL1 + MLP
CAV = CA + 3 * P
CPHI = CA + 3 * D
CW1 = CPHI + NE * NS
WALL = CW1 + NE * MLP
CHUNK = 256
N1, N2, L1B, E1B = 6, 14, 18, 24
NCHUNK = WALL // CHUNK
QKV_CHUNKS = -(-CL1 // CHUNK)
QKV = QKV_CHUNKS * CHUNK
A_CHUNKS = CW1 // CHUNK
VB = 7 * HD
EPS = 1e-5
NEG = -1.0e30


def build(nc, x, xe, wall0, wall1, rel, wp, w2a, w2e, bias_cols, bias_rows, b2r, c_ident, c_keys,
          c_border, c_mask, out):
    with ExitStack() as ctx:
        def sb(name, shape, dt=F32):
            return ctx.enter_context(nc.sbuf_tensor(name, shape, dt))

        def sem(name):
            return ctx.enter_context(nc.semaphore(name))

        xres = sb("xres", [P, B * TT, D])
        ws = sb("ws", [P, 4, CW1], F32R)
        with nc.sbuf_tensor("room", [P, 4 * (WALL - CW1)], F32) as room:
            pass
        wx = sb("wx", [P, 4, WALL - CW1], F32R)
        xs = sb("xs", [P, 3, N + P + 4 * QT], F32R)
        ident = sb("ident", [P, P])
        wproj = sb("wproj", [P, 2, 2, D])
        bcol = sb("bcol", [P, 48])
        brow = sb("brow", [P, 2, D])
        stage = sb("stage", [P, 2, CHUNK])
        st6 = sb("st6", [P, NT + 1, 6])
        mv = sb("mv", [P, NT + 1, 2])
        rstd = sb("rstd", [P, NT + 1])
        mhalf = sb("mhalf", [P, NT + 1])
        xn = sb("xn", [P, NT + 1, 256])
        xt = sb("xt", [P, 2, N + P])
        nm = sb("nm", [P, 2, HG])
        rs = sb("rs", [P, 2, HG])
        cnm = nm.rearrange("p a b -> p (a b)").rearrange("p (a b) -> p a b", b=2)
        AREA = 16640
        area = sb("area", [P, AREA])
        ps = ctx.enter_context(nc.psum_tensor("ps", [P, 8, 512], F32))

        def views(spec):
            got, at = [], 0
            for shape in spec:
                size = 1
                for n in shape:
                    size *= n
                v = area[:, at:at + size]
                if len(shape) == 2:
                    v = v.rearrange("p (a b) -> p a b", b=shape[1])
                elif len(shape) == 3:
                    v = v.rearrange("p (a b c) -> p a b c", b=shape[1], c=shape[2])
                elif len(shape) == 4:
                    v = v.rearrange("p (a b c d) -> p a b c d", b=shape[1], c=shape[2], d=shape[3])
                got.append(v)
                at += size
            assert at <= AREA, at
            return got

        (qs, qb, ka, kae, pp, pt, xedge) = views([
            (2 * HP, T), (2 * HP, EREAL), (HP, 2, T), (HP, 2, EKEYS), (2, 2 * UH, EKEYS), (2, 2, 512), (D,)])
        ve = room[:, 0:NT * HP * VB].rearrange("p (t a c) -> p t a c", a=HP, c=VB)
        vee = room[:, NT * HP * VB:(NT + 3) * HP * VB].rearrange("p (t a c) -> p t a c", a=HP, c=VB)
        den = room[:, (NT + 3) * HP * VB:(NT + 3) * HP * VB + 2 * N].rearrange("p (u n) -> p u n", u=2)
        at = (NT + 3) * HP * VB + 2 * N
        relt = room[:, at:at + 2 * W * P].rearrange("p (a b) -> p a b", b=P)
        first = pp.rearrange("p a b c -> p (a b c)")[:, 0:2 * QKV].rearrange("p (k c) -> p k c", k=2)
        kc, kec = pt[:, 0, 1, 0:T], pt[:, 1, 0, 0:EKEYS]
        qraw = pp.rearrange("p a b c -> p (a b c)")[:, 0:G * N].rearrange("p (g n) -> p g n", g=G)
        (hT, w2l) = views([(MC, N), (MC, D)])
        (cqk, cq2, cv, cp, cpt, co) = views([(2, N), (2, N), (NT, AH, AD + 1), (2, 3 * P), (2, 3 * P), (NT, D)])
        (cc, _, ct, dt_, w2x, b2row) = views([(2, NE * NS), (1024,), (ST, N), (2, ST, T), (NE * MC, D), (NE, D)])
        dd = cc, dt_[:, 0].rearrange("p s t -> p (s t)").rearrange("p (j c) -> p j c", j=2)
        yy = area[:, 0:2 * ST * D].rearrange("p (b s d) -> p b s d", b=2, d=D)
        dstart = 2 * NE * NS + 1024 + ST * N
        hTd = area[:, dstart:dstart + MC * N].rearrange("p (a b) -> p a b", b=N)
        slots = [ws[:, k, 0:NE * 2 * NS] for k in range(3)]
        dstat = sb("dstat", [P, 6, 2 * ST])
        identb = sb("identb", [P, P], BF16)
        maskb = sb("maskb", [P, P], BF16)
        ot0, ot1 = area[:, AREA - 2 * N:AREA - N], area[:, AREA - N:AREA]

        ld_x, ld_w, ld_c, ld_l2, ld_w2 = sem("ld_x"), sem("ld_w"), sem("ld_c"), sem("ld_l2"), sem("ld_w2")
        ld_p, ld_e, ld_q, ld_r = sem("ld_p"), sem("ld_e"), sem("ld_q"), sem("ld_r")
        setup_dve, setup_pool, setup_act = sem("setup_dve"), sem("setup_pool"), sem("setup_act")
        dve_own, pool_own = sem("dve_own"), sem("pool_own")
        w_split, q_hi, q_lo = sem("w_split"), sem("q_hi"), sem("q_lo")
        ln_mv, ln_rstd, ln_xn = sem("ln_mv"), sem("ln_rstd"), sem("ln_xn")
        ln_tr, ln_tr_e, ln_xt, ln_xt_e, ln_split = sem("ln_tr"), sem("ln_tr_e"), sem("ln_xt"), sem("ln_xt_e"), sem("ln_split")
        a_q, a_k, a_v, a_qraw, a_ka, a_ve, a_kae = (sem(n) for n in ("a_q", "a_k", "a_v", "a_qraw", "a_ka", "a_ve", "a_kae"))
        a_rel, a_qa, a_qw, a_kb, a_qb = (sem(n) for n in ("a_rel", "a_qa", "a_qw", "a_kb", "a_qb"))
        a_s, a_nm, a_p, a_t, a_ptd, a_pta, a_o, a_on = (sem(n) for n in ("a_s", "a_nm", "a_p", "a_t", "a_ptd", "a_pta", "a_o", "a_on"))
        o_tr, o_td, o_ta, o_proj, o_res = (sem(n) for n in ("o_tr", "o_td", "o_ta", "o_proj", "o_res"))
        b_h, b_gelu, b_y, b_res = (sem(n) for n in ("b_h", "b_gelu", "b_y", "b_res"))
        c_qk, c_v, c_qt, c_ve, c_s, c_nm, c_p, c_t, c_pt, c_o, c_on = (
            sem(n) for n in ("c_qk", "c_v", "c_qt", "c_ve", "c_s", "c_nm", "c_p", "c_t", "c_pt", "c_o", "c_on"))
        d_l, d_nrm, d_c, d_ct, d_cte, d_lt, d_ncm, d_dt, d_own, d_dn, d_dtr, d_de, d_da, d_st, d_sh, d_ss = (
            sem("d_" + n) for n in ("l", "nrm", "c", "ct", "cte", "lt", "ncm", "dt", "own", "dn", "dtr", "de", "da", "st", "sh", "ss"))
        d_h, d_gelu, d_y, d_ye, d_o, d_res, stored = (sem(n) for n in ("d_h", "d_gelu", "d_y", "d_ye", "d_o", "d_res", "stored"))

        mm = nc.tensor.matmul

        def product(out_, wcols, xcols, weights_moving=False):
            x0, x1, x2 = xcols
            c0, c1 = wcols
            w_ = ws[:, :, c0:c1] if c0 < CW1 else wx[:, :, c0 - CW1:c1 - CW1]
            pairs = [(w_[:, 0], x0), (w_[:, 1], x0), (w_[:, 0], x1), (w_[:, 2], x2), (w_[0:R1, 3], x2[0:R1])]
            for n, (wp_, xp_) in enumerate(pairs):
                l, r = (xp_, wp_) if weights_moving else (wp_, xp_)
                last = mm(out_, l, r, start=n == 0, stop=n == len(pairs) - 1)
            return last

        def xcols(a, b):
            return [xs[:, k, a:b] for k in range(3)]

        def scols(a, b):
            return [s[:, a:b] for s in slots]

        def loop(eng, body):
            with eng.Fori(0, PAIRS - 1) as it:
                body(it, True)
            body(PAIRS - 1, False)

        a_xw, a_own, c_own, ln_hi = sem("a_xw"), sem("a_own"), sem("c_own"), sem("ln_hi")

        def unit(u):
            if u < MAIN:
                return QR, 2, 2 * QT, u // HP, u % HP
            return P, 1, EKEYS, None, u - MAIN

        def operands(a):
            return a % 2 * G + a // 2

        from_one = dict(pe=(a_v, a_s, b_y, d_st, d_o, d_y, o_proj), dve=(o_res, b_res, a_ptd, a_on, d_res, d_ye, d_ss), act=(b_gelu, d_cte, d_gelu, a_pta))

        def start_counts(eng, name):
            for s_ in from_one[name]:
                eng.sem_inc(s_, 1)

        def slot_cols(t, b, h):
            return t.rearrange("p (e b s) -> p e b s", e=NE, b=2)[:, 2 * h:2 * h + 2, b, :]

        gate = [sem(f"gate_{n}") for n in ("pe", "dve", "pool")]

        def gated(eng, n):
            eng.sem_inc(gate[n], 1)

        def position_terms(copy, cols, q):
            got = ps[:, REL_BANKS[cols][q], 0:384].rearrange("p (k a x) -> p a k x", k=4, a=2 * G)
            for r in range(HG):
                rows = slice(64 * (r % 2) + 32 * cols, 64 * (r % 2) + 32 * cols + 32)
                to = qs[rows, r // 2 * 2 * G:(r // 2 + 1) * 2 * G].rearrange("p a (y x) -> p a y x", x=W)
                to = to.rearrange("p a y x -> p a x y") if cols else to
                last = copy(to[:, :, 4 * q:4 * q + 4, :], got[32 * r:32 * r + 32])
            return last

        block = ctx.enter_context(nc.Block())

        @block.sync
        def _(sp):
            sp.dma_start(xres[:, 0:NT, :], x[0:N].rearrange("(t p) d -> p t d", p=P)).then_inc(ld_x, 16)
            sp.dma_start(xedge, xe[0]).then_inc(ld_x, 16)
            for k, wall in enumerate((wall0, wall1)):
                sp.dma_start(first[:, k], wall[:, 0:QKV]).then_inc(ld_q, 16)
            for dst, src in ((ident[:], c_ident), (bcol[:], bias_cols), (brow[:], bias_rows), (kc, c_keys),
                             (kec, c_border), (pt[:, 0, 0, 0:P], c_mask)):
                sp.dma_start(dst, src).then_inc(ld_c, 16)
            sp.wait_ge(setup_pool, 3)
            for r in range(HG):
                q = slice(32 * r, 32 * r + 32)
                sp.dma_start(relt[q, :, q], rel[q]).then_inc(ld_p, 16)
            sp.dma_start(xres[:, NT:, :], x[N:].rearrange("(t p) d -> p t d", p=P)).then_inc(ld_r, 16)
            sp.dma_start(wproj[:], wp).then_inc(ld_r, 16)
            for n in range(1, PAIRS):
                sp.wait_ge(ln_xn, n)
                sp.dma_start(xedge, xe[n]).then_inc(ld_e, 16)
            sp.wait_ge(o_res, 1 + 2 * PAIRS)
            sp.dma_start(w2l, w2a).then_inc(ld_l2, 16)
            sp.wait_ge(o_res, 1 + 4 * PAIRS)
            sp.dma_start(w2x, w2e).then_inc(ld_w2, 16)
            sp.dma_start(b2row, b2r).then_inc(ld_w2, 16)
            for it in range(PAIRS):
                sp.wait_ge(d_res, 1 + NT * (it + 1))
                sp.dma_start(out[it * N:(it + 1) * N].rearrange("(t p) d -> p t d", p=P),
                             xres[:, it * NT:(it + 1) * NT, :]).then_inc(stored, 16)
            sp.wait_ge(stored, 16 * PAIRS)

        @block.gpsimd
        def _(pool):
            own = [0]

            def step(ins):
                own[0] += 1
                ins.then_inc(pool_own, 1)

            nc.gpsimd.memset(mhalf[:], -0.5).then_inc(setup_pool, 1)
            pool.wait_ge(setup_pool, 1)
            nc.gpsimd.memset(ot1[R1:P, :], 1.0).then_inc(setup_pool, 1)
            pool.wait_ge(setup_pool, 2)
            nc.gpsimd.memset(relt.rearrange("p a b -> p (a b)"), 0.0).then_inc(setup_pool, 1)
            pool.wait_ge(setup_pool, 3)

            def norm_scale(f, tiles, k):
                pool.wait_ge(ln_mv, f + 1)
                gated(pool, 2)
                nc.gpsimd.tensor_scalar(rstd[:, 0:tiles], mv[:, 0:tiles, 1], EPS, 1.0, ALU.add, ALU.mult).then_inc(pool_own, 1)
                pool.wait_ge(pool_own, k)
                nc.gpsimd.tensor_tensor(rstd[:, 0:tiles], rstd[:, 0:tiles], mhalf[:, 0:tiles], ALU.pow).then_inc(ln_rstd, 1)

            def split_chunk(c, k):
                pool.wait_ge(ld_w, (c - QKV_CHUNKS) * 32 + 32)
                gated(pool, 2)
                to, cols = ws, bass.ds(c * CHUNK, CHUNK)
                if isinstance(c, int) and c >= A_CHUNKS:
                    to, cols = wx, bass.ds(c * CHUNK - CW1, CHUNK)
                nc.gpsimd.tensor_copy(to[:, 0, cols], stage[:, 0, :]).then_inc(pool_own, 1)
                nc.gpsimd.tensor_copy(to[:, 2, cols], stage[:, 1, :]).then_inc(pool_own, 1)
                pool.wait_ge(pool_own, k + 2)
                nc.gpsimd.tensor_tensor(to[:, 1, cols], stage[:, 0, :], to[:, 0, cols].bitcast(F32), ALU.subtract).then_inc(pool_own, 1)
                nc.gpsimd.tensor_tensor(to[0:R1, 3, cols], stage[0:R1, 1, :], to[0:R1, 2, cols].bitcast(F32), ALU.subtract).then_inc(pool_own, 1)
                pool.wait_ge(pool_own, k + 4)
                pool.sem_inc(w_split, 1)
                if isinstance(c, int) and c == NCHUNK - 1:
                    return
                cols2 = bass.ds((c + 1) * CHUNK, CHUNK)
                pool.dma_start(stage[:, 0, :], wall0[:, cols2]).then_inc(ld_w, 16)
                pool.dma_start(stage[:, 1, :], wall1[:, cols2]).then_inc(ld_w, 16)

            norm_scale(0, NT + 1, 1)
            pool.dma_start(stage[:, 0, :], wall0[:, QKV:QKV + CHUNK]).then_inc(ld_w, 16)
            pool.dma_start(stage[:, 1, :], wall1[:, QKV:QKV + CHUNK]).then_inc(ld_w, 16)
            k = 1
            k0 = k
            rest = A_CHUNKS - QKV_CHUNKS
            per = rest // (PAIRS - 1)
            assert per * (PAIRS - 1) == rest

            def body(it, nxt, chunks):
                n = 4 * per + 1
                base = it * n + k0
                pool.wait_ge(ln_split, it + 1)
                pool.wait_ge(a_v, 1 + it * 3)
                gated(pool, 2)
                for k in range(3):
                    nc.gpsimd.tensor_copy(xs[:, k, N + P:].rearrange("p (i y x) -> p i y x", i=2, x=WS),
                                          xs[:, k, 0:N].bitcast(F32).rearrange("p (i y x) -> p i y x", i=2, x=W)[:, :, 0:WS, 0:WS])\
                        .then_inc(a_xw, 1)
                pool.wait_ge(a_ka, it + 1)
                pool.wait_ge(a_kb, it * 2 + 2)
                pool.wait_ge(a_s, 1 + it * UNITS)
                gated(pool, 2)
                kf = ka.rearrange("p g i t -> p (g i) t")
                kef = kae.rearrange("p g i t -> p (g i) t")
                nc.gpsimd.tensor_copy(kef[:, :, 0:WS * EW].rearrange("p a (y x) -> p a y x", x=EW),
                                      kf[:, :, 0:WS * W].rearrange("p a (y x) -> p a y x", x=W)[:, :, :, WS:W]).then_inc(a_kae, 1)
                nc.gpsimd.tensor_copy(kef[:, :, EREAL // 2:EREAL], kf[:, :, WS * W:T]).then_inc(a_kae, 1)
                pool.wait_ge(a_qa, it * 4 + 4)
                pool.wait_ge(a_qw, it * 4 + 4)
                gated(pool, 2)
                nc.gpsimd.tensor_copy(qb[:, :, 0:EREAL // 2].rearrange("p a (y x) -> p a y x", x=EW),
                                      qs.rearrange("p a (y x) -> p a y x", x=W)[:, :, :, WS:W]).then_inc(a_qb, 1)
                nc.gpsimd.tensor_copy(qb[:, :, EREAL // 2:EREAL], qs[:, :, WS * W:T]).then_inc(a_qb, 1)
                if nxt:
                    norm_scale(it + 1, NT + 1, base + 1)
                for c in range(chunks):
                    split_chunk(it * per + QKV_CHUNKS + c, base + nxt + 4 * c)

            with pool.Fori(0, PAIRS - 1) as it:
                body(it, True, per)
            body(PAIRS - 1, False, 0)
            k1 = (PAIRS - 1) * (4 * per + 1) + k0
            chunk = A_CHUNKS
            for ph in range(1, 4):
                for n in range(PAIRS):
                    k1 += 1
                    norm_scale(4 * ph + n, NT, k1)
                    upto = min(NCHUNK, A_CHUNKS + max(0, 4 * ph + n - 4) + 2 * max(0, 4 * ph + n - 8))
                    if ph == 1 and n == 1:
                        pool.wait_ge(o_res, 1 + 2 * PAIRS)
                    while chunk < upto:
                        split_chunk(chunk, k1)
                        k1 += 4
                        chunk += 1

        @block.vector
        def _(dve):
            V = nc.vector
            start_counts(dve, "dve")

            def tiles_of(n, tiles):
                return [xres[:, n * NT + j, :] for j in range(NT)] + ([xedge] if tiles > NT else [])

            def front_norm(f, n, tiles, used=()):
                front_stats(f, n, tiles)
                front_scale(f, n, tiles, range(tiles), used)

            def front_stats(f, n, tiles):
                xt_ = tiles_of(n, tiles)
                if not isinstance(f, int):
                    dve.wait_ge(ld_r, 32)
                if tiles > NT:
                    dve.wait_ge(ld_e, 16 * n)
                for j in range(tiles):
                    last = V.bn_stats(st6[:, j, :], xt_[j])
                last.then_inc(dve_own, 1)
                dve.wait_ge(dve_own, f + 1)
                gated(dve, 1)
                for j in range(tiles):
                    last = V.bn_aggr(mv[:, j, :], st6[:, j, :])
                last.then_inc(ln_mv, 1)

            def front_scale(f, n, tiles, js, used=()):
                xt_ = tiles_of(n, tiles)
                if js[0] == 0:
                    dve.wait_ge(ln_rstd, f + 1)
                    dve.wait_ge(ln_tr, 2 * f)
                    for s_, v_ in used:
                        dve.wait_ge(s_, v_)
                for j in js:
                    V.tensor_scalar(xn[:, j, 0:D], xt_[j], mv[:, j, 0:1], rstd[:, j:j + 1], ALU.subtract, ALU.mult)
                    last = V.tensor_scalar(xn[:, j, D:256], xt_[j][:, P:D], mv[:, j, 0:1], rstd[:, j:j + 1],
                                           ALU.subtract, ALU.mult)
                if js[-1] == tiles - 1:
                    last.then_inc(ln_xn, 1)

            def front_split(f, tiles, *used, parts=(0, 1, 2)):
                c = tiles * P
                if 0 in parts:
                    dve.wait_ge(ln_xt, 2 * f + 2)
                    if tiles > NT:
                        dve.wait_ge(ln_xt_e, f + 1)
                    for s_, v_ in used:
                        dve.wait_ge(s_, v_)
                    V.tensor_copy(xs[:, 0, 0:c], xt[:, 0, 0:c])
                    V.tensor_copy(xs[:, 2, 0:c], xt[:, 1, 0:c]).then_inc(ln_hi, 1)
                if 1 in parts:
                    dve.wait_ge(ln_hi, f + 1)
                    V.tensor_tensor(xs[:, 1, 0:c], xt[:, 0, 0:c], xs[:, 0, 0:c].bitcast(F32), ALU.subtract)
                if 2 in parts:
                    V.tensor_tensor(xs[R1:P, 2, 0:c], xt[R1:P, 1, 0:c], xs[R1:P, 2, 0:c].bitcast(F32), ALU.subtract)\
                        .then_inc(ln_split, 1)

            def residual(it, banks, ready, n0, done):
                for b in range(2):
                    dve.wait_ge(ready, 2 * n0 + b + 2)
                    rows = xres[:, bass.ds(it * NT + 2 * b, 2), :]
                    V.tensor_tensor(rows, ps[:, banks[b], 0:2 * D].rearrange("p (t d) -> p t d", d=D), rows,
                                    ALU.add).then_inc(done, 1)

            def heads(v_):
                return v_.rearrange("p a (b c) -> p a b c", c=HD)[:, :, 0:5:4, :]

            dve.wait_ge(ld_x, 32)
            front_norm(0, 0, NT + 1)
            dve.wait_ge(ld_c, 16 * 6)
            V.tensor_scalar(bcol[:, 3:6], bcol[:, 3:6], HD ** -0.5, None, ALU.mult)
            V.tensor_scalar(bcol[:, 10:12], bcol[:, 10:12], AD ** -0.5, None, ALU.mult).then_inc(setup_dve, 1)
            dve.wait_ge(q_hi, 1)
            V.tensor_tensor(ws[:, 1, 0:QKV], first[:, 0], ws[:, 0, 0:QKV].bitcast(F32), ALU.subtract)
            V.tensor_tensor(ws[0:R1, 3, 0:QKV], first[0:R1, 1], ws[0:R1, 2, 0:QKV].bitcast(F32), ALU.subtract).then_inc(q_lo, 1)
            front_split(0, NT + 1)
            V.memset(room[:, 0:(NT + 3) * HP * VB], 0.0).then_inc(setup_dve, 1)
            dve.wait_ge(setup_dve, 2)
            for v_ in (ve, vee):
                V.memset(v_.rearrange("p t a (b c) -> p (t a) b c", c=HD)[:, :, 2:7:4, :], 1.0)
            for s in range(3):
                rows = slice(EREAL, P) if s < 2 else slice(0, P)
                V.tensor_copy(heads(vee[rows, s]), brow[rows, 0, :].rearrange("p (a b c) -> p a b c", b=2, c=HD))
            V.tensor_copy(maskb[:], pt[:, 0, 0, 0:P])
            V.tensor_copy(identb[:], ident[:]).then_inc(setup_dve, 1)

            def body_a(it, nxt):
                for g in (0,):
                    dve.wait_ge(a_k, it * G + g + 1)
                    for r in range(HG):
                        last = V.tensor_scalar(ka[64 * (r % 2):64 * (r % 2) + HD, r // 2 * G + g].rearrange("p i t -> p (i t)"),
                                               ps[32 * r:32 * r + HD, 3 + g, :], HD ** -0.5,
                                               bcol[32 * r:32 * r + HD, 3 + g:4 + g], ALU.mult, ALU.add)
                    last.then_inc(a_ka, 1)
                for i in range(2):
                    dve.wait_ge(a_v, 1 + it * 3 + i + 1)
                    for t in range(2):
                        V.tensor_tensor(heads(ve[0:QT, 2 * i + t]),
                                        ps[0:QT, 6 if i == 0 else 0, t * D:t * D + D].rearrange("p (a b c) -> p a b c", b=2, c=HD),
                                        brow[0:QT, 0, :].rearrange("p (a b c) -> p a b c", b=2, c=HD), ALU.add).then_inc(a_ve, 1)
                dve.wait_ge(a_v, 1 + it * 3 + 3)
                for i in range(2):
                    V.tensor_tensor(heads(vee[0:EREAL, i]),
                                    ps[EREAL * i:EREAL * i + EREAL, 1, 0:D].rearrange("p (a b c) -> p a b c", b=2, c=HD),
                                    brow[0:EREAL, 0, :].rearrange("p (a b c) -> p a b c", b=2, c=HD), ALU.add).then_inc(a_ve, 1)
                for q in range(4):
                    dve.wait_ge(a_rel, it * 4 + q + 1)
                    position_terms(V.tensor_copy, 1, q).then_inc(a_qw, 1)
                base = it * UNITS
                for u in range(UNITS + 2):
                    if u < UNITS:
                        rows, parts, keys, i, h = unit(u)
                        dve.wait_ge(a_s, 1 + base + u + 1)
                        if u >= 2:
                            dve.wait_ge(a_p, base + u - 1)
                        b0 = UH * (u % 2)
                        V.tensor_reduce(nm[0:rows, u % 2, 0:UH * parts],
                                        ps[0:rows, b0:b0 + UH, 0:parts * keys].rearrange("p h (t k) -> p h t k", k=keys),
                                        AX.X, ALU.max, negate=True).then_inc(a_nm, 1)
                    if 1 <= u <= UNITS:
                        rows, parts, keys, i, h = unit(u - 1)
                        half, wide = keys // 2, UH * parts * rows
                        dve.wait_ge(a_t, base + u)
                        if u >= 3:
                            dve.wait_ge(a_o, base + u - 2)
                        V.tensor_copy(pt[0:half, (u - 1) % 2, 0, 0:wide], ps[0:half, 4, 0:wide]).then_inc(a_ptd, 1)
                    if u >= 2:
                        v = u - 2
                        rows, parts, keys, i, h = unit(v)
                        dve.wait_ge(a_o, base + v + 1)
                        n = parts * rows
                        dn = den[0:32, v % 2, 0:n]
                        V.reciprocal(dn, ps[32:64, 6, 0:n]).then_inc(a_own, 1)
                        dve.wait_ge(a_own, base + v + 1)
                        at = slice(32 * (h % 4), 32 * (h % 4) + 32)
                        dst = (ot0 if h < 4 else ot1)[at]
                        if parts == 2:
                            V.tensor_tensor(dst[:, i * T:i * T + n], ps[0:32, 6, 0:n], dn, ALU.mult).then_inc(a_on, 1)
                        else:
                            d3 = dst.rearrange("p (i t) -> p i t", i=2)
                            p3, n3 = (b_.rearrange("p (i t) -> p i t", i=2) for b_ in (ps[0:32, 6, 0:n], dn))
                            V.tensor_tensor(d3[:, :, 0:WS * W].rearrange("p i (y x) -> p i y x", x=W)[:, :, :, WS:W],
                                            p3[:, :, 0:WS * EW].rearrange("p i (y x) -> p i y x", x=EW),
                                            n3[:, :, 0:WS * EW].rearrange("p i (y x) -> p i y x", x=EW), ALU.mult)
                            V.tensor_tensor(d3[:, :, WS * W:T], p3[:, :, EREAL // 2:EREAL], n3[:, :, EREAL // 2:EREAL],
                                            ALU.mult).then_inc(a_on, 1)
                    front = (it + 1, it + 1, NT + 1) if nxt else (PAIRS, 0, NT)
                    if u == 5:
                        front_stats(*front)
                    if u == 7:
                        front_scale(*front, range(0, 3), [(ln_tr_e, it + 1)])
                    if u == 8:
                        front_scale(*front, range(3, front[2]))
                    if 13 <= u < 16:
                        front_split(it + 1, front[2], (a_v, 3 * it + 4), parts=(u - 13,))
                residual(it, (6, 7), o_proj, it, o_res)

            loop(dve, body_a)

            def body_b(it, nxt):
                front_norm(it + (PAIRS + 1), it + 1 if nxt else 0, NT)
                front_split(it + (PAIRS + 1), NT, (b_h, MC * it + MC))
                residual(it, (4, 5), b_y, it, b_res)

            loop(dve, body_b)

            dve.wait_ge(b_res, 1 + 2 * PAIRS)
            V.memset(cv.rearrange("p a b c -> p (a b c)"), 1.0).then_inc(setup_dve, 1)
            dve.wait_ge(setup_dve, 4)

            def body_c(it, nxt):
                for b in range(2):
                    dve.wait_ge(c_v, it * 2 + b + 1)
                    for t in range(2):
                        last = V.tensor_tensor(cv[:, 2 * b + t, :, 0:AD],
                                               ps[:, 3 + b, t * D:t * D + D].rearrange("p (h c) -> p h c", c=AD),
                                               brow[:, 1, :].rearrange("p (h c) -> p h c", c=AD), ALU.add)
                    last.then_inc(c_ve, 1)
                n = 2 * AH
                base = it * n
                for u in range(n + 2):
                    if u < n:
                        dve.wait_ge(c_s, base + u + 1)
                        if u >= 4:
                            dve.wait_ge(c_p, base + u - 3)
                        V.reduce_max(cnm[:, u % 4, 0:1], ps[:, u % 3, 0:P], AX.X, negate=True)
                        V.reduce_max(cnm[:, u % 4, 1:2], ps[:, u % 3, P:3 * P], AX.X, negate=True).then_inc(c_nm, 1)
                    if u >= 2:
                        v = u - 2
                        b, h = v // AH, v % AH
                        dve.wait_ge(c_o, base + v + 1)
                        po = ps[:, 5 + v % 2, 0:2 * (AD + 1)].rearrange("p (t c) -> p t c", c=AD + 1)
                        V.reciprocal(rs[:, v % 2, 0:2], po[:, :, AD]).then_inc(c_own, 1)
                        dve.wait_ge(c_own, base + v + 1)
                        V.tensor_tensor(co[:, 2 * b:2 * b + 2, AD * h:AD * h + AD], po[:, :, 0:AD],
                                        rs[:, v % 2, 0:2].unsqueeze(2).broadcast_to([P, 2, AD]), ALU.mult).then_inc(c_on, 1)
                    front = it + (2 * PAIRS + 1), it + 1 if nxt else 0, NT
                    if u == 0:
                        front_stats(*front)
                    if u in (1, 2):
                        front_scale(*front, range(2 * u - 2, 2 * u))
                    if u >= 5:
                        front_split(it + (2 * PAIRS + 1), NT, (c_v, 2 * it + 2), parts=(u - 5,))
                dve.wait_ge(o_tr, it + 1)
                V.tensor_copy(ot1[0:R1, :], ps[0:R1, 4, :]).then_inc(o_td, 1)
                residual(it, (5, 6), o_proj, it + PAIRS, o_res)

            loop(dve, body_c)

            ncm, csum, rcs, nrm, rsum, rrs = (dstat[:, k, :] for k in range(6))

            def body_d(it, nxt):
                for n in range(NT + 1):
                    if n < NT:
                        dve.wait_ge(d_l, it * NT + n + 1)
                        V.reduce_max(nrm[:, n:n + 1], ps[:, n % 2 * 2:n % 2 * 2 + 2, :].rearrange("p a c -> p (a c)"),
                                     AX.X, negate=True).then_inc(d_nrm, 1)
                        for k in (2 * n, 2 * n + 1):
                            dve.wait_ge(d_lt, it * ST + k + 1)
                            V.tensor_reduce(ncm[:, 2 * k:2 * k + 2], ps[:, 6 + k % 2, :].rearrange("p (b t) -> p b t", b=2),
                                            AX.X, ALU.max, negate=True).then_inc(d_ncm, 1)
                    if n:
                        k = 2 * n - 2
                        dve.wait_ge(d_dt, it * ST + k + 2)
                        V.reciprocal(rcs[:, 2 * k:2 * k + 4], csum[:, 2 * k:2 * k + 4]).then_inc(d_own, 1)
                        dve.wait_ge(d_own, it * NT + n)
                        for st in (k, k + 1):
                            V.tensor_tensor(dt_[:, :, st, :], dt_[:, :, st, :],
                                            rcs[:, 2 * st:2 * st + 2].unsqueeze(2).broadcast_to([P, 2, T]),
                                            ALU.mult).then_inc(d_dn, 1)
                for b in range(2):
                    dve.wait_ge(d_dtr, it * NT + 2 * b + 1)
                    V.tensor_copy(dd[b][:, 0, :], ps[:, (4, 0)[b]:(6, 2)[b], :].rearrange("p a c -> p (a c)")).then_inc(d_de, 1)
                for b in range(2):
                    for h in range(2):
                        dve.wait_ge(d_sh, it * 4 + 2 * b + h + 1)
                        bank = (4, 0)[b] + h
                        V.tensor_tensor(slot_cols(slots[1], b, h), ps[:, bank, :].rearrange("p (e s) -> p e s", e=2),
                                        slot_cols(slots[0], b, h).bitcast(F32), ALU.subtract)
                        V.tensor_tensor(slot_cols(slots[2], b, h)[R1:P],
                                        ps[R1:P, bank + 2, :].rearrange("p (e s) -> p e s", e=2),
                                        slot_cols(slots[2], b, h)[R1:P].bitcast(F32), ALU.subtract).then_inc(d_ss, 1)
                V.reciprocal(rrs[:, 0:NT], rsum[:, 0:NT])
                if nxt:
                    front_norm(it + (3 * PAIRS + 1), it + 1, NT, [(d_st, 1 + 4 * it + 4)])
                for e in range(NE):
                    for b in range(2):
                        dve.wait_ge(d_y, 1 + it * 2 * NE + 2 * e + b + 1)
                        V.tensor_tensor(yy[:, b, 2 * e:2 * e + 2, :],
                                        ps[:, 4 + b, 0:2 * D].rearrange("p (s d) -> p s d", d=D),
                                        b2row[:, e, :].unsqueeze(1).broadcast_to([P, 2, D]), ALU.add).then_inc(d_ye, 1)
                    if nxt and e == 3:
                        front_split(it + (3 * PAIRS + 1), NT, (d_l, NT * it + NT), (d_lt, ST * it + ST))
                for n in range(NT):
                    if n % 2 == 0:
                        dve.wait_ge(d_o, 1 + it * 2 + n // 2 + 1)
                    xt_ = xres[:, it * NT + n, :]
                    V.scalar_tensor_tensor(xt_, ps[:, 6 + n // 2, (n % 2) * D:(n % 2) * D + D], rrs[:, n:n + 1], xt_,
                                           ALU.mult, ALU.add).then_inc(d_res, 1)

            loop(dve, body_d)

        @block.scalar
        def _(act):
            A = nc.scalar
            start_counts(act, "act")

            def front_turned(f, tiles, affine):
                for k in range(3 if tiles > NT else 2):
                    front_turned_part(f, affine, k)

            def front_turned_part(f, affine, k):
                def norm(k):
                    if not affine:
                        return {}
                    return dict(scale=bcol[:, affine + k:affine + k + 1], bias=bcol[:, affine + 2 + k:affine + 3 + k])
                if k == 0:
                    act.wait_ge(ln_split, f)
                if k < 2:
                    act.wait_ge(ln_tr, 2 * f + k + 1)
                    A.activation(xt[:, k, 0:N], ps[:, 7, :], ACT.Identity, **norm(k)).then_inc(ln_xt, 1)
                else:
                    act.wait_ge(ln_tr_e, f + 1)
                    for k in range(2):
                        last = A.activation(xt[:, k, N:N + P], ps[:, 7, k * P:k * P + P], ACT.Identity, **norm(k))
                    last.then_inc(ln_xt_e, 1)

            act.wait_ge(ld_q, 32)
            for k in range(2):
                last = A.copy(ws[:, 2 * k, 0:QKV], first[:, k])
            last.then_inc(q_hi, 1)
            act.wait_ge(ld_c, 16 * 6)
            A.copy(ka.rearrange("p a i t -> p (a i) t"), kc.unsqueeze(1).broadcast_to([P, 2 * HP, T])).then_inc(setup_act, 1)
            front_turned(0, NT + 1, N1)
            A.copy(kae.rearrange("p a i t -> p (a i) t"), kec.unsqueeze(1).broadcast_to([P, 2 * HP, EKEYS])).then_inc(setup_act, 1)
            act.wait_ge(setup_act, 2)
            act.wait_ge(setup_dve, 1)
            for a in range(HP):
                for r in (0, 1):
                    src = slice(32 * (2 * (a // G) + r), 32 * (2 * (a // G) + r) + HD)
                    last = A.activation(kae[64 * r:64 * r + HD, a, :, EREAL:EKEYS],
                                        kec[src, EREAL:EKEYS].unsqueeze(1).broadcast_to([HD, 2, EPAD]), ACT.Identity,
                                        bias=bcol[src, 3 + a % G:4 + a % G])
            last.then_inc(setup_act, 1)

            def body_a(it, nxt):
                for g in range(G):
                    act.wait_ge(a_q, it * G + g + 1)
                    A.activation(qraw[:, g, :], ps[:, g, :], ACT.Identity, bias=bcol[:, g:g + 1]).then_inc(a_qraw, 1)
                for g in (1, 2):
                    act.wait_ge(a_k, it * G + g + 1)
                    for r in range(HG):
                        last = A.activation(ka[64 * (r % 2):64 * (r % 2) + HD, r // 2 * G + g].rearrange("p i t -> p (i t)"),
                                            ps[32 * r:32 * r + HD, 3 + g, :], ACT.Identity, scale=HD ** -0.5,
                                            bias=bcol[32 * r:32 * r + HD, 3 + g:4 + g])
                    last.then_inc(a_kb, 1)
                for q in range(4):
                    act.wait_ge(a_rel, it * 4 + q + 1)
                    position_terms(A.copy, 0, q).then_inc(a_qa, 1)
                base = it * UNITS
                for u in range(UNITS + 1):
                    if u >= 1:
                        rows, parts, keys, i, h = unit(u - 1)
                        half, wide = keys // 2, UH * parts * rows
                        act.wait_ge(a_t, base + u)
                        if u >= 3:
                            act.wait_ge(a_o, base + u - 2)
                        A.activation(pt[0:half, (u - 1) % 2, 1, 0:wide], ps[0:half, 5, 0:wide], ACT.Copy)\
                            .then_inc(a_pta, 1)
                    if u < UNITS:
                        rows, parts, keys, i, h = unit(u)
                        act.wait_ge(a_nm, base + u + 1)
                        for k in range(UH * parts):
                            c0 = k % parts * keys
                            last = A.activation(pp[0:rows, u % 2, k, 0:keys],
                                                ps[0:rows, UH * (u % 2) + k // parts, c0:c0 + keys],
                                                ACT.Exp, bias=nm[0:rows, u % 2, k:k + 1])
                        last.then_inc(a_p, 1)
                    if 9 <= u < (12 if nxt else 11):
                        front_turned_part(it + 1, N1 if nxt else N2, u - 9)
            loop(act, body_a)
            act.wait_ge(o_res, 1 + 2 * PAIRS)

            def body_b(it, nxt):
                act.wait_ge(b_y, 1 + it * 2)
                for m in range(MC):
                    act.wait_ge(b_h, it * MC + m + 1)
                    A.activation(hT[:, m, :], ps[:, m % 4, :], ACT.Gelu, bias=bcol[:, L1B + m:L1B + m + 1]).then_inc(b_gelu, 1)
                    if m >= MC - 2:
                        front_turned_part(it + (PAIRS + 1), N2 if nxt else 0, m - (MC - 2))

            loop(act, body_b)

            def body_c(it, nxt):
                act.wait_ge(c_qk, it * 3 + 1)
                A.activation(cqk[:, 0, :], ps[:, 0, :], ACT.Identity, scale=AD ** -0.5, bias=bcol[:, 10:11])
                act.wait_ge(c_qk, it * 3 + 2)
                A.activation(cqk[:, 1, :], ps[:, 1, :], ACT.Identity, bias=bcol[:, 12:13])
                act.wait_ge(c_qk, it * 3 + 3)
                A.activation(cq2[0:AD, 0, :], ps[0:AD, 2, :], ACT.Identity, scale=AD ** -0.5, bias=bcol[0:AD, 11:12])
                A.activation(cq2[0:AD, 1, :], ps[AD:P, 2, :], ACT.Identity, bias=bcol[AD:P, 13:14]).then_inc(c_qt, 1)
                n = 2 * AH
                base = it * n
                for u in range(n + 1):
                    if u >= 1:
                        act.wait_ge(c_t, base + u)
                        if u >= 3:
                            act.wait_ge(c_o, base + u - 2)
                        A.activation(cpt[:, (u - 1) % 2, :], ps[:, 3 + (u - 1) % 2, 0:3 * P], ACT.Copy).then_inc(c_pt, 1)
                    if u < n:
                        act.wait_ge(c_nm, base + u + 1)
                        A.activation(cp[:, u % 2, 0:P], ps[:, u % 3, 0:P], ACT.Exp, bias=cnm[:, u % 4, 0:1])
                        A.activation(cp[:, u % 2, P:3 * P], ps[:, u % 3, P:3 * P], ACT.Exp, bias=cnm[:, u % 4, 1:2]).then_inc(c_p, 1)
                    if u in (3, 4):
                        front_turned_part(it + (2 * PAIRS + 1), 0, u - 3)
                act.wait_ge(o_tr, it + 1)
                A.activation(ot0[:], ps[:, 3, :], ACT.Copy).then_inc(o_ta, 1)

            loop(act, body_c)
            ncm, csum, rcs, nrm, rsum, rrs = (dstat[:, k, :] for k in range(6))

            def body_d(it, nxt):
                act.wait_ge(d_o, 1 + it * 2)
                for n in range(NT + 1):
                    if n < NT:
                        act.wait_ge(d_nrm, it * NT + n + 1)
                        if n >= 2:
                            act.wait_ge(d_ct, it * NT + n - 1)
                        A.activation(cc[:, n % 2, :], ps[:, n % 2 * 2:n % 2 * 2 + 2, :].rearrange("p a c -> p (a c)"),
                                     ACT.Exp, bias=nrm[:, n:n + 1], accum_out=rsum[:, n:n + 1]).then_inc(d_c, 1)
                    if n:
                        act.wait_ge(d_ct, it * NT + n)
                        A.activation(ct[:, :, n * P - P:n * P], ps[:, 4:6, :].rearrange("p a (s c) -> p (a s) c", c=P), ACT.Copy)\
                            .then_inc(d_cte, 1)
                    if n < NT:
                        for k in (2 * n, 2 * n + 1):
                            act.wait_ge(d_ncm, it * ST + k + 1)
                            for b in range(2):
                                last = A.activation(dt_[:, b, k, :], ps[:, 6 + k % 2, b * T:b * T + T], ACT.Exp,
                                                    bias=ncm[:, 2 * k + b:2 * k + b + 1],
                                                    accum_out=csum[:, 2 * k + b:2 * k + b + 1])
                            last.then_inc(d_dt, 1)
                for b in range(2):
                    act.wait_ge(d_dtr, it * NT + 2 * b + 2)
                    A.activation(dd[b][:, 1, :], ps[:, (6, 2)[b]:(8, 4)[b], :].rearrange("p a c -> p (a c)"), ACT.Copy)\
                        .then_inc(d_da, 1)
                for b in range(2):
                    for h in range(2):
                        act.wait_ge(d_st, 1 + it * 4 + 2 * b + h + 1)
                        bank = (4, 0)[b] + h
                        A.activation(slot_cols(slots[0], b, h), ps[:, bank, :].rearrange("p (e s) -> p e s", e=2), ACT.Copy)
                        A.activation(slot_cols(slots[2], b, h), ps[:, bank + 2, :].rearrange("p (e s) -> p e s", e=2),
                                     ACT.Copy).then_inc(d_sh, 1)
                for e in range(NE):
                    if nxt and e in (1, 2):
                        front_turned_part(it + (3 * PAIRS + 1), 0, e - 1)
                    act.wait_ge(d_y, 1 + it * 2 * NE + 2 * e)
                    for m in range(MC):
                        act.wait_ge(d_h, it * NE * MC + e * MC + m + 1)
                        A.activation(hTd[:, m, :], ps[:, H_BANKS[(e * MC + m) % 4], :], ACT.Gelu_apprx_tanh,
                                     bias=bcol[:, E1B + e * MC + m:E1B + e * MC + m + 1]).then_inc(d_gelu, 1)

            loop(act, body_d)

        @block.tensor
        def _(pe):
            tr = nc.tensor.transpose
            start_counts(pe, "pe")

            def front_turn(f, tiles, *free):
                for k in range(3 if tiles > NT else 2):
                    front_turn_part(f, k, *free)

            def front_turn_part(f, k, *free):
                if k == 0:
                    pe.wait_ge(ln_xn, f + 1)
                    for s_, v_ in free:
                        pe.wait_ge(s_, v_)
                pe.wait_ge(ln_xt, 2 * f + k)
                if k < 2:
                    for j in range(NT):
                        last = tr(ps[:, 7, j * P:j * P + P], xn[:, j, k * P:k * P + P], ident[:])
                    last.then_inc(ln_tr, 1)
                else:
                    for k in range(2):
                        last = tr(ps[:, 7, k * P:k * P + P], xn[:, NT, k * P:k * P + P], ident[:])
                    last.then_inc(ln_tr_e, 1)

            pe.wait_ge(ld_c, 16 * 6)
            front_turn(0, NT + 1)
            pe.wait_ge(ld_p, 16 * HG)
            pe.wait_ge(q_hi, 1)
            pe.wait_ge(q_lo, 1)

            def scores_full(u, i, h):
                for t in range(2):
                    for k in range(UH):
                        q = slice(64 * k, 64 * k + 64)
                        keys = ka[q, operands(h), i, :].rearrange("p (y x) -> p y x", x=W)[:, 0:WS, 0:WS]
                        last = mm(ps[0:QR, UH * (u % 2) + k, 2 * QT * t:2 * QT * t + 2 * QT],
                                  qs[q, 2 * operands(h) + i, QR * t:QR * t + QR], keys, start=True, stop=True)
                return last

            def scores_border(u, h):
                for i in range(2):
                    for k in range(UH):
                        q = slice(64 * k, 64 * k + 64)
                        last = mm(ps[64 * i:64 * i + 64, UH * (u % 2) + k, 0:EKEYS],
                                  qb[q, 2 * operands(h) + i, :], kae[q, operands(h), i, :], start=True, stop=True)
                return last

            def queries(g):
                product(ps[:, g, :], (CQ + g * P, CQ + g * P + P), xcols(0, N)).then_inc(a_q, 1)

            def body_a(it, nxt):
                for g in range(G):
                    product(ps[:, 3 + g, :], (CK + g * P, CK + g * P + P), xcols(0, N)).then_inc(a_k, 1)
                pe.wait_ge(o_res, 1 + it * 2)
                for i in range(2):
                    if i:
                        pe.wait_ge(a_qraw, it * G + 1)
                    pe.wait_ge(a_xw, it * 3 + 3)
                    for t in range(2):
                        at = N + P + (2 * i + t) * QT
                        last = product(ps[0:QT, 6 if i == 0 else 0, t * D:t * D + D], (CV, CV + D),
                                       xcols(at, at + QT), True)
                    last.then_inc(a_v, 1)
                pe.wait_ge(a_qraw, it * G + 2)
                product(ps[:, 1, 0:D], (CV, CV + D), xcols(N, N + P), True).then_inc(a_v, 1)
                pe.wait_ge(a_qraw, it * G + 3)
                gated(pe, 0)
                q4 = qraw.rearrange("p g (i t) -> p (g i) t", i=2)
                for step in range(4):
                    if step == 1:
                        pe.wait_ge(a_ka, it + 1)
                        pe.wait_ge(a_kb, it * 2 + 1)
                    if step == 2:
                        pe.wait_ge(a_kb, it * 2 + 2)
                        pe.wait_ge(a_ve, it * 6 + 2)
                    if step == 3:
                        pe.wait_ge(a_ve, it * 6 + 6)
                    if step:
                        gated(pe, 0)
                    for k in range(4):
                        at = 4 * step + k
                        for cols in range(2):
                            rows = q4.rearrange("p a (y x) -> p a y x", x=W)
                            last = mm(ps[:, REL_BANKS[cols][step], 96 * k:96 * k + 96], relt[:, W * cols + at, :],
                                      rows[:, :, :, at] if cols else rows[:, :, at, :], start=True, stop=True)
                    last.then_inc(a_rel, 1)
                base = it * UNITS
                for u in range(UNITS + 2):
                    if u < UNITS:
                        rows, parts, keys, i, h = unit(u)
                        if u == 0:
                            pe.wait_ge(a_qa, it * 4 + 4)
                            pe.wait_ge(a_qw, it * 4 + 4)
                        if u >= 2:
                            pe.wait_ge(a_p, base + u - 1)
                        if u == MAIN:
                            pe.wait_ge(a_kae, it * 2 + 2)
                            pe.wait_ge(a_qb, it * 2 + 2)
                        gated(pe, 0)
                        (scores_full(u, i, h) if u < MAIN else scores_border(u, h)).then_inc(a_s, 1)
                    if 1 <= u <= UNITS:
                        v = u - 1
                        rows, parts, keys, i, h = unit(v)
                        half = keys // 2
                        pe.wait_ge(a_p, base + u)
                        pe.wait_ge(a_ptd, 1 + base + v)
                        pe.wait_ge(a_pta, 1 + base + v)
                        for k in range(2):
                            for n in range(UH * parts):
                                last = tr(ps[0:half, 4 + k, n * rows:n * rows + rows],
                                          pp[0:rows, v % 2, n, k * half:k * half + half], ident[0:rows, 0:rows])
                        last.then_inc(a_t, 1)
                    if nxt and u >= UNITS:
                        if u == UNITS:
                            pe.wait_ge(ln_split, it + 2)
                        queries(u - UNITS)
                    if u >= 2:
                        v = u - 2
                        rows, parts, keys, i, h = unit(v)
                        pe.wait_ge(a_ptd, 1 + base + v + 1)
                        pe.wait_ge(a_pta, 1 + base + v + 1)
                        pe.wait_ge(a_on, 1 + base + v)
                        for n in range(UH):
                            at, vc = n * parts * rows, slice(n * 3 * HD, n * 3 * HD + 4 * HD)
                            if parts == 2:
                                for k in range(2):
                                    last = mm(ps[0:64, 6, 0:2 * QR], ve[0:QT, 2 * i + k, h, vc],
                                              pt[0:QT, v % 2, k, at:at + 2 * QR], start=n + k == 0, stop=n + k == 2)
                            else:
                                for part in ((None, 0, 1), (0, 1, None))[n]:
                                    if part is None:
                                        last = mm(ps[0:64, 6, 0:P], vee[:, 2, h, vc], pt[:, v % 2, 1, at:at + P],
                                                  start=n == 0, stop=n == 1)
                                    else:
                                        last = mm(ps[0:64, 6, 64 * part:64 * part + 64], vee[:, part, h, vc],
                                                  pt[:, v % 2, 0, at + 64 * part:at + 64 * part + 64], start=False, stop=False)
                        last.then_inc(a_o, 1)
                    if 9 <= u < (12 if nxt else 11):
                        front_turn_part(it + 1, u - 9, (ln_xt_e, it + 1))
                if nxt:
                    queries(2)
                pe.wait_ge(a_on, 1 + base + UNITS)
                project(0, (6, 7))

            def project(which, banks):
                for j in range(NT):
                    dst = ps[:, banks[j // 2], (j % 2) * D:(j % 2) * D + D]
                    mm(dst, ot0[:, j * P:j * P + P], wproj[:, which, 0, :], start=True, stop=False)
                    last = mm(dst, ot1[0:R1 + 1, j * P:j * P + P], wproj[0:R1 + 1, which, 1, :], start=False, stop=True)
                    if j % 2:
                        last.then_inc(o_proj, 1)

            pe.wait_ge(ln_split, 1)
            for g in range(G):
                queries(g)
            pe.wait_ge(setup_pool, 3)
            pe.wait_ge(setup_dve, 3)
            pe.wait_ge(setup_act, 3)
            pe.wait_ge(ld_r, 32)
            loop(pe, body_a)

            pe.wait_ge(w_split, A_CHUNKS - QKV_CHUNKS)
            pe.wait_ge(o_res, 1 + 2 * PAIRS)

            def body_b(it, nxt):
                pe.wait_ge(ln_split, it + (PAIRS + 1))
                for m in range(MC):
                    pe.wait_ge(b_gelu, 1 + it * MC + max(0, m - 3))
                    product(ps[:, m % 4, :], (CL1 + m * P, CL1 + m * P + P), xcols(0, N)).then_inc(b_h, 1)
                    if m >= MC - 2:
                        front_turn_part(it + (PAIRS + 1), m - (MC - 2))
                pe.wait_ge(ld_l2, 16)
                pe.wait_ge(b_gelu, 1 + it * MC + MC - 1)
                pe.wait_ge(b_res, 1 + it * 2)
                for j in range(NT):
                    dst = ps[:, 4 + j // 2, (j % 2) * D:(j % 2) * D + D]
                    mm(dst, ot1[96:97, 0:P], wproj[96:97, 0, 1, :], start=True, stop=False)
                    for m in range(MC):
                        if j == 0 and m == MC - 1:
                            pe.wait_ge(b_gelu, 1 + it * MC + MC)
                        last = mm(dst, hT[:, m, j * P:j * P + P], w2l[:, m, :], start=False, stop=m == MC - 1)
                    if j % 2:
                        last.then_inc(b_y, 1)

            loop(pe, body_b)

            pe.wait_ge(b_res, 1 + 2 * PAIRS)

            def queries_keys(split):
                pe.wait_ge(ln_split, split)
                for k in range(3):
                    product(ps[:, k, :], (CA + k * P, CA + k * P + P), xcols(0, N)).then_inc(c_qk, 1)

            queries_keys(2 * PAIRS + 1)

            def body_c(it, nxt):
                pe.wait_ge(o_res, 1 + it * 2 + 2 * PAIRS)
                for j in range(NT):
                    last = product(ps[:, 3 + j // 2, (j % 2) * D:(j % 2) * D + D], (CAV, CAV + D),
                                   xcols(j * P, j * P + P), True)
                    if j % 2:
                        last.then_inc(c_v, 1)
                n = 2 * AH
                base = it * n
                pe.wait_ge(c_qt, it + 1)
                pe.wait_ge(c_ve, it * 2 + 2)
                for u in range(-2, n + 1):
                    if u + 2 < n:
                        v = u + 2
                        b, h = v // AH, v % AH
                        if v >= 3:
                            pe.wait_ge(c_p, base + v - 2)
                        if h < 2:
                            rows = slice(AD * h, AD * h + AD)
                            q, k = cqk[rows, 0, :], cqk[rows, 1, :]
                        else:
                            q, k = cq2[0:AD, 0, :], cq2[0:AD, 1, :]
                        t0 = b * T
                        bank = ps[:, v % 3, :]
                        mm(bank[:, 0:P], q[:, t0:t0 + P], k[:, t0:t0 + P], start=True, stop=False)
                        mm(bank[:, 0:P], identb[:], maskb[:], start=False, stop=True)
                        mm(bank[:, P:3 * P], q[:, t0 + P:t0 + T], k[:, t0:t0 + T], start=True, stop=False)
                        mm(bank[:, 2 * P:3 * P], identb[:], maskb[:], start=False, stop=True).then_inc(c_s, 1)
                    if 0 <= u < n:
                        pe.wait_ge(c_p, base + u + 1)
                        if u >= 2:
                            pe.wait_ge(c_pt, base + u - 1)
                        for k in range(3):
                            last = tr(ps[:, 3 + u % 2, k * P:k * P + P], cp[:, u % 2, k * P:k * P + P], ident[:])
                        last.then_inc(c_t, 1)
                    if u >= 1:
                        v = u - 1
                        b, h = v // AH, v % AH
                        pe.wait_ge(c_pt, base + v + 1)
                        if v >= 2:
                            pe.wait_ge(c_on, base + v - 1)
                        bank = ps[:, 5 + v % 2, :]
                        mm(bank[:, 0:AD + 1], cpt[:, v % 2, 0:P], cv[:, 2 * b, h, :], start=True, stop=True)
                        mm(bank[:, AD + 1:2 * AD + 2], cpt[:, v % 2, P:2 * P], cv[:, 2 * b, h, :], start=True, stop=False)
                        mm(bank[:, AD + 1:2 * AD + 2], cpt[:, v % 2, 2 * P:3 * P], cv[:, 2 * b + 1, h, :], start=False,
                           stop=True).then_inc(c_o, 1)
                    if u in (2, 3):
                        front_turn_part(it + (2 * PAIRS + 1), u - 2)
                if nxt:
                    queries_keys(it + (2 * PAIRS + 2))
                pe.wait_ge(c_on, base + n)
                for j in range(NT):
                    tr(ps[:, 3, j * P:j * P + P], co[:, j, 0:P], ident[:])
                for j in range(NT):
                    last = tr(ps[0:R1, 4, j * P:j * P + P], co[:, j, P:D], ident[:])
                last.then_inc(o_tr, 1)
                pe.wait_ge(o_td, it + 1)
                pe.wait_ge(o_ta, it + 1)
                project(1, (5, 6))

            loop(pe, body_c)

            pe.wait_ge(o_res, 1 + 4 * PAIRS)

            def body_d(it, nxt):
                pe.wait_ge(ln_split, it + (3 * PAIRS + 1))
                for n in range(NT + 1):
                    if n < NT:
                        if n >= 2:
                            pe.wait_ge(d_c, it * NT + n - 1)
                        for c in range(2):
                            last = product(ps[:, n % 2 * 2 + c, :], (CPHI + 512 * c, CPHI + 512 * c + 512),
                                           xcols(n * P, n * P + P), True)
                        last.then_inc(d_l, 1)
                    if n:
                        pe.wait_ge(d_c, it * NT + n)
                        if n > 1:
                            pe.wait_ge(d_cte, 1 + it * NT + n - 1)
                        for s in range(ST):
                            last = tr(ps[:, 4 + s // 4, (s % 4) * P:(s % 4) * P + P], cc[:, (n - 1) % 2, s * P:s * P + P], ident[:])
                        last.then_inc(d_ct, 1)
                    if n < NT:
                        for k in (2 * n, 2 * n + 1):
                            if k < 2:
                                pe.wait_ge(d_res, 1 + it * NT)
                            else:
                                pe.wait_ge(d_dt, it * ST + k - 1)
                            product(ps[:, 6 + k % 2, :], (CPHI + k * P, CPHI + k * P + P), xcols(0, N)).then_inc(d_lt, 1)
                pe.wait_ge(d_dn, it * ST + ST)
                pe.wait_ge(d_cte, 1 + it * NT + NT)
                for n in range(NT):
                    for s in range(ST):
                        last = tr(ps[:, (4, 6, 0, 2)[n] + s // 4, (s % 4) * P:(s % 4) * P + P],
                                  dt_[:, n // 2, s, n % 2 * P:n % 2 * P + P], ident[:])
                    last.then_inc(d_dtr, 1)
                for b in range(2):
                    pe.wait_ge(d_de, it * 2 + b + 1)
                    pe.wait_ge(d_da, it * 2 + b + 1)
                    if b:
                        gated(pe, 0)
                    for h in range(2):
                        for part in range(2):
                            for j in range(2):
                                last = mm(ps[:, (4, 0)[b] + 2 * part + h, :], xn[:, 2 * b + j, part * P:part * P + P],
                                          dd[b][:, j, 512 * h:512 * h + 512], start=j == 0, stop=j == 1)
                        last.then_inc(d_st, 1)
                pe.wait_ge(ld_w2, 32)
                pe.wait_ge(w_split, NCHUNK - QKV_CHUNKS)
                pe.wait_ge(d_ss, 1 + it * 4 + 3)
                for e in range(NE):
                    for m in range(MC):
                        if e == 0 and m == 2:
                            pe.wait_ge(d_ss, 1 + it * 4 + 4)
                        pe.wait_ge(d_gelu, 1 + it * NE * MC + max(0, e * MC + m - 3))
                        product(ps[:, H_BANKS[(e * MC + m) % 4], :], (CW1 + (e * MC + m) * P, CW1 + (e * MC + m) * P + P),
                                scols(512 * e, 512 * e + 512)).then_inc(d_h, 1)
                    pe.wait_ge(d_gelu, 1 + it * NE * MC + e * MC + MC - 1)
                    pe.wait_ge(d_ye, 1 + it * 2 * NE + 2 * e)
                    for b in range(2):
                        for s in range(2):
                            for m in range(MC):
                                if b + s == 0 and m == MC - 1:
                                    pe.wait_ge(d_gelu, 1 + it * NE * MC + e * MC + MC)
                                last = mm(ps[:, 4 + b, s * D:s * D + D], hTd[:, m, b * T + s * P:b * T + s * P + P],
                                          w2x[:, e * MC + m, :], start=m == 0, stop=m == MC - 1)
                        last.then_inc(d_y, 1)
                    if nxt and e < 2:
                        front_turn_part(it + (3 * PAIRS + 1), e)
                pe.wait_ge(d_ye, 1 + it * 2 * NE + 2 * NE - 2)
                for n in range(NT):
                    for s in range(ST):
                        if n == 0 and s == ST - 2:
                            pe.wait_ge(d_ye, 1 + it * 2 * NE + 2 * NE)
                        last = mm(ps[:, 6 + n // 2, (n % 2) * D:(n % 2) * D + D], ct[:, s, n * P:n * P + P],
                                  yy[:, n // 2, s, :], start=s == 0, stop=s == ST - 1)
                    if n % 2:
                        last.then_inc(d_o, 1)

            loop(pe, body_d)


INPUTS = ("x", "xe", "wall0", "wall1", "rel", "wp", "w2a", "w2e", "bias_cols", "bias_rows", "b2r", "c_ident", "c_keys",
          "c_border", "c_mask")


def lay_out(v):
    import numpy as np

    f = np.float32
    v = {k.replace("L0_conv_", "c_").replace("L1_attn_", "a_").replace("L1_ffn_", "f_"): np.asarray(a) for k, a in v.items()}
    x = v["x"].astype(f, copy=False)
    border = np.concatenate([x[:, :, WS:W].reshape(B, -1, D), x[:, WS:H].reshape(B, -1, D)], 1)

    def spread(w):
        out = np.zeros((w.shape[0], G, HG, 32), f)
        out[..., 0:HD] = w.reshape(-1, G, HG, HD)
        return out.reshape(w.shape[0], G * P)

    qkv, aq = v["c_qkv_w"], v["a_W_qkv"]
    wall = np.concatenate([
        spread(qkv[:, 0:D]), spread(qkv[:, D:2 * D]), qkv[:, 2 * D:], v["c_lin1_w"],
        aq[:, 0:P], aq[:, D:D + P], aq[:, P:D], aq[:, D + P:2 * D], aq[:, 2 * D:],
        v["f_phi"].reshape(NE * NS, D).T, v["f_w1"].transpose(1, 0, 2).reshape(D, NE * MLP)], 1)
    rel = np.zeros((HG, 32, 2, W, 32), f)
    for c in range(HD):
        rel[:, c, 0, :, c] = 1
    for y in range(W):
        for k in range(WS):
            rel[:, 0:HD, 0, y, HD + k] = v["c_rel_pos_h"][y % WS - k + WS - 1]
            rel[:, 0:HD, 1, y, HD + k] = v["c_rel_pos_w"][y % WS - k + WS - 1]
        rel[:, HD, :, y, 30 + (y >= WS)] = 1
    wp = np.zeros((P, 2, 2, D), f)
    for n, (w, b) in enumerate(((v["c_proj_w"], v["c_proj_b"]), (v["a_W_out"], v["a_b_out"]))):
        wp[:, n, 0], wp[0:R1, n, 1], wp[R1, n, 1] = w[0:P], w[P:], b
    wp[96, 0, 1] = v["c_lin2_b"]
    cols = np.zeros((P, 48), f)
    cb, ab = v["c_qkv_b"], v["a_b_qkv"]
    cols[:, 0:G] = spread(cb[None, 0:D]).reshape(G, P).T
    cols[:, 0:G].reshape(HG, 32, G)[:, HD] = 1
    cols[:, G:2 * G] = spread(cb[None, D:2 * D]).reshape(G, P).T
    for at, w, b in ((N1, v["c_n1_w"], v["c_n1_b"]), (N2, v["c_n2_w"], v["c_n2_b"])):
        cols[:, at], cols[:, at + 1] = w[0:P], np.concatenate([w[P:], w[P:]])
        cols[:, at + 2], cols[:, at + 3] = b[0:P], np.concatenate([b[P:], b[P:]])
    cols[:, 10], cols[0:AD, 11], cols[:, 12], cols[AD:P, 13] = ab[0:P], ab[P:D], ab[D:D + P], ab[D + P:2 * D]
    cols[:, L1B:L1B + MC] = v["c_lin1_b"].reshape(MC, P).T
    cols[:, E1B:E1B + NE * MC] = v["f_b1"].reshape(NE * MC, P).T
    rows = np.concatenate([cb[None, 2 * D:], ab[None, 2 * D:], v["f_b2"]])
    def key(y, xx, y0=0, y1=0, x0=0, x1=0):
        got = np.zeros((2, 64), f)
        got[:, HD + y % WS] = got[:, 32 + HD + xx % WS] = 1
        got[:, 30], got[:, 31], got[:, 62], got[:, 63] = y0 * NEG, y1 * NEG, x0 * NEG, x1 * NEG
        return got.reshape(P)

    def real(y, xx):
        if y < WS and xx < WS:
            return key(y, xx)
        return key(y, xx, y0=y >= WS, y1=y < WS, x0=xx >= WS, x1=xx < WS)

    ckeys = np.stack([real(y, xx) for y in range(H) for xx in range(W)], 1)
    cborder = np.stack(
        [real(y, xx) if y < WS else key(y, xx, x0=1, x1=1) for y in range(H) for xx in range(WS, W)]
        + [real(y, xx) for y in range(WS, H) for xx in range(W)]
        + [key(y, xx, x0=y < EW, y0=xx < EW) for y in range(WS) for xx in range(WS) if y >= EW or xx >= EW], 1)
    mask = np.where(np.arange(P)[None] > np.arange(P)[:, None], NEG, 0).astype(f)
    got = dict(
        x=x.reshape(B * T, D), xe=border.reshape(PAIRS, P, D), wall0=wall[0:P], wall1=np.concatenate([wall[P:], wall[P:]]),
        rel=rel.reshape(P, 2 * W, 32), wp=wp, w2a=v["c_lin2_w"].reshape(MC, P, D).transpose(1, 0, 2),
        w2e=v["f_w2"].reshape(NE * MC, P, D).transpose(1, 0, 2), bias_cols=cols,
        bias_rows=np.broadcast_to(rows[None, 0:2], (P, 2, D)), b2r=np.broadcast_to(rows[None, 2:], (P, NE, D)), c_ident=np.eye(P, dtype=f),
        c_keys=ckeys, c_border=cborder, c_mask=mask)
    return {k: np.ascontiguousarray(a) for k, a in got.items()}


def kernel(**inputs):
    import concourse.bacc as bacc
    from concourse.bass_utils import run_bass_kernel_spmd

    laid = lay_out(inputs)
    nc = bacc.Bacc("TRN2", target_bir_lowering=False, num_devices=1)
    args = {k: nc.dram_tensor("in_" + k, laid[k].shape, F32, kind="ExternalInput").ap() for k in INPUTS}
    out = nc.dram_tensor("out", (B * T, D), F32, kind="ExternalOutput").ap()
    build(nc, **args, out=out)
    r = run_bass_kernel_spmd(nc, [{"in_" + k: laid[k] for k in INPUTS}], core_ids=[0])
    return r.results[0]["out"].reshape(B, H, W, D)
```

```python
from contextlib import ExitStack

import concourse.bass as bass
from concourse import mybir

P = 128
F32 = mybir.dt.float32
F32R = mybir.dt.float32r
BF16 = mybir.dt.bfloat16
ALU = mybir.AluOpType
ACT = mybir.ActivationFunctionType
AX = mybir.AxisListType

B, H, W, D = 8, 16, 16, 192
T = H * W
TT = T // P
PAIRS = B // 2
NT = 2 * TT
N = NT * P
R1 = D - P
MLP = 4 * D
MC = MLP // P
WS, NH, HD = 14, 12, 16
G, HG = 3, 4
HP = NH // 2
HALF = WS // 2
QT = HALF * WS
QR = HALF * W
EW = W - WS
EREAL = 2 * H * EW
EPAD = WS * WS - EW * EW
EKEYS = EREAL + EPAD
UH = 2
MAIN = 2 * NH // UH
UNITS = MAIN + NH // UH
V_BANKS = 7, 6, 5
REL_BANKS = (2, 4, 5, 1), (7, 3, 6, 0)
AH, AD = 3, 64
NE, NS = 4, 256
ST = NE * NS // P
CQ, CK, CV = 0, G * P, 2 * G * P
CL1 = CV + D
CA = CL1 + MLP
CAV = CA + 3 * P
CPHI = CA + 3 * D
CW1 = CPHI + NE * NS
WALL = CW1 + NE * MLP
CHUNK = 256
N1, CQB, CKB, N2, L1B = (2 * G + n for n in (0, 4, 6, 8, 12))
E1B = L1B + MC
NCHUNK = WALL // CHUNK
QKV_CHUNKS = -(-CL1 // CHUNK)
QKV = QKV_CHUNKS * CHUNK
A_CHUNKS = CW1 // CHUNK
L2ROW = 96
VB = 7 * HD
EPS = 1e-5
NEG = -1.0e30


def build(nc, x, xe, wall0, wall1, rel, wp, w2a, w2e, bias_cols, bias_rows, b2r, c_ident, c_keys,
          c_border, c_mask, out):
    with ExitStack() as ctx:
        def sb(name, shape, dt=F32):
            return ctx.enter_context(nc.sbuf_tensor(name, shape, dt))

        def sem(name):
            return ctx.enter_context(nc.semaphore(name))

        xres = sb("xres", [P, B * TT, D])
        ws = sb("ws", [P, 4, CW1], F32R)
        with nc.sbuf_tensor("room", [P, 4 * (WALL - CW1)], F32) as room:
            pass
        wx = sb("wx", [P, 4, WALL - CW1], F32R)
        xs = sb("xs", [P, 3, N + P + 4 * QT], F32R)
        ident = sb("ident", [P, P])
        wproj = sb("wproj", [P, 2, 2, D])
        bcol = sb("bcol", [P, 48])
        brow = sb("brow", [P, 2, D])
        stage = sb("stage", [P, 2, CHUNK])
        st6 = sb("st6", [P, NT + 1, 6])
        mv = sb("mv", [P, NT + 1, 2])
        rstd = sb("rstd", [P, NT + 1])
        mhalf = sb("mhalf", [P, NT + 1])
        xn = sb("xn", [P, NT + 1, 256])
        xt = sb("xt", [P, 2, N + P])
        nm = sb("nm", [P, 2, HG])
        rs = sb("rs", [P, 2, HG])
        cnm = nm.rearrange("p a b -> p (a b)").rearrange("p (a b) -> p a b", b=2)
        AREA = 16640
        area = sb("area", [P, AREA])
        ps = ctx.enter_context(nc.psum_tensor("ps", [P, 8, 512], F32))

        def views(spec):
            got, at = [], 0
            for shape in spec:
                size = 1
                for n in shape:
                    size *= n
                v = area[:, at:at + size]
                if len(shape) == 2:
                    v = v.rearrange("p (a b) -> p a b", b=shape[1])
                elif len(shape) == 3:
                    v = v.rearrange("p (a b c) -> p a b c", b=shape[1], c=shape[2])
                elif len(shape) == 4:
                    v = v.rearrange("p (a b c d) -> p a b c d", b=shape[1], c=shape[2], d=shape[3])
                got.append(v)
                at += size
            assert at <= AREA, at
            return got

        (qs, qb, ka, kae, pp, pt, xedge) = views([
            (2 * HP, T), (2 * HP, EREAL), (HP, 2, T), (HP, 2, EKEYS), (2, 2 * UH, EKEYS), (2, 2, 512), (D,)])
        ve = room[:, 0:NT * HP * VB].rearrange("p (t a c) -> p t a c", a=HP, c=VB)
        vee = room[:, NT * HP * VB:(NT + 3) * HP * VB].rearrange("p (t a c) -> p t a c", a=HP, c=VB)
        den = room[:, (NT + 3) * HP * VB:(NT + 3) * HP * VB + 2 * N].rearrange("p (u n) -> p u n", u=2)
        at = (NT + 3) * HP * VB + 2 * N
        relt = room[:, at:at + 2 * W * P].rearrange("p (a b) -> p a b", b=P)
        first = pp.rearrange("p a b c -> p (a b c)")[:, 0:2 * QKV].rearrange("p (k c) -> p k c", k=2)
        kc, kec = pt[:, 0, 1, 0:T], pt[:, 1, 0, 0:EKEYS]
        qraw = pp.rearrange("p a b c -> p (a b c)")[:, 0:G * N].rearrange("p (g n) -> p g n", g=G)
        (hT, w2l) = views([(MC, N), (MC, D)])
        (cqk, cq2, cv, cp, cpt, co) = views([(2, N), (2, N), (NT, AH, AD + 1), (2, 3 * P), (2, 3 * P), (NT, D)])
        (cc, _, ct, dt_, w2x, b2row) = views([(2, NE * NS), (1024,), (ST, N), (2, ST, T), (NE * MC, D), (NE, D)])
        dd = cc, dt_[:, 0].rearrange("p s t -> p (s t)").rearrange("p (j c) -> p j c", j=2)
        yy = area[:, 0:2 * ST * D].rearrange("p (b s d) -> p b s d", b=2, d=D)
        dstart = 2 * NE * NS + 1024 + ST * N
        hTd = area[:, dstart:dstart + MC * N].rearrange("p (a b) -> p a b", b=N)
        slots = [ws[:, k, 0:NE * 2 * NS] for k in range(3)]
        dstat = sb("dstat", [P, 6, 2 * ST])
        identb = sb("identb", [P, P], BF16)
        maskb = sb("maskb", [P, P], BF16)
        ot0, ot1 = area[:, AREA - 2 * N:AREA - N], area[:, AREA - N:AREA]

        ld_x, ld_w, ld_c, ld_l2, ld_w2, ld_p, ld_e, ld_q, ld_r = (
            sem(n) for n in ("ld_x", "ld_w", "ld_c", "ld_l2", "ld_w2", "ld_p", "ld_e", "ld_q", "ld_r"))
        setup_dve, setup_pool, setup_act, dve_own, pool_own = (
            sem(n) for n in ("setup_dve", "setup_pool", "setup_act", "dve_own", "pool_own"))
        w_split, q_hi, q_lo = (
            sem(n) for n in ("w_split", "q_hi", "q_lo"))
        ln_mv, ln_rstd, ln_xn, ln_tr, ln_tr_e, ln_xt, ln_xt_e, ln_hi, ln_split = (
            sem(n) for n in ("ln_mv", "ln_rstd", "ln_xn", "ln_tr", "ln_tr_e", "ln_xt", "ln_xt_e", "ln_hi", "ln_split"))
        a_q, a_k, a_v, a_qraw, a_ka, a_kb, a_ve, a_kae, a_rel, a_qa = (
            sem(n) for n in ("a_q", "a_k", "a_v", "a_qraw", "a_ka", "a_kb", "a_ve", "a_kae", "a_rel", "a_qa"))
        a_qw, a_qb, a_xw = (
            sem(n) for n in ("a_qw", "a_qb", "a_xw"))
        a_s, a_nm, a_p, a_t, a_pta, a_o, a_own, a_on = (
            sem(n) for n in ("a_s", "a_nm", "a_p", "a_t", "a_pta", "a_o", "a_own", "a_on"))
        o_tr, o_td, o_ta, o_proj, o_res = (
            sem(n) for n in ("o_tr", "o_td", "o_ta", "o_proj", "o_res"))
        b_h, b_gelu, b_y, b_res = (
            sem(n) for n in ("b_h", "b_gelu", "b_y", "b_res"))
        c_qk, c_v, c_qt, c_ve, c_s, c_nm, c_p, c_t, c_pt, c_o = (
            sem(n) for n in ("c_qk", "c_v", "c_qt", "c_ve", "c_s", "c_nm", "c_p", "c_t", "c_pt", "c_o"))
        c_own, c_on = (
            sem(n) for n in ("c_own", "c_on"))
        d_l, d_nrm, d_c, d_ct, d_cte = (
            sem(n) for n in ("d_l", "d_nrm", "d_c", "d_ct", "d_cte"))
        d_lt, d_ncm, d_dt, d_own, d_dn, d_dtr, d_de, d_da = (
            sem(n) for n in ("d_lt", "d_ncm", "d_dt", "d_own", "d_dn", "d_dtr", "d_de", "d_da"))
        d_st, d_sh, d_ss, d_h, d_gelu, d_y, d_ye, d_o, d_res, stored = (
            sem(n) for n in ("d_st", "d_sh", "d_ss", "d_h", "d_gelu", "d_y", "d_ye", "d_o", "d_res", "stored"))

        mm = nc.tensor.matmul

        def product(out_, wcols, xcols, weights_moving=False):
            x0, x1, x2 = xcols
            c0, c1 = wcols
            w_ = ws[:, :, c0:c1] if c0 < CW1 else wx[:, :, c0 - CW1:c1 - CW1]
            pairs = [(w_[:, 0], x0), (w_[:, 1], x0), (w_[:, 0], x1), (w_[:, 2], x2), (w_[0:R1, 3], x2[0:R1])]
            for n, (wp_, xp_) in enumerate(pairs):
                l, r = (xp_, wp_) if weights_moving else (wp_, xp_)
                last = mm(out_, l, r, start=n == 0, stop=n == len(pairs) - 1)
            return last

        def xcols(a, b):
            return [xs[:, k, a:b] for k in range(3)]

        def scols(a, b):
            return [s[:, a:b] for s in slots]

        def loop(eng, body):
            with eng.Fori(0, PAIRS - 1) as it:
                body(it, True)
            body(PAIRS - 1, False)

        def unit(u):
            if u < MAIN:
                return QR, 2, 2 * QT, u // HP, u % HP
            return P, 1, EKEYS, None, u - MAIN

        def operands(a):
            return a % 2 * G + a // 2

        from_one = dict(pe=(a_v, a_s, b_y, d_st, d_o, d_y, o_proj), dve=(o_res, b_res, a_on, d_res, d_ye, d_ss),
                        act=(b_gelu, d_cte, d_gelu, a_pta))

        def start_counts(eng, name):
            for s_ in from_one[name]:
                eng.sem_inc(s_, 1)

        def slot_cols(t, b, h):
            return t.rearrange("p (e b s) -> p e b s", e=NE, b=2)[:, 2 * h:2 * h + 2, b, :]

        gate = [sem(f"gate_{n}") for n in ("pe", "dve", "pool")]

        def gated(eng, n):
            eng.sem_inc(gate[n], 1)

        def position_terms(copy, cols, q):
            got = ps[:, REL_BANKS[cols][q], 0:384].rearrange("p (k a x) -> p a k x", k=4, a=2 * G)
            for r in range(HG):
                rows = slice(64 * (r % 2) + 32 * cols, 64 * (r % 2) + 32 * cols + 32)
                to = qs[rows, r // 2 * 2 * G:(r // 2 + 1) * 2 * G].rearrange("p a (y x) -> p a y x", x=W)
                to = to.rearrange("p a y x -> p a x y") if cols else to
                last = copy(to[:, :, 4 * q:4 * q + 4, :], got[32 * r:32 * r + 32])
            return last

        block = ctx.enter_context(nc.Block())

        @block.sync
        def _(sp):
            sp.dma_start(xres[:, 0:NT, :], x[0:N].rearrange("(t p) d -> p t d", p=P)).then_inc(ld_x, 16)
            sp.dma_start(xedge, xe[0]).then_inc(ld_x, 16)
            for k, wall in enumerate((wall0, wall1)):
                sp.dma_start(first[:, k], wall[:, 0:QKV]).then_inc(ld_q, 16)
            for dst, src in ((ident[:], c_ident), (bcol[:], bias_cols), (brow[:], bias_rows), (kc, c_keys),
                             (kec, c_border), (pt[:, 0, 0, 0:P], c_mask)):
                sp.dma_start(dst, src).then_inc(ld_c, 16)
            sp.wait_ge(setup_pool, 3)
            for r in range(HG):
                q = slice(32 * r, 32 * r + 32)
                sp.dma_start(relt[q, :, q], rel[q]).then_inc(ld_p, 16)
            sp.dma_start(xres[:, NT:, :], x[N:].rearrange("(t p) d -> p t d", p=P)).then_inc(ld_r, 16)
            sp.dma_start(wproj[:], wp).then_inc(ld_r, 16)
            for n in range(1, PAIRS):
                sp.wait_ge(ln_xn, n)
                sp.dma_start(xedge, xe[n]).then_inc(ld_e, 16)
            sp.wait_ge(o_res, 1 + 2 * PAIRS)
            sp.dma_start(w2l, w2a).then_inc(ld_l2, 16)
            sp.wait_ge(o_res, 1 + 4 * PAIRS)
            sp.dma_start(w2x, w2e).then_inc(ld_w2, 16)
            sp.dma_start(b2row, b2r).then_inc(ld_w2, 16)
            for it in range(PAIRS):
                sp.wait_ge(d_res, 1 + NT * (it + 1))
                sp.dma_start(out[it * N:(it + 1) * N].rearrange("(t p) d -> p t d", p=P),
                             xres[:, it * NT:(it + 1) * NT, :]).then_inc(stored, 16)
            sp.wait_ge(stored, 16 * PAIRS)

        @block.gpsimd
        def _(pool):
            nc.gpsimd.memset(mhalf[:], -0.5).then_inc(setup_pool, 1)
            pool.wait_ge(setup_pool, 1)
            nc.gpsimd.memset(ot1[R1:P, :], 1.0).then_inc(setup_pool, 1)
            pool.wait_ge(setup_pool, 2)
            nc.gpsimd.memset(relt.rearrange("p a b -> p (a b)"), 0.0).then_inc(setup_pool, 1)
            pool.wait_ge(setup_pool, 3)

            def norm_scale(f, tiles, k):
                pool.wait_ge(ln_mv, f + 1)
                gated(pool, 2)
                nc.gpsimd.tensor_scalar(rstd[:, 0:tiles], mv[:, 0:tiles, 1], EPS, 1.0, ALU.add, ALU.mult)\
                    .then_inc(pool_own, 1)
                pool.wait_ge(pool_own, k)
                nc.gpsimd.tensor_tensor(rstd[:, 0:tiles], rstd[:, 0:tiles], mhalf[:, 0:tiles], ALU.pow)\
                    .then_inc(ln_rstd, 1)

            def split_chunk(c, k, experts=False, final=False):
                pool.wait_ge(ld_w, (c - QKV_CHUNKS) * 32 + 32)
                gated(pool, 2)
                to, cols = ws, bass.ds(c * CHUNK, CHUNK)
                if experts:
                    to, cols = wx, bass.ds(c * CHUNK - CW1, CHUNK)
                nc.gpsimd.tensor_copy(to[:, 0, cols], stage[:, 0, :]).then_inc(pool_own, 1)
                nc.gpsimd.tensor_copy(to[:, 2, cols], stage[:, 1, :]).then_inc(pool_own, 1)
                pool.wait_ge(pool_own, k + 2)
                nc.gpsimd.tensor_tensor(to[:, 1, cols], stage[:, 0, :], to[:, 0, cols].bitcast(F32), ALU.subtract)\
                    .then_inc(pool_own, 1)
                nc.gpsimd.tensor_tensor(to[0:R1, 3, cols], stage[0:R1, 1, :], to[0:R1, 2, cols].bitcast(F32), ALU.subtract)\
                    .then_inc(pool_own, 1)
                pool.wait_ge(pool_own, k + 4)
                pool.sem_inc(w_split, 1)
                if final:
                    return
                cols2 = bass.ds((c + 1) * CHUNK, CHUNK)
                pool.dma_start(stage[:, 0, :], wall0[:, cols2]).then_inc(ld_w, 16)
                pool.dma_start(stage[:, 1, :], wall1[:, cols2]).then_inc(ld_w, 16)

            norm_scale(0, NT + 1, 1)
            pool.dma_start(stage[:, 0, :], wall0[:, QKV:QKV + CHUNK]).then_inc(ld_w, 16)
            pool.dma_start(stage[:, 1, :], wall1[:, QKV:QKV + CHUNK]).then_inc(ld_w, 16)
            k0 = 1
            rest = A_CHUNKS - QKV_CHUNKS
            per = rest // (PAIRS - 1)
            assert per * (PAIRS - 1) == rest

            def body(it, nxt, chunks):
                n = 4 * per + 1
                base = it * n + k0
                pool.wait_ge(ln_split, it + 1)
                pool.wait_ge(a_v, 1 + it * 3)
                gated(pool, 2)
                for k in range(3):
                    nc.gpsimd.tensor_copy(xs[:, k, N + P:].rearrange("p (i y x) -> p i y x", i=2, x=WS),
                                          xs[:, k, 0:N].bitcast(F32).rearrange("p (i y x) -> p i y x", i=2, x=W)[:, :, 0:WS, 0:WS])\
                        .then_inc(a_xw, 1)
                pool.wait_ge(a_ka, it + 1)
                pool.wait_ge(a_kb, it * 2 + 2)
                pool.wait_ge(a_s, 1 + it * UNITS)
                gated(pool, 2)
                kf = ka.rearrange("p g i t -> p (g i) t")
                kef = kae.rearrange("p g i t -> p (g i) t")
                nc.gpsimd.tensor_copy(kef[:, :, 0:WS * EW].rearrange("p a (y x) -> p a y x", x=EW),
                                      kf[:, :, 0:WS * W].rearrange("p a (y x) -> p a y x", x=W)[:, :, :, WS:W])\
                                          .then_inc(a_kae, 1)
                nc.gpsimd.tensor_copy(kef[:, :, EREAL // 2:EREAL], kf[:, :, WS * W:T]).then_inc(a_kae, 1)
                pool.wait_ge(a_qa, it * 4 + 4)
                pool.wait_ge(a_qw, it * 4 + 4)
                gated(pool, 2)
                nc.gpsimd.tensor_copy(qb[:, :, 0:EREAL // 2].rearrange("p a (y x) -> p a y x", x=EW),
                                      qs.rearrange("p a (y x) -> p a y x", x=W)[:, :, :, WS:W]).then_inc(a_qb, 1)
                nc.gpsimd.tensor_copy(qb[:, :, EREAL // 2:EREAL], qs[:, :, WS * W:T]).then_inc(a_qb, 1)
                if nxt:
                    norm_scale(it + 1, NT + 1, base + 1)
                for c in range(chunks):
                    split_chunk(it * per + QKV_CHUNKS + c, base + nxt + 4 * c)

            with pool.Fori(0, PAIRS - 1) as it:
                body(it, True, per)
            body(PAIRS - 1, False, 0)
            k1 = (PAIRS - 1) * (4 * per + 1) + k0
            chunk = A_CHUNKS
            for ph in range(1, 4):
                for n in range(PAIRS):
                    k1 += 1
                    norm_scale(4 * ph + n, NT, k1)
                    upto = min(NCHUNK, A_CHUNKS + max(0, 4 * ph + n - 4) + 2 * max(0, 4 * ph + n - 8))
                    if ph == 1 and n == 1:
                        pool.wait_ge(o_res, 1 + 2 * PAIRS)
                    while chunk < upto:
                        split_chunk(chunk, k1, experts=chunk >= A_CHUNKS, final=chunk == NCHUNK - 1)
                        k1 += 4
                        chunk += 1

        @block.vector
        def _(dve):
            V = nc.vector
            start_counts(dve, "dve")

            def tiles_of(n, tiles):
                return [xres[:, n * NT + j, :] for j in range(NT)] + ([xedge] if tiles > NT else [])

            def front_norm(f, n, tiles, used=()):
                front_stats(f, n, tiles)
                front_scale(f, n, tiles, range(tiles), used)

            def front_stats(f, n, tiles):
                xt_ = tiles_of(n, tiles)
                if tiles > NT:
                    dve.wait_ge(ld_e, 16 * n)
                for j in range(tiles):
                    last = V.bn_stats(st6[:, j, :], xt_[j])
                last.then_inc(dve_own, 1)
                dve.wait_ge(dve_own, f + 1)
                gated(dve, 1)
                for j in range(tiles):
                    last = V.bn_aggr(mv[:, j, :], st6[:, j, :])
                last.then_inc(ln_mv, 1)

            def front_scale(f, n, tiles, js, used=()):
                xt_ = tiles_of(n, tiles)
                if js[0] == 0:
                    dve.wait_ge(ln_rstd, f + 1)
                    dve.wait_ge(ln_tr, 2 * f)
                    for s_, v_ in used:
                        dve.wait_ge(s_, v_)
                for j in js:
                    V.tensor_scalar(xn[:, j, 0:D], xt_[j], mv[:, j, 0:1], rstd[:, j:j + 1], ALU.subtract, ALU.mult)
                    last = V.tensor_scalar(xn[:, j, D:256], xt_[j][:, P:D], mv[:, j, 0:1], rstd[:, j:j + 1],
                                           ALU.subtract, ALU.mult)
                if js[-1] == tiles - 1:
                    last.then_inc(ln_xn, 1)

            def front_split(f, tiles, *used, parts=(0, 1, 2)):
                c = tiles * P
                if 0 in parts:
                    dve.wait_ge(ln_xt, 2 * f + 2)
                    if tiles > NT:
                        dve.wait_ge(ln_xt_e, f + 1)
                    for s_, v_ in used:
                        dve.wait_ge(s_, v_)
                    V.tensor_copy(xs[:, 0, 0:c], xt[:, 0, 0:c])
                    V.tensor_copy(xs[:, 2, 0:c], xt[:, 1, 0:c]).then_inc(ln_hi, 1)
                if 1 in parts:
                    dve.wait_ge(ln_hi, f + 1)
                    V.tensor_tensor(xs[:, 1, 0:c], xt[:, 0, 0:c], xs[:, 0, 0:c].bitcast(F32), ALU.subtract)
                if 2 in parts:
                    V.tensor_tensor(xs[R1:P, 2, 0:c], xt[R1:P, 1, 0:c], xs[R1:P, 2, 0:c].bitcast(F32), ALU.subtract)\
                        .then_inc(ln_split, 1)

            def residual(it, banks, ready, n0, done):
                for b in range(2):
                    dve.wait_ge(ready, 2 * n0 + b + 2)
                    rows = xres[:, bass.ds(it * NT + 2 * b, 2), :]
                    V.tensor_tensor(rows, ps[:, banks[b], 0:2 * D].rearrange("p (t d) -> p t d", d=D), rows,
                                    ALU.add).then_inc(done, 1)

            def heads(v_):
                return v_.rearrange("p a (b c) -> p a b c", c=HD)[:, :, 0:5:4, :]

            dve.wait_ge(ld_x, 32)
            front_norm(0, 0, NT + 1)
            dve.wait_ge(ld_c, 16 * 6)
            V.tensor_scalar(bcol[:, G:2 * G], bcol[:, G:2 * G], HD ** -0.5, None, ALU.mult)
            V.tensor_scalar(bcol[:, CQB:CQB + 2], bcol[:, CQB:CQB + 2], AD ** -0.5, None, ALU.mult)\
                .then_inc(setup_dve, 1)
            dve.wait_ge(q_hi, 1)
            V.tensor_tensor(ws[:, 1, 0:QKV], first[:, 0], ws[:, 0, 0:QKV].bitcast(F32), ALU.subtract)
            V.tensor_tensor(ws[0:R1, 3, 0:QKV], first[0:R1, 1], ws[0:R1, 2, 0:QKV].bitcast(F32), ALU.subtract)\
                .then_inc(q_lo, 1)
            front_split(0, NT + 1)
            V.memset(room[:, 0:(NT + 3) * HP * VB], 0.0).then_inc(setup_dve, 1)
            dve.wait_ge(setup_dve, 2)
            for v_ in (ve, vee):
                V.memset(v_.rearrange("p t a (b c) -> p (t a) b c", c=HD)[:, :, 2:7:4, :], 1.0)
            for s in range(3):
                rows = slice(EREAL, P) if s < 2 else slice(0, P)
                V.tensor_copy(heads(vee[rows, s]), brow[rows, 0, :].rearrange("p (a b c) -> p a b c", b=2, c=HD))
            V.tensor_copy(maskb[:], pt[:, 0, 0, 0:P])
            V.tensor_copy(identb[:], ident[:]).then_inc(setup_dve, 1)

            def body_a(it, nxt):
                dve.wait_ge(a_k, it * G + 1)
                for r in range(HG):
                    to = ka[64 * (r % 2):64 * (r % 2) + HD, r // 2 * G].rearrange("p i t -> p (i t)")
                    last = V.tensor_scalar(to, ps[32 * r:32 * r + HD, G, :], HD ** -0.5,
                                           bcol[32 * r:32 * r + HD, G:G + 1], ALU.mult, ALU.add)
                last.then_inc(a_ka, 1)
                for q in range(4):
                    dve.wait_ge(a_rel, it * 4 + q + 1)
                    position_terms(V.tensor_copy, 1, q).then_inc(a_qw, 1)
                for i in range(2):
                    dve.wait_ge(a_v, 1 + it * 3 + i + 1)
                    for t in range(2):
                        V.tensor_tensor(heads(ve[0:QT, 2 * i + t]),
                                        ps[0:QT, V_BANKS[i], t * D:t * D + D].rearrange("p (a b c) -> p a b c", b=2, c=HD),
                                        brow[0:QT, 0, :].rearrange("p (a b c) -> p a b c", b=2, c=HD), ALU.add)\
                                            .then_inc(a_ve, 1)
                dve.wait_ge(a_v, 1 + it * 3 + 3)
                for i in range(2):
                    V.tensor_tensor(heads(vee[0:EREAL, i]),
                                    ps[EREAL * i:EREAL * i + EREAL, V_BANKS[2], 0:D].rearrange("p (a b c) -> p a b c", b=2, c=HD),
                                    brow[0:EREAL, 0, :].rearrange("p (a b c) -> p a b c", b=2, c=HD), ALU.add)\
                                        .then_inc(a_ve, 1)
                base = it * UNITS
                for u in range(UNITS + 2):
                    if u < UNITS:
                        rows, parts, keys, i, h = unit(u)
                        dve.wait_ge(a_s, 1 + base + u + 1)
                        if u >= 2:
                            dve.wait_ge(a_p, base + u - 1)
                        b0 = UH * (u % 2)
                        V.tensor_reduce(nm[0:rows, u % 2, 0:UH * parts],
                                        ps[0:rows, b0:b0 + UH, 0:parts * keys].rearrange("p h (t k) -> p h t k", k=keys),
                                        AX.X, ALU.max, negate=True).then_inc(a_nm, 1)
                    if u >= 2:
                        v = u - 2
                        rows, parts, keys, i, h = unit(v)
                        dve.wait_ge(a_o, base + v + 1)
                        n = parts * rows
                        dn = den[0:32, v % 2, 0:n]
                        V.reciprocal(dn, ps[32:64, 6, 0:n]).then_inc(a_own, 1)
                        dve.wait_ge(a_own, base + v + 1)
                        at = slice(32 * (h % 4), 32 * (h % 4) + 32)
                        dst = (ot0 if h < 4 else ot1)[at]
                        if parts == 2:
                            V.tensor_tensor(dst[:, i * T:i * T + n], ps[0:32, 6, 0:n], dn, ALU.mult).then_inc(a_on, 1)
                        else:
                            d3 = dst.rearrange("p (i t) -> p i t", i=2)
                            p3, n3 = (b_.rearrange("p (i t) -> p i t", i=2) for b_ in (ps[0:32, 6, 0:n], dn))
                            V.tensor_tensor(d3[:, :, 0:WS * W].rearrange("p i (y x) -> p i y x", x=W)[:, :, :, WS:W],
                                            p3[:, :, 0:WS * EW].rearrange("p i (y x) -> p i y x", x=EW),
                                            n3[:, :, 0:WS * EW].rearrange("p i (y x) -> p i y x", x=EW), ALU.mult)
                            V.tensor_tensor(d3[:, :, WS * W:T], p3[:, :, EREAL // 2:EREAL], n3[:, :, EREAL // 2:EREAL],
                                            ALU.mult).then_inc(a_on, 1)
                    front = (it + 1, it + 1, NT + 1) if nxt else (PAIRS, 0, NT)
                    if u == 5:
                        if nxt:
                            dve.wait_ge(ld_r, 32)
                        front_stats(*front)
                    if u == 7:
                        front_scale(*front, range(0, 3), [(ln_tr_e, it + 1)])
                    if u == 8:
                        front_scale(*front, range(3, front[2]))
                    if 13 <= u < 16:
                        front_split(it + 1, front[2], (a_v, 3 * it + 4), parts=(u - 13,))
                residual(it, (6, 7), o_proj, it, o_res)

            loop(dve, body_a)

            def body_b(it, nxt):
                front_norm(it + (PAIRS + 1), it + 1 if nxt else 0, NT)
                front_split(it + (PAIRS + 1), NT, (b_h, MC * it + MC))
                residual(it, (4, 5), b_y, it, b_res)

            loop(dve, body_b)

            dve.wait_ge(b_res, 1 + 2 * PAIRS)
            V.memset(cv.rearrange("p a b c -> p (a b c)"), 1.0).then_inc(setup_dve, 1)
            dve.wait_ge(setup_dve, 4)

            def body_c(it, nxt):
                front = it + (2 * PAIRS + 1), it + 1 if nxt else 0, NT
                front_stats(*front)
                for b in range(2):
                    dve.wait_ge(c_v, it * 2 + b + 1)
                    for t in range(2):
                        last = V.tensor_tensor(cv[:, 2 * b + t, :, 0:AD],
                                               ps[:, 3 + b, t * D:t * D + D].rearrange("p (h c) -> p h c", c=AD),
                                               brow[:, 1, :].rearrange("p (h c) -> p h c", c=AD), ALU.add)
                    last.then_inc(c_ve, 1)
                n = 2 * AH
                base = it * n
                for u in range(n + 2):
                    if u < n:
                        dve.wait_ge(c_s, base + u + 1)
                        if u >= 4:
                            dve.wait_ge(c_p, base + u - 3)
                        V.reduce_max(cnm[:, u % 4, 0:1], ps[:, u % 3, 0:P], AX.X, negate=True)
                        V.reduce_max(cnm[:, u % 4, 1:2], ps[:, u % 3, P:3 * P], AX.X, negate=True).then_inc(c_nm, 1)
                    if u >= 2:
                        v = u - 2
                        b, h = v // AH, v % AH
                        dve.wait_ge(c_o, base + v + 1)
                        po = ps[:, 5 + v % 2, 0:2 * (AD + 1)].rearrange("p (t c) -> p t c", c=AD + 1)
                        V.reciprocal(rs[:, v % 2, 0:2], po[:, :, AD]).then_inc(c_own, 1)
                        dve.wait_ge(c_own, base + v + 1)
                        V.tensor_tensor(co[:, 2 * b:2 * b + 2, AD * h:AD * h + AD], po[:, :, 0:AD],
                                        rs[:, v % 2, 0:2].unsqueeze(2).broadcast_to([P, 2, AD]), ALU.mult)\
                                            .then_inc(c_on, 1)
                    if u < 2:
                        front_scale(*front, range(2 * u, 2 * u + 2))
                    if 5 <= u < 8:
                        front_split(it + (2 * PAIRS + 1), NT, (c_v, 2 * it + 2), parts=(u - 5,))
                dve.wait_ge(o_tr, it + 1)
                V.tensor_copy(ot1[0:R1, :], ps[0:R1, 4, :]).then_inc(o_td, 1)
                residual(it, (5, 6), o_proj, it + PAIRS, o_res)

            loop(dve, body_c)

            ncm, csum, rcs, nrm, rsum, rrs = (dstat[:, k, :] for k in range(6))

            def body_d(it, nxt):
                for n in range(NT + 1):
                    if n < NT:
                        dve.wait_ge(d_l, it * NT + n + 1)
                        V.reduce_max(nrm[:, n:n + 1], ps[:, n % 2 * 2:n % 2 * 2 + 2, :].rearrange("p a c -> p (a c)"),
                                     AX.X, negate=True).then_inc(d_nrm, 1)
                        for k in (2 * n, 2 * n + 1):
                            dve.wait_ge(d_lt, it * ST + k + 1)
                            V.tensor_reduce(ncm[:, 2 * k:2 * k + 2], ps[:, 6 + k % 2, :].rearrange("p (b t) -> p b t", b=2),
                                            AX.X, ALU.max, negate=True).then_inc(d_ncm, 1)
                    if n:
                        k = 2 * n - 2
                        dve.wait_ge(d_dt, it * ST + k + 2)
                        V.reciprocal(rcs[:, 2 * k:2 * k + 4], csum[:, 2 * k:2 * k + 4]).then_inc(d_own, 1)
                        dve.wait_ge(d_own, it * NT + n)
                        for st in (k, k + 1):
                            V.tensor_tensor(dt_[:, :, st, :], dt_[:, :, st, :],
                                            rcs[:, 2 * st:2 * st + 2].unsqueeze(2).broadcast_to([P, 2, T]),
                                            ALU.mult).then_inc(d_dn, 1)
                for b in range(2):
                    dve.wait_ge(d_dtr, it * NT + 2 * b + 1)
                    V.tensor_copy(dd[b][:, 0, :], ps[:, 4 * b:4 * b + 2, :].rearrange("p a c -> p (a c)"))\
                        .then_inc(d_de, 1)
                for b in range(2):
                    for h in range(2):
                        dve.wait_ge(d_sh, it * 4 + 2 * b + h + 1)
                        bank = 4 * b + h
                        V.tensor_tensor(slot_cols(slots[1], b, h), ps[:, bank, :].rearrange("p (e s) -> p e s", e=2),
                                        slot_cols(slots[0], b, h).bitcast(F32), ALU.subtract)
                        V.tensor_tensor(slot_cols(slots[2], b, h)[R1:P],
                                        ps[R1:P, bank + 2, :].rearrange("p (e s) -> p e s", e=2),
                                        slot_cols(slots[2], b, h)[R1:P].bitcast(F32), ALU.subtract).then_inc(d_ss, 1)
                V.reciprocal(rrs[:, 0:NT], rsum[:, 0:NT])
                if nxt:
                    front_norm(it + (3 * PAIRS + 1), it + 1, NT, [(d_st, 1 + 4 * it + 4)])
                for e in range(NE):
                    for b in range(2):
                        dve.wait_ge(d_y, 1 + it * 2 * NE + 2 * e + b + 1)
                        V.tensor_tensor(yy[:, b, 2 * e:2 * e + 2, :],
                                        ps[:, 4 + b, 0:2 * D].rearrange("p (s d) -> p s d", d=D),
                                        b2row[:, e, :].unsqueeze(1).broadcast_to([P, 2, D]), ALU.add).then_inc(d_ye, 1)
                    if nxt and e == 3:
                        front_split(it + (3 * PAIRS + 1), NT, (d_l, NT * it + NT), (d_lt, ST * it + ST))
                for n in range(NT):
                    if n % 2 == 0:
                        dve.wait_ge(d_o, 1 + it * 2 + n // 2 + 1)
                    xt_ = xres[:, it * NT + n, :]
                    V.scalar_tensor_tensor(xt_, ps[:, 6 + n // 2, (n % 2) * D:(n % 2) * D + D], rrs[:, n:n + 1], xt_,
                                           ALU.mult, ALU.add).then_inc(d_res, 1)

            loop(dve, body_d)

        @block.scalar
        def _(act):
            A = nc.scalar
            start_counts(act, "act")

            def front_turned(f, tiles, affine):
                for k in range(3 if tiles > NT else 2):
                    front_turned_part(f, affine, k)

            def front_turned_part(f, affine, k):
                def norm(k):
                    if not affine:
                        return {}
                    return dict(scale=bcol[:, affine + k:affine + k + 1], bias=bcol[:, affine + 2 + k:affine + 3 + k])
                if k == 0:
                    act.wait_ge(ln_split, f)
                if k < 2:
                    act.wait_ge(ln_tr, 2 * f + k + 1)
                    A.activation(xt[:, k, 0:N], ps[:, 7, :], ACT.Identity, **norm(k)).then_inc(ln_xt, 1)
                else:
                    act.wait_ge(ln_tr_e, f + 1)
                    for k in range(2):
                        last = A.activation(xt[:, k, N:N + P], ps[:, 7, k * P:k * P + P], ACT.Identity, **norm(k))
                    last.then_inc(ln_xt_e, 1)

            act.wait_ge(ld_q, 32)
            for k in range(2):
                last = A.copy(ws[:, 2 * k, 0:QKV], first[:, k])
            last.then_inc(q_hi, 1)
            act.wait_ge(ld_c, 16 * 6)
            A.copy(ka.rearrange("p a i t -> p (a i) t"), kc.unsqueeze(1).broadcast_to([P, 2 * HP, T]))\
                .then_inc(setup_act, 1)
            front_turned(0, NT + 1, N1)
            A.copy(kae.rearrange("p a i t -> p (a i) t"), kec.unsqueeze(1).broadcast_to([P, 2 * HP, EKEYS]))\
                .then_inc(setup_act, 1)
            act.wait_ge(setup_act, 2)
            act.wait_ge(setup_dve, 1)
            for a in range(HP):
                for r in (0, 1):
                    src = slice(32 * (2 * (a // G) + r), 32 * (2 * (a // G) + r) + HD)
                    last = A.activation(kae[64 * r:64 * r + HD, a, :, EREAL:EKEYS],
                                        kec[src, EREAL:EKEYS].unsqueeze(1).broadcast_to([HD, 2, EPAD]), ACT.Identity,
                                        bias=bcol[src, G + a % G:G + 1 + a % G])
            last.then_inc(setup_act, 1)

            def body_a(it, nxt):
                for g in range(G):
                    act.wait_ge(a_q, it * G + g + 1)
                    A.activation(qraw[:, g, :], ps[:, g, :], ACT.Identity, bias=bcol[:, g:g + 1]).then_inc(a_qraw, 1)
                for g in (1, 2):
                    act.wait_ge(a_k, it * G + g + 1)
                    for r in range(HG):
                        to = ka[64 * (r % 2):64 * (r % 2) + HD, r // 2 * G + g].rearrange("p i t -> p (i t)")
                        last = A.activation(to, ps[32 * r:32 * r + HD, G + g, :], ACT.Identity, scale=HD ** -0.5,
                                            bias=bcol[32 * r:32 * r + HD, G + g:G + g + 1])
                    last.then_inc(a_kb, 1)
                for q in range(4):
                    act.wait_ge(a_rel, it * 4 + q + 1)
                    position_terms(A.copy, 0, q).then_inc(a_qa, 1)
                base = it * UNITS
                for u in range(UNITS + 1):
                    if u >= 1:
                        rows, parts, keys, i, h = unit(u - 1)
                        half, wide = keys // 2, UH * parts * rows
                        act.wait_ge(a_t, base + u)
                        if u >= 3:
                            act.wait_ge(a_o, base + u - 2)
                        A.activation(pt[0:half, (u - 1) % 2, :, 0:wide], ps[0:half, 4:6, 0:wide], ACT.Copy)\
                            .then_inc(a_pta, 1)
                    if u < UNITS:
                        rows, parts, keys, i, h = unit(u)
                        act.wait_ge(a_nm, base + u + 1)
                        for k in range(UH * parts):
                            c0 = k % parts * keys
                            last = A.activation(pp[0:rows, u % 2, k, 0:keys],
                                                ps[0:rows, UH * (u % 2) + k // parts, c0:c0 + keys],
                                                ACT.Exp, bias=nm[0:rows, u % 2, k:k + 1])
                        last.then_inc(a_p, 1)
                    if 9 <= u < (12 if nxt else 11):
                        front_turned_part(it + 1, N1 if nxt else N2, u - 9)
            loop(act, body_a)
            act.wait_ge(o_res, 1 + 2 * PAIRS)

            def body_b(it, nxt):
                act.wait_ge(b_y, 1 + it * 2)
                for m in range(MC):
                    act.wait_ge(b_h, it * MC + m + 1)
                    A.activation(hT[:, m, :], ps[:, m % 4, :], ACT.Gelu, bias=bcol[:, L1B + m:L1B + m + 1])\
                        .then_inc(b_gelu, 1)
                front_turned(it + (PAIRS + 1), NT, N2 if nxt else 0)

            loop(act, body_b)

            def body_c(it, nxt):
                act.wait_ge(c_qk, it * 3 + 1)
                A.activation(cqk[:, 0, :], ps[:, 0, :], ACT.Identity, scale=AD ** -0.5, bias=bcol[:, CQB:CQB + 1])
                act.wait_ge(c_qk, it * 3 + 2)
                A.activation(cqk[:, 1, :], ps[:, 1, :], ACT.Identity, bias=bcol[:, CKB:CKB + 1])
                act.wait_ge(c_qk, it * 3 + 3)
                A.activation(cq2[0:AD, 0, :], ps[0:AD, 2, :], ACT.Identity, scale=AD ** -0.5, bias=bcol[0:AD, CQB + 1:CQB + 2])
                A.activation(cq2[0:AD, 1, :], ps[AD:P, 2, :], ACT.Identity, bias=bcol[AD:P, CKB + 1:CKB + 2])\
                    .then_inc(c_qt, 1)
                n = 2 * AH
                base = it * n
                for u in range(n + 1):
                    if u < n:
                        act.wait_ge(c_nm, base + u + 1)
                        A.activation(cp[:, u % 2, 0:P], ps[:, u % 3, 0:P], ACT.Exp, bias=cnm[:, u % 4, 0:1])
                        A.activation(cp[:, u % 2, P:3 * P], ps[:, u % 3, P:3 * P], ACT.Exp, bias=cnm[:, u % 4, 1:2])\
                            .then_inc(c_p, 1)
                    if u >= 1:
                        act.wait_ge(c_t, base + u)
                        if u >= 3:
                            act.wait_ge(c_o, base + u - 2)
                        A.activation(cpt[:, (u - 1) % 2, :], ps[:, 3 + (u - 1) % 2, 0:3 * P], ACT.Copy)\
                            .then_inc(c_pt, 1)
                    if u in (2, 3):
                        front_turned_part(it + (2 * PAIRS + 1), 0, u - 2)
                act.wait_ge(o_tr, it + 1)
                A.activation(ot0[:], ps[:, 3, :], ACT.Copy).then_inc(o_ta, 1)

            loop(act, body_c)
            ncm, csum, rcs, nrm, rsum, rrs = (dstat[:, k, :] for k in range(6))

            def body_d(it, nxt):
                act.wait_ge(d_o, 1 + it * 2)
                for n in range(NT + 1):
                    if n < NT:
                        act.wait_ge(d_nrm, it * NT + n + 1)
                        if n >= 2:
                            act.wait_ge(d_ct, it * NT + n - 1)
                        A.activation(cc[:, n % 2, :], ps[:, n % 2 * 2:n % 2 * 2 + 2, :].rearrange("p a c -> p (a c)"),
                                     ACT.Exp, bias=nrm[:, n:n + 1], accum_out=rsum[:, n:n + 1]).then_inc(d_c, 1)
                    if n:
                        act.wait_ge(d_ct, it * NT + n)
                        A.activation(ct[:, :, n * P - P:n * P], ps[:, 4:6, :].rearrange("p a (s c) -> p (a s) c", c=P), ACT.Copy)\
                            .then_inc(d_cte, 1)
                    if n < NT:
                        for k in (2 * n, 2 * n + 1):
                            act.wait_ge(d_ncm, it * ST + k + 1)
                            for b in range(2):
                                last = A.activation(dt_[:, b, k, :], ps[:, 6 + k % 2, b * T:b * T + T], ACT.Exp,
                                                    bias=ncm[:, 2 * k + b:2 * k + b + 1],
                                                    accum_out=csum[:, 2 * k + b:2 * k + b + 1])
                            last.then_inc(d_dt, 1)
                for b in range(2):
                    act.wait_ge(d_dtr, it * NT + 2 * b + 2)
                    A.activation(dd[b][:, 1, :], ps[:, 4 * b + 2:4 * b + 4, :].rearrange("p a c -> p (a c)"), ACT.Copy)\
                        .then_inc(d_da, 1)
                for b in range(2):
                    for h in range(2):
                        act.wait_ge(d_st, 1 + it * 4 + 2 * b + h + 1)
                        bank = 4 * b + h
                        A.activation(slot_cols(slots[0], b, h), ps[:, bank, :].rearrange("p (e s) -> p e s", e=2), ACT.Copy)
                        A.activation(slot_cols(slots[2], b, h), ps[:, bank + 2, :].rearrange("p (e s) -> p e s", e=2),
                                     ACT.Copy).then_inc(d_sh, 1)
                for e in range(NE):
                    if nxt and e in (1, 2):
                        front_turned_part(it + (3 * PAIRS + 1), 0, e - 1)
                    act.wait_ge(d_y, 1 + it * 2 * NE + 2 * e)
                    for m in range(MC):
                        act.wait_ge(d_h, it * NE * MC + e * MC + m + 1)
                        A.activation(hTd[:, m, :], ps[:, (e * MC + m) % 4, :], ACT.Gelu_apprx_tanh,
                                     bias=bcol[:, E1B + e * MC + m:E1B + e * MC + m + 1]).then_inc(d_gelu, 1)

            loop(act, body_d)

        @block.tensor
        def _(pe):
            tr = nc.tensor.transpose
            start_counts(pe, "pe")

            def front_turn(f, tiles):
                for k in range(3 if tiles > NT else 2):
                    front_turn_part(f, k)

            def front_turn_part(f, k, *free):
                if k == 0:
                    pe.wait_ge(ln_xn, f + 1)
                    for s_, v_ in free:
                        pe.wait_ge(s_, v_)
                pe.wait_ge(ln_xt, 2 * f + k)
                if k < 2:
                    for j in range(NT):
                        last = tr(ps[:, 7, j * P:j * P + P], xn[:, j, k * P:k * P + P], ident[:])
                    last.then_inc(ln_tr, 1)
                else:
                    for k in range(2):
                        last = tr(ps[:, 7, k * P:k * P + P], xn[:, NT, k * P:k * P + P], ident[:])
                    last.then_inc(ln_tr_e, 1)

            pe.wait_ge(ld_c, 16 * 6)
            front_turn(0, NT + 1)
            pe.wait_ge(ld_p, 16 * HG)
            pe.wait_ge(q_hi, 1)
            pe.wait_ge(q_lo, 1)

            def scores_full(u, i, h):
                for t in range(2):
                    for k in range(UH):
                        q = slice(64 * k, 64 * k + 64)
                        keys = ka[q, operands(h), i, :].rearrange("p (y x) -> p y x", x=W)[:, 0:WS, 0:WS]
                        last = mm(ps[0:QR, UH * (u % 2) + k, 2 * QT * t:2 * QT * t + 2 * QT],
                                  qs[q, 2 * operands(h) + i, QR * t:QR * t + QR], keys, start=True, stop=True)
                return last

            def scores_border(u, h):
                for i in range(2):
                    for k in range(UH):
                        q = slice(64 * k, 64 * k + 64)
                        last = mm(ps[64 * i:64 * i + 64, UH * (u % 2) + k, 0:EKEYS],
                                  qb[q, 2 * operands(h) + i, :], kae[q, operands(h), i, :], start=True, stop=True)
                return last

            def queries(g):
                product(ps[:, g, :], (CQ + g * P, CQ + g * P + P), xcols(0, N)).then_inc(a_q, 1)

            def body_a(it, nxt):
                for g in range(G):
                    product(ps[:, 3 + g, :], (CK + g * P, CK + g * P + P), xcols(0, N)).then_inc(a_k, 1)
                pe.wait_ge(o_res, 1 + it * 2)
                pe.wait_ge(a_qraw, it * G + 3)
                gated(pe, 0)
                q4 = qraw.rearrange("p g (i t) -> p (g i) t", i=2)
                for step in range(4):
                    if step == 1:
                        pe.wait_ge(a_ka, it + 1)
                        pe.wait_ge(a_kb, it * 2 + 1)
                    if step == 2:
                        pe.wait_ge(a_kb, it * 2 + 2)
                    if step:
                        gated(pe, 0)
                    for k in range(4):
                        at = 4 * step + k
                        for cols in range(2):
                            rows = q4.rearrange("p a (y x) -> p a y x", x=W)
                            last = mm(ps[:, REL_BANKS[cols][step], 96 * k:96 * k + 96], relt[:, W * cols + at, :],
                                      rows[:, :, :, at] if cols else rows[:, :, at, :], start=True, stop=True)
                    last.then_inc(a_rel, 1)
                pe.wait_ge(a_xw, it * 3 + 3)
                for i in range(2):
                    pe.wait_ge(a_qw, it * 4 + 1 + 2 * i)
                    gated(pe, 0)
                    for t in range(2):
                        at = N + P + (2 * i + t) * QT
                        last = product(ps[0:QT, V_BANKS[i], t * D:t * D + D], (CV, CV + D), xcols(at, at + QT), True)
                    last.then_inc(a_v, 1)
                pe.wait_ge(a_qa, it * 4 + 3)
                gated(pe, 0)
                product(ps[:, V_BANKS[2], 0:D], (CV, CV + D), xcols(N, N + P), True).then_inc(a_v, 1)
                base = it * UNITS
                for u in range(UNITS + 2):
                    if u < UNITS:
                        rows, parts, keys, i, h = unit(u)
                        if u == 0:
                            pe.wait_ge(a_qa, it * 4 + 4)
                            pe.wait_ge(a_qw, it * 4 + 4)
                        if u >= 2:
                            pe.wait_ge(a_p, base + u - 1)
                        if u == MAIN:
                            pe.wait_ge(a_kae, it * 2 + 2)
                            pe.wait_ge(a_qb, it * 2 + 2)
                        gated(pe, 0)
                        (scores_full(u, i, h) if u < MAIN else scores_border(u, h)).then_inc(a_s, 1)
                    if 1 <= u <= UNITS:
                        v = u - 1
                        rows, parts, keys, i, h = unit(v)
                        half = keys // 2
                        if v == 0:
                            pe.wait_ge(a_ve, it * 6 + 6)
                        pe.wait_ge(a_p, base + u)
                        pe.wait_ge(a_pta, 1 + base + v)
                        for k in range(2):
                            for n in range(UH * parts):
                                last = tr(ps[0:half, 4 + k, n * rows:n * rows + rows],
                                          pp[0:rows, v % 2, n, k * half:k * half + half], ident[0:rows, 0:rows])
                        last.then_inc(a_t, 1)
                    if nxt and u >= UNITS:
                        if u == UNITS:
                            pe.wait_ge(ln_split, it + 2)
                        queries(u - UNITS)
                    if u >= 2:
                        v = u - 2
                        rows, parts, keys, i, h = unit(v)
                        pe.wait_ge(a_pta, 1 + base + v + 1)
                        pe.wait_ge(a_on, 1 + base + v)
                        for n in range(UH):
                            at, vc = n * parts * rows, slice(n * 3 * HD, n * 3 * HD + 4 * HD)
                            if parts == 2:
                                for k in range(2):
                                    last = mm(ps[0:64, 6, 0:2 * QR], ve[0:QT, 2 * i + k, h, vc],
                                              pt[0:QT, v % 2, k, at:at + 2 * QR], start=n + k == 0, stop=n + k == 2)
                            else:
                                for part in ((None, 0, 1), (0, 1, None))[n]:
                                    if part is None:
                                        last = mm(ps[0:64, 6, 0:P], vee[:, 2, h, vc], pt[:, v % 2, 1, at:at + P],
                                                  start=n == 0, stop=n == 1)
                                    else:
                                        last = mm(ps[0:64, 6, 64 * part:64 * part + 64], vee[:, part, h, vc],
                                                  pt[:, v % 2, 0, at + 64 * part:at + 64 * part + 64], start=False, stop=False)
                        last.then_inc(a_o, 1)
                    if 9 <= u < (12 if nxt else 11):
                        front_turn_part(it + 1, u - 9, (ln_xt_e, it + 1))
                if nxt:
                    queries(2)
                pe.wait_ge(a_on, 1 + base + UNITS)
                project(0, (6, 7))

            def project(which, banks):
                for j in range(NT):
                    dst = ps[:, banks[j // 2], (j % 2) * D:(j % 2) * D + D]
                    mm(dst, ot0[:, j * P:j * P + P], wproj[:, which, 0, :], start=True, stop=False)
                    last = mm(dst, ot1[0:R1 + 1, j * P:j * P + P], wproj[0:R1 + 1, which, 1, :], start=False, stop=True)
                    if j % 2:
                        last.then_inc(o_proj, 1)

            pe.wait_ge(ln_split, 1)
            for g in range(G):
                queries(g)
            pe.wait_ge(setup_pool, 3)
            pe.wait_ge(setup_dve, 3)
            pe.wait_ge(setup_act, 3)
            pe.wait_ge(ld_r, 32)
            loop(pe, body_a)

            pe.wait_ge(w_split, A_CHUNKS - QKV_CHUNKS)
            pe.wait_ge(o_res, 1 + 2 * PAIRS)

            def body_b(it, nxt):
                pe.wait_ge(ln_split, it + (PAIRS + 1))
                for m in range(MC):
                    pe.wait_ge(b_gelu, 1 + it * MC + max(0, m - 3))
                    product(ps[:, m % 4, :], (CL1 + m * P, CL1 + m * P + P), xcols(0, N)).then_inc(b_h, 1)
                front_turn_part(it + (PAIRS + 1), 0)
                pe.wait_ge(ld_l2, 16)
                pe.wait_ge(b_gelu, 1 + it * MC + MC - 1)
                pe.wait_ge(b_res, 1 + it * 2)
                for j in range(NT):
                    dst = ps[:, 4 + j // 2, (j % 2) * D:(j % 2) * D + D]
                    mm(dst, ot1[L2ROW:L2ROW + 1, 0:P], wproj[L2ROW:L2ROW + 1, 0, 1, :], start=True, stop=False)
                    for m in range(MC):
                        if j == 0 and m == MC - 1:
                            pe.wait_ge(b_gelu, 1 + it * MC + MC)
                        last = mm(dst, hT[:, m, j * P:j * P + P], w2l[:, m, :], start=False, stop=m == MC - 1)
                    if j % 2:
                        last.then_inc(b_y, 1)
                    if j == 1:
                        front_turn_part(it + (PAIRS + 1), 1)

            loop(pe, body_b)

            pe.wait_ge(b_res, 1 + 2 * PAIRS)

            def queries_keys(split):
                pe.wait_ge(ln_split, split)
                for k in range(3):
                    product(ps[:, k, :], (CA + k * P, CA + k * P + P), xcols(0, N)).then_inc(c_qk, 1)

            queries_keys(2 * PAIRS + 1)

            def body_c(it, nxt):
                pe.wait_ge(o_res, 1 + it * 2 + 2 * PAIRS)
                n = 2 * AH
                base = it * n
                pe.wait_ge(c_qt, it + 1)
                for u in range(-2, n + 1):
                    if u < 0:
                        for j in (2 * u + 4, 2 * u + 5):
                            last = product(ps[:, 5 + u, (j % 2) * D:(j % 2) * D + D], (CAV, CAV + D),
                                           xcols(j * P, j * P + P), True)
                        last.then_inc(c_v, 1)
                    if u + 2 < n:
                        v = u + 2
                        b, h = v // AH, v % AH
                        if v >= 3:
                            pe.wait_ge(c_p, base + v - 2)
                        if h < 2:
                            rows = slice(AD * h, AD * h + AD)
                            q, k = cqk[rows, 0, :], cqk[rows, 1, :]
                        else:
                            q, k = cq2[0:AD, 0, :], cq2[0:AD, 1, :]
                        t0 = b * T
                        bank = ps[:, v % 3, :]
                        mm(bank[:, 0:P], q[:, t0:t0 + P], k[:, t0:t0 + P], start=True, stop=False)
                        mm(bank[:, 0:P], identb[:], maskb[:], start=False, stop=True)
                        mm(bank[:, P:3 * P], q[:, t0 + P:t0 + T], k[:, t0:t0 + T], start=True, stop=False)
                        mm(bank[:, 2 * P:3 * P], identb[:], maskb[:], start=False, stop=True).then_inc(c_s, 1)
                    if 0 <= u < n:
                        if u == 0:
                            pe.wait_ge(c_ve, it * 2 + 2)
                        pe.wait_ge(c_p, base + u + 1)
                        if u >= 2:
                            pe.wait_ge(c_pt, base + u - 1)
                        for k in range(3):
                            last = tr(ps[:, 3 + u % 2, k * P:k * P + P], cp[:, u % 2, k * P:k * P + P], ident[:])
                        last.then_inc(c_t, 1)
                    if u >= 1:
                        v = u - 1
                        b, h = v // AH, v % AH
                        pe.wait_ge(c_pt, base + v + 1)
                        if v >= 2:
                            pe.wait_ge(c_on, base + v - 1)
                        bank = ps[:, 5 + v % 2, :]
                        mm(bank[:, 0:AD + 1], cpt[:, v % 2, 0:P], cv[:, 2 * b, h, :], start=True, stop=True)
                        mm(bank[:, AD + 1:2 * AD + 2], cpt[:, v % 2, P:2 * P], cv[:, 2 * b, h, :], start=True, stop=False)
                        mm(bank[:, AD + 1:2 * AD + 2], cpt[:, v % 2, 2 * P:3 * P], cv[:, 2 * b + 1, h, :], start=False,
                           stop=True).then_inc(c_o, 1)
                    if u in (1, 2):
                        front_turn_part(it + (2 * PAIRS + 1), u - 1)
                if nxt:
                    queries_keys(it + (2 * PAIRS + 2))
                pe.wait_ge(c_on, base + n)
                for j in range(NT):
                    tr(ps[:, 3, j * P:j * P + P], co[:, j, 0:P], ident[:])
                for j in range(NT):
                    last = tr(ps[0:R1, 4, j * P:j * P + P], co[:, j, P:D], ident[:])
                last.then_inc(o_tr, 1)
                pe.wait_ge(o_td, it + 1)
                pe.wait_ge(o_ta, it + 1)
                project(1, (5, 6))

            loop(pe, body_c)

            pe.wait_ge(o_res, 1 + 4 * PAIRS)

            def body_d(it, nxt):
                pe.wait_ge(ln_split, it + (3 * PAIRS + 1))
                for n in range(NT + 1):
                    if n < NT:
                        if n >= 2:
                            pe.wait_ge(d_c, it * NT + n - 1)
                        for c in range(2):
                            last = product(ps[:, n % 2 * 2 + c, :], (CPHI + 512 * c, CPHI + 512 * c + 512),
                                           xcols(n * P, n * P + P), True)
                        last.then_inc(d_l, 1)
                    if n:
                        pe.wait_ge(d_c, it * NT + n)
                        if n > 1:
                            pe.wait_ge(d_cte, 1 + it * NT + n - 1)
                        for s in range(ST):
                            last = tr(ps[:, 4 + s // 4, (s % 4) * P:(s % 4) * P + P], cc[:, (n - 1) % 2, s * P:s * P + P], ident[:])
                        last.then_inc(d_ct, 1)
                    if n < NT:
                        for k in (2 * n, 2 * n + 1):
                            if k < 2:
                                pe.wait_ge(d_res, 1 + it * NT)
                            else:
                                pe.wait_ge(d_dt, it * ST + k - 1)
                            product(ps[:, 6 + k % 2, :], (CPHI + k * P, CPHI + k * P + P), xcols(0, N))\
                                .then_inc(d_lt, 1)

                def turn_dispatch(n, tiles):
                    for s in tiles:
                        last = tr(ps[:, 2 * n + s // 4, (s % 4) * P:(s % 4) * P + P],
                                  dt_[:, n // 2, s, n % 2 * P:n % 2 * P + P], ident[:])
                    return last

                pe.wait_ge(d_dn, it * ST + ST - 2)
                for n in range(2):
                    turn_dispatch(n, range(ST - 2))
                pe.wait_ge(d_dn, it * ST + ST)
                pe.wait_ge(d_cte, 1 + it * NT + NT)
                for n in range(NT):
                    turn_dispatch(n, range(ST - 2, ST) if n < 2 else range(ST)).then_inc(d_dtr, 1)
                for b in range(2):
                    pe.wait_ge(d_de, it * 2 + b + 1)
                    pe.wait_ge(d_da, it * 2 + b + 1)
                    if b:
                        gated(pe, 0)
                    for h in range(2):
                        for part in range(2):
                            for j in range(2):
                                last = mm(ps[:, 4 * b + 2 * part + h, :], xn[:, 2 * b + j, part * P:part * P + P],
                                          dd[b][:, j, 512 * h:512 * h + 512], start=j == 0, stop=j == 1)
                        last.then_inc(d_st, 1)
                pe.wait_ge(ld_w2, 32)
                pe.wait_ge(w_split, NCHUNK - QKV_CHUNKS)
                pe.wait_ge(d_ss, 1 + it * 4 + 3)
                for e in range(NE):
                    for m in range(MC):
                        if e == 0 and m == 2:
                            pe.wait_ge(d_ss, 1 + it * 4 + 4)
                        pe.wait_ge(d_gelu, 1 + it * NE * MC + max(0, e * MC + m - 3))
                        product(ps[:, (e * MC + m) % 4, :], (CW1 + (e * MC + m) * P, CW1 + (e * MC + m) * P + P),
                                scols(512 * e, 512 * e + 512)).then_inc(d_h, 1)
                    pe.wait_ge(d_gelu, 1 + it * NE * MC + e * MC + MC - 1)
                    pe.wait_ge(d_ye, 1 + it * 2 * NE + 2 * e)
                    for b in range(2):
                        for s in range(2):
                            for m in range(MC):
                                if b + s == 0 and m == MC - 1:
                                    pe.wait_ge(d_gelu, 1 + it * NE * MC + e * MC + MC)
                                last = mm(ps[:, 4 + b, s * D:s * D + D], hTd[:, m, b * T + s * P:b * T + s * P + P],
                                          w2x[:, e * MC + m, :], start=m == 0, stop=m == MC - 1)
                        last.then_inc(d_y, 1)
                    if nxt and e < 2:
                        front_turn_part(it + (3 * PAIRS + 1), e)
                pe.wait_ge(d_ye, 1 + it * 2 * NE + 2 * NE - 2)
                for n in range(NT):
                    for s in range(ST):
                        if n == 0 and s == ST - 2:
                            pe.wait_ge(d_ye, 1 + it * 2 * NE + 2 * NE)
                        last = mm(ps[:, 6 + n // 2, (n % 2) * D:(n % 2) * D + D], ct[:, s, n * P:n * P + P],
                                  yy[:, n // 2, s, :], start=s == 0, stop=s == ST - 1)
                    if n % 2:
                        last.then_inc(d_o, 1)

            loop(pe, body_d)


INPUTS = ("x", "xe", "wall0", "wall1", "rel", "wp", "w2a", "w2e", "bias_cols", "bias_rows", "b2r", "c_ident", "c_keys",
          "c_border", "c_mask")


def lay_out(v):
    import numpy as np

    f = np.float32
    v = {k.replace("L0_conv_", "c_").replace("L1_attn_", "a_").replace("L1_ffn_", "f_"): np.asarray(a)
         for k, a in v.items()}
    x = v["x"]
    border = np.concatenate([x[:, :, WS:W].reshape(B, -1, D), x[:, WS:H].reshape(B, -1, D)], 1)

    def spread(w):
        out = np.zeros((w.shape[0], G, HG, 32), f)
        out[..., 0:HD] = w.reshape(-1, G, HG, HD)
        return out.reshape(w.shape[0], G * P)

    qkv, aq = v["c_qkv_w"], v["a_W_qkv"]
    wall = np.concatenate([
        spread(qkv[:, 0:D]), spread(qkv[:, D:2 * D]), qkv[:, 2 * D:], v["c_lin1_w"],
        aq[:, 0:P], aq[:, D:D + P], aq[:, P:D], aq[:, D + P:2 * D], aq[:, 2 * D:],
        v["f_phi"].reshape(NE * NS, D).T, v["f_w1"].transpose(1, 0, 2).reshape(D, NE * MLP)], 1)
    rel = np.zeros((HG, 32, 2, W, 32), f)
    for c in range(HD):
        rel[:, c, 0, :, c] = 1
    for y in range(W):
        for k in range(WS):
            rel[:, 0:HD, 0, y, HD + k] = v["c_rel_pos_h"][y % WS - k + WS - 1]
            rel[:, 0:HD, 1, y, HD + k] = v["c_rel_pos_w"][y % WS - k + WS - 1]
        rel[:, HD, :, y, 30 + (y >= WS)] = 1
    wp = np.zeros((P, 2, 2, D), f)
    for n, (w, b) in enumerate(((v["c_proj_w"], v["c_proj_b"]), (v["a_W_out"], v["a_b_out"]))):
        wp[:, n, 0], wp[0:R1, n, 1], wp[R1, n, 1] = w[0:P], w[P:], b
    wp[L2ROW, 0, 1] = v["c_lin2_b"]
    cols = np.zeros((P, 48), f)
    cb, ab = v["c_qkv_b"], v["a_b_qkv"]
    cols[:, 0:G] = spread(cb[None, 0:D]).reshape(G, P).T
    cols[:, 0:G].reshape(HG, 32, G)[:, HD] = 1
    cols[:, G:2 * G] = spread(cb[None, D:2 * D]).reshape(G, P).T
    for at, w, b in ((N1, v["c_n1_w"], v["c_n1_b"]), (N2, v["c_n2_w"], v["c_n2_b"])):
        cols[:, at], cols[:, at + 1] = w[0:P], np.concatenate([w[P:], w[P:]])
        cols[:, at + 2], cols[:, at + 3] = b[0:P], np.concatenate([b[P:], b[P:]])
    cols[:, CQB], cols[0:AD, CQB + 1] = ab[0:P], ab[P:D]
    cols[:, CKB], cols[AD:P, CKB + 1] = ab[D:D + P], ab[D + P:2 * D]
    cols[:, L1B:L1B + MC] = v["c_lin1_b"].reshape(MC, P).T
    cols[:, E1B:E1B + NE * MC] = v["f_b1"].reshape(NE * MC, P).T
    rows = np.concatenate([cb[None, 2 * D:], ab[None, 2 * D:], v["f_b2"]])
    def key(y, xx, y0=0, y1=0, x0=0, x1=0):
        got = np.zeros((2, 64), f)
        got[:, HD + y % WS] = got[:, 32 + HD + xx % WS] = 1
        got[:, 30], got[:, 31], got[:, 62], got[:, 63] = y0 * NEG, y1 * NEG, x0 * NEG, x1 * NEG
        return got.reshape(P)

    def real(y, xx):
        if y < WS and xx < WS:
            return key(y, xx)
        return key(y, xx, y0=y >= WS, y1=y < WS, x0=xx >= WS, x1=xx < WS)

    ckeys = np.stack([real(y, xx) for y in range(H) for xx in range(W)], 1)
    cborder = np.stack(
        [real(y, xx) if y < WS else key(y, xx, x0=1, x1=1) for y in range(H) for xx in range(WS, W)]
        + [real(y, xx) for y in range(WS, H) for xx in range(W)]
        + [key(y, xx, x0=y < EW, y0=xx < EW) for y in range(WS) for xx in range(WS) if y >= EW or xx >= EW], 1)
    mask = np.where(np.arange(P)[None] > np.arange(P)[:, None], NEG, 0).astype(f)
    got = dict(
        x=x.reshape(B * T, D), xe=border.reshape(PAIRS, P, D), wall0=wall[0:P],
        wall1=np.concatenate([wall[P:], wall[P:]]),
        rel=rel.reshape(P, 2 * W, 32), wp=wp, w2a=v["c_lin2_w"].reshape(MC, P, D).transpose(1, 0, 2),
        w2e=v["f_w2"].reshape(NE * MC, P, D).transpose(1, 0, 2), bias_cols=cols,
        bias_rows=np.broadcast_to(rows[None, 0:2], (P, 2, D)), b2r=np.broadcast_to(rows[None, 2:], (P, NE, D)),
        c_ident=np.eye(P, dtype=f),
        c_keys=ckeys, c_border=cborder, c_mask=mask)
    return {k: np.ascontiguousarray(a) for k, a in got.items()}


def kernel(**inputs):
    import concourse.bacc as bacc
    from concourse.bass_utils import run_bass_kernel_spmd

    laid = lay_out(inputs)
    nc = bacc.Bacc("TRN2", target_bir_lowering=False, num_devices=1)
    args = {k: nc.dram_tensor("in_" + k, laid[k].shape, F32, kind="ExternalInput").ap() for k in INPUTS}
    out = nc.dram_tensor("out", (B * T, D), F32, kind="ExternalOutput").ap()
    build(nc, **args, out=out)
    r = run_bass_kernel_spmd(nc, [{"in_" + k: laid[k] for k in INPUTS}], core_ids=[0])
    return r.results[0]["out"].reshape(B, H, W, D)
```
